# Optimizing a Trainium2 kernel written in Bass

```python
import numpy as np
import jax
import jax.numpy as jnp

def _softmax(x, axis=-1):
    return jax.nn.softmax(x, axis=axis)

def _gelu(x):
    return jax.nn.gelu(x, approximate=True)

def _silu(x):
    return jax.nn.silu(x)

def _sigmoid(x):
    return jax.nn.sigmoid(x)

def _layernorm(x, axis=-1, eps=1e-05):
    m = jnp.mean(x, axis=axis, keepdims=True)
    v = jnp.var(x, axis=axis, keepdims=True)
    return (x - m) / jnp.sqrt(v + eps)

def _scatter_add(tgt, idx, src, axis=0):
    return tgt.at[idx].add(src)

def _segment_sum(src, seg, n):
    return jax.ops.segment_sum(src, seg, n)
kernel_name = 'mk_adj_preln_d4_adj_r2_05f67f'

def setup_inputs(seed: int=0):
    np.random.seed(seed)
    _w = jnp.asarray

    def _rec_inputs():
        import jax
        import jax.numpy as jnp
        _gk = jax.random.key(seed)
        x = -0.0002928 + 1 * jax.random.normal(jax.random.fold_in(_gk, 1), (32, 256, 128), jnp.float32)
        _a = jax.random.bernoulli(jax.random.fold_in(_gk, 2), 0.0078125, (32, 256, 256))
        _af = _a.astype(jnp.float32)
        _af = _af * jax.random.uniform(jax.random.fold_in(_gk, 3), (32, 256, 256), jnp.float32, 0.05, 0.999995)
        adj = _af
        return (x, adj)
    x, adj = _rec_inputs()

    def _L0_gnn_setup():
        import jax, jax.numpy as jnp
        import numpy as np
        B, N, D = (4, 2048, 128)
        DENSITY = 0.02
        key = jax.random.key(seed)
        kx, ka1, ka2, kwt, kbt, kwh, kth = jax.random.split(key, 7)
        x = jax.random.normal(kx, (B, N, D), dtype=jnp.float32)
        mask = jax.random.uniform(ka1, (B, N, N)) < DENSITY
        vals = jax.random.uniform(ka2, (B, N, N), dtype=jnp.float32)
        adj = jnp.where(mask, vals, 0.0).astype(jnp.float32)
        s = 0.02
        W_t = s * jax.random.normal(kwt, (D, D), dtype=jnp.float32)
        b_t = s * jax.random.normal(kbt, (D,), dtype=jnp.float32)
        W_h = s * jax.random.normal(kwh, (D, D), dtype=jnp.float32)
        theta = s * jax.random.normal(kth, (D, D), dtype=jnp.float32)
        return {'x': x, 'adj': adj, 'W_t': W_t, 'b_t': b_t, 'W_h': W_h, 'theta': theta}
    _L0_gnn_all = _L0_gnn_setup()
    _L0_gnn_in = {k: v for k, v in _L0_gnn_all.items() if k in ('W_t', 'b_t', 'W_h', 'theta')}
    del _L0_gnn_all

    def _L1_gnn_setup():
        import jax, jax.numpy as jnp
        import numpy as np
        LN_EPS = 1e-05
        key = jax.random.key(seed)
        k1, k2, k3, k4 = jax.random.split(key, 4)
        B, N, F, O = (8, 1024, 128, 128)
        x = jax.random.normal(k1, (B, N, F), dtype=jnp.float32)
        adj = jax.random.uniform(k2, (B, N, N), dtype=jnp.float32)
        gamma = jnp.ones((F,), jnp.float32)
        beta = jnp.zeros((F,), jnp.float32)
        W_self = jax.random.normal(k3, (F, O), dtype=jnp.float32) * (1.0 / np.sqrt(F))
        W_neigh = jax.random.normal(k4, (F, O), dtype=jnp.float32) * (1.0 / np.sqrt(F))
        return {'x': x, 'adj': adj, 'gamma': gamma, 'beta': beta, 'W_self': W_self, 'W_neigh': W_neigh}
    _L1_gnn_all = _L1_gnn_setup()
    _L1_gnn_in = {k: v for k, v in _L1_gnn_all.items() if k in ('gamma', 'beta', 'W_self', 'W_neigh')}
    del _L1_gnn_all

    def _L2_gnn_setup():
        import jax, jax.numpy as jnp
        import numpy as np
        B, N, D, H = (8, 1024, 128, 512)
        RMS_EPS = 1e-06

        def _rmsnorm(h, w, eps=RMS_EPS):
            var = jnp.mean(jnp.square(h), axis=-1, keepdims=True)
            return h * jax.lax.rsqrt(var + eps) * w
        key = jax.random.key(seed)
        ks = jax.random.split(key, 5)
        x = jax.random.normal(ks[0], (B, N, D), dtype=jnp.float32)
        adjacency = jax.random.uniform(ks[1], (B, N, N), dtype=jnp.float32)
        epsilon = jnp.zeros((), dtype=jnp.float32)
        W1 = jax.random.normal(ks[2], (D, H), dtype=jnp.float32) * (1.0 / np.sqrt(D))
        b1 = jnp.zeros((H,), dtype=jnp.float32)
        rms_weight = jnp.ones((H,), dtype=jnp.float32)
        W2 = jax.random.normal(ks[3], (H, D), dtype=jnp.float32) * (1.0 / np.sqrt(H))
        b2 = jnp.zeros((D,), dtype=jnp.float32)
        return {'x': x, 'adjacency': adjacency, 'epsilon': epsilon, 'W1': W1, 'b1': b1, 'rms_weight': rms_weight, 'W2': W2, 'b2': b2}
    _L2_gnn_all = _L2_gnn_setup()
    _L2_gnn_in = {k: v for k, v in _L2_gnn_all.items() if k in ('epsilon', 'W1', 'b1', 'rms_weight', 'W2', 'b2')}
    del _L2_gnn_all

    def _L3_gnn_setup():
        import jax, jax.numpy as jnp
        import numpy as np
        DIM = 128
        HEADS = 8
        BS = 8
        N = 512
        NEG = -1000000000.0
        key = jax.random.key(seed)
        ks = jax.random.split(key, 8)
        feats = jax.random.normal(ks[0], (BS, N, DIM), dtype=jnp.float32)
        adj_mat = (jax.random.uniform(ks[1], (BS, N, N)) < 0.1).astype(jnp.float32)
        s = 1.0 / np.sqrt(DIM)
        fc_w = jax.random.normal(ks[2], (DIM, DIM * HEADS), dtype=jnp.float32) * s
        fc_b = jnp.zeros((DIM * HEADS,), dtype=jnp.float32)
        q_w = jax.random.normal(ks[3], (DIM, 1), dtype=jnp.float32) * s
        q_b = jnp.zeros((1,), dtype=jnp.float32)
        k_w = jax.random.normal(ks[4], (DIM, 1), dtype=jnp.float32) * s
        k_b = jnp.zeros((1,), dtype=jnp.float32)
        fp_w = jax.random.normal(ks[5], (DIM * HEADS, DIM), dtype=jnp.float32) * (1.0 / np.sqrt(DIM * HEADS))
        fp_b = jnp.zeros((DIM,), dtype=jnp.float32)
        return {'feats': feats, 'adj_mat': adj_mat, 'fc_w': fc_w, 'fc_b': fc_b, 'q_w': q_w, 'q_b': q_b, 'k_w': k_w, 'k_b': k_b, 'fp_w': fp_w, 'fp_b': fp_b}
    _L3_gnn_all = _L3_gnn_setup()
    _L3_gnn_in = {k: v for k, v in _L3_gnn_all.items() if k in ('fc_w', 'fc_b', 'q_w', 'q_b', 'k_w', 'k_b', 'fp_w', 'fp_b')}
    del _L3_gnn_all
    return {'x': x, 'adj': adj, 'L0_gnn_W_t': _L0_gnn_in['W_t'], 'L0_gnn_b_t': _L0_gnn_in['b_t'], 'L0_gnn_W_h': _L0_gnn_in['W_h'], 'L0_gnn_theta': _L0_gnn_in['theta'], 'L1_gnn_gamma': _L1_gnn_in['gamma'], 'L1_gnn_beta': _L1_gnn_in['beta'], 'L1_gnn_W_self': _L1_gnn_in['W_self'], 'L1_gnn_W_neigh': _L1_gnn_in['W_neigh'], 'L2_gnn_epsilon': _L2_gnn_in['epsilon'], 'L2_gnn_W1': _L2_gnn_in['W1'], 'L2_gnn_b1': _L2_gnn_in['b1'], 'L2_gnn_rms_weight': _L2_gnn_in['rms_weight'], 'L2_gnn_W2': _L2_gnn_in['W2'], 'L2_gnn_b2': _L2_gnn_in['b2'], 'L3_gnn_fc_w': _L3_gnn_in['fc_w'], 'L3_gnn_fc_b': _L3_gnn_in['fc_b'], 'L3_gnn_q_w': _L3_gnn_in['q_w'], 'L3_gnn_q_b': _L3_gnn_in['q_b'], 'L3_gnn_k_w': _L3_gnn_in['k_w'], 'L3_gnn_k_b': _L3_gnn_in['k_b'], 'L3_gnn_fp_w': _L3_gnn_in['fp_w'], 'L3_gnn_fp_b': _L3_gnn_in['fp_b']}

def reference(x, adj, L0_gnn_W_t, L0_gnn_b_t, L0_gnn_W_h, L0_gnn_theta, L1_gnn_gamma, L1_gnn_beta, L1_gnn_W_self, L1_gnn_W_neigh, L2_gnn_epsilon, L2_gnn_W1, L2_gnn_b1, L2_gnn_rms_weight, L2_gnn_W2, L2_gnn_b2, L3_gnn_fc_w, L3_gnn_fc_b, L3_gnn_q_w, L3_gnn_q_b, L3_gnn_k_w, L3_gnn_k_b, L3_gnn_fp_w, L3_gnn_fp_b):
    import jax
    import jax.numpy as jnp

    def _L0_gnn_ref(x, adj, W_t, b_t, W_h, theta):
        import jax, jax.numpy as jnp
        import numpy as np
        B, N, D = (4, 2048, 128)
        DENSITY = 0.02
        in_degrees = jnp.sum(adj, axis=-1)
        norm = jnp.power(in_degrees + 1e-06, -0.5)[..., None]
        f_hom = jnp.einsum('bnd,de->bne', x, theta) * norm
        f_hom = jnp.einsum('bnm,bmd->bnd', adj, f_hom) * norm
        f_het = jnp.einsum('bnd,de->bne', x, W_h)
        gate = jax.nn.sigmoid(jnp.einsum('bnd,de->bne', x, W_t) + b_t)
        out = gate * f_hom + (1.0 - gate) * f_het
        return jax.nn.elu(out)

    def _L1_gnn_ref(x, adj, gamma, beta, W_self, W_neigh):
        import jax, jax.numpy as jnp
        import numpy as np
        LN_EPS = 1e-05
        mu = jnp.mean(x, axis=-1, keepdims=True)
        var = jnp.mean(jnp.square(x - mu), axis=-1, keepdims=True)
        xn = (x - mu) * jax.lax.rsqrt(var + LN_EPS) * gamma + beta
        d_out = jnp.sum(adj, axis=1)
        d_in = jnp.sum(adj, axis=2)
        s_out = jnp.where(d_out != 0, jax.lax.rsqrt(d_out), 0.0)
        s_in = jnp.where(d_in != 0, jax.lax.rsqrt(d_in), 0.0)
        A_norm = s_out[:, :, None] * adj * s_in[:, None, :]
        eye = jnp.eye(adj.shape[1], dtype=adj.dtype)
        L = eye[None, :, :] - A_norm
        neighbor = jnp.einsum('bij,bjf->bif', L, xn)
        pre = xn @ W_self + neighbor @ W_neigh
        return jax.nn.softplus(pre)

    def _L2_gnn_ref(x, adjacency, epsilon, W1, b1, rms_weight, W2, b2):
        import jax, jax.numpy as jnp
        import numpy as np
        B, N, D, H = (8, 1024, 128, 512)
        RMS_EPS = 1e-06

        def _rmsnorm(h, w, eps=RMS_EPS):
            var = jnp.mean(jnp.square(h), axis=-1, keepdims=True)
            return h * jax.lax.rsqrt(var + eps) * w
        neighbor_sum = jnp.einsum('bnm,bmd->bnd', adjacency, x)
        agg = epsilon * x + neighbor_sum
        h = jnp.einsum('bnd,dh->bnh', agg, W1) + b1
        h = jax.nn.silu(_rmsnorm(h, rms_weight))
        out = jnp.einsum('bnh,hd->bnd', h, W2) + b2
        return out

    def _L3_gnn_ref(feats, adj_mat, fc_w, fc_b, q_w, q_b, k_w, k_b, fp_w, fp_b):
        import jax, jax.numpy as jnp
        import numpy as np
        DIM = 128
        HEADS = 8
        BS = 8
        N = 512
        NEG = -1000000000.0
        bs, n, dim = feats.shape
        feat_proj = (feats @ fc_w + fc_b).reshape(bs, n, HEADS, dim).transpose(0, 2, 1, 3)
        q = feat_proj @ q_w + q_b
        k = feat_proj @ k_w + k_b
        logits = q + jnp.swapaxes(k, -1, -2)
        masked = logits + (1.0 - adj_mat[:, None]) * NEG
        masked = jax.nn.leaky_relu(masked, negative_slope=0.01)
        attn = jax.nn.softmax(masked, axis=-1)
        out = attn @ feat_proj
        out = out.transpose(0, 2, 1, 3).reshape(bs, n, HEADS * dim)
        out = out @ fp_w + fp_b + feats
        return jax.nn.sigmoid(out)
    h = jnp.maximum(_layernorm(x, axis=-1), 0.0)
    x = x + _L0_gnn_ref(h, adj, L0_gnn_W_t, L0_gnn_b_t, L0_gnn_W_h, L0_gnn_theta)
    h = jnp.maximum(_layernorm(x, axis=-1), 0.0)
    x = x + _L1_gnn_ref(h, adj, L1_gnn_gamma, L1_gnn_beta, L1_gnn_W_self, L1_gnn_W_neigh)
    h = jnp.maximum(_layernorm(x, axis=-1), 0.0)
    x = x + _L2_gnn_ref(h, adj, L2_gnn_epsilon, L2_gnn_W1, L2_gnn_b1, L2_gnn_rms_weight, L2_gnn_W2, L2_gnn_b2)
    h = jnp.maximum(_layernorm(x, axis=-1), 0.0)
    x = x + _L3_gnn_ref(h, adj, L3_gnn_fc_w, L3_gnn_fc_b, L3_gnn_q_w, L3_gnn_q_b, L3_gnn_k_w, L3_gnn_k_b, L3_gnn_fp_w, L3_gnn_fp_b)
    return x

_drawn_inputs = setup_inputs


def setup_inputs(seed=0):
    import zlib

    import numpy as np

    out = dict(_drawn_inputs(seed))
    spreads = {'L1_gnn_gamma': (1.0, 0.6),
     'L1_gnn_beta': (0.0, 0.8),
     'L2_gnn_b1': (0.0, 0.372),
     'L2_gnn_rms_weight': (1.0, 0.6),
     'L2_gnn_b2': (0.0, 0.8),
     'L3_gnn_fc_b': (0.0, 0.8),
     'L3_gnn_fp_b': (0.0, 0.8)}
    factors = {'L0_gnn_b_t': 5.634, 'L0_gnn_W_h': 6.572, 'L3_gnn_fc_w': 5.835, 'L3_gnn_fp_w': 5.751}
    for name, (base, spread) in spreads.items():
        noise = np.random.default_rng([zlib.crc32(name.encode()), seed]).standard_normal(out[name].shape)
        drawn = base * np.exp(spread * noise) if base else spread * noise
        out[name] = jnp.asarray(drawn.astype(out[name].dtype))
    for name, factor in factors.items():
        out[name] = (out[name] * factor).astype(out[name].dtype)
    return out
```

```python
import concourse.bass as bass
from concourse import mybir
from contextlib import ExitStack


class Signal:

    def __init__(self, semaphore, per_pair):
        self.semaphore = semaphore
        self.per_pair = per_pair

    def at(self, pair, k=None):
        return pair * self.per_pair + (self.per_pair if k is None else k)


def due(count):
    return not isinstance(count, int) or count > 0


def four_layer_gnn_kernel(nc, x, adj, theta, w_h, w_t, b_t, gamma, beta, w_self, w_neigh, epsilon,
                          w1, b1, rms_w, w2, b2, fc_w, fc_b, q_w, q_b, k_w, k_b, fp_w, fp_b,
                          row_select, out):
    fp32 = mybir.dt.float32
    bf16 = mybir.dt.bfloat16
    ALU = mybir.AluOpType
    ACT = mybir.ActivationFunctionType

    B, N, D = x.shape
    P = 128
    HALVES = N // P
    R = 2 * HALVES
    PAIRS = B // 2
    HID = w1.shape[1]
    HB = HID // P
    HEADS = fc_w.shape[1] // D
    GROUPS = 2 * HEADS // 2
    GPG = GROUPS // 2
    QROWS = 96
    SLOPE = 0.01
    NEG = -1e9
    FLOOR = -40.0
    SB = 4
    LOADED = 16

    adj_v = adj.rearrange("b n m -> (b n) m").rearrange("(t r p) m -> t p r m", r=R, p=P)
    x_v = x.rearrange("b n d -> (b n) d").rearrange("(t r p) d -> t p r d", r=R, p=P)
    out_v = out.rearrange("b n d -> (b n) d").rearrange("(b r p) d -> b p r d", r=HALVES, p=P)

    ctx = ExitStack()
    with ctx:
        def sb(name, shape, dt=fp32):
            return ctx.enter_context(nc.sbuf_tensor(name, shape, dt))

        def sem(name):
            return ctx.enter_context(nc.semaphore(name))

        def signal(name, per_pair=1):
            return Signal(sem(name), per_pair)

        ident = sb("ident", [P, P])
        ones = sb("ones", [P, P])
        eps_ident = sb("eps_ident", [P, P])
        w_proj = sb("w_proj", [P, 3 * D])
        w_l1 = sb("w_l1", [P, 2 * D])
        w1_sb = sb("w1_sb", [P, HID])
        w2_sb = sb("w2_sb", [P, HB, D])
        b1_sb = sb("b1_sb", [P, HB])
        rmsw_sb = sb("rmsw_sb", [P, HB])
        gamma_sb = sb("gamma_sb", [P, 1])
        beta_sb = sb("beta_sb", [P, 1])
        w_head = sb("w_head", [P, HEADS * D])
        w_qk = sb("w_qk", [P, 3, 32])
        b_qk = sb("b_qk", [QROWS, 1])
        select = sb("select", [QROWS, 2 + 2 * HEADS])
        bt_rows = sb("bt_rows", [P, D])
        b2_rows = sb("b2_rows", [P, D])
        bfin_rows = sb("bfin_rows", [P, D])
        eps_col = sb("eps_col", [P, 1])
        bias_row = sb("bias_row", [1, 3 * D + 1])
        qkw_sb = sb("qkw_sb", [P, 2])
        qkb_sb = sb("qkb_sb", [1, 2])
        qkb_row = sb("qkb_row", [1, 3, 32])
        fcb_sb = sb("fcb_sb", [P, HEADS])
        bq_prod = sb("bq_prod", [P, 3, 32])
        ln_guard = sb("ln_guard", [P, 1])
        rms_guard = sb("rms_guard", [P, 1])
        fence = sb("fence", [P, 16])
        fence_pool = sb("fence_pool", [P, 4])

        A = [sb(f"A{i}", [P, R, N]) for i in range(2)]
        AT = [sb(f"AT{i}", [P, 2, HALVES, N]) for i in range(2)]
        M = [sb(f"M{i}", [P, R, N]) for i in range(2)]
        x_in = sb("x_in", [P, R, D])
        X = [sb(f"X{i}", [P, R, D]) for i in range(2)]
        XH = [sb(f"XH{i}", [P, R, D]) for i in range(2)]
        ZH = [sb(f"ZH{i}", [P, R, D]) for i in range(2)]
        G = [sb(f"G{i}", [P, R, HEADS, D]) for i in range(2)]
        q_rows = [sb(f"q_rows{i}", [QROWS, 2 * N], bf16) for i in range(2)]
        k_rows = [sb(f"k_rows{i}", [QROWS, HEADS, 2 * N], bf16) for i in range(2)]

        st_e = sb("st_e", [P, R, 6])
        mv_e = sb("mv_e", [P, R, 2])
        lv_e = sb("lv_e", [P, R])
        rs_e = sb("rs_e", [P, R])
        xn_e = sb("xn_e", [P, R, D])
        h1_e = sb("h1_e", [P, R, D])
        ht_e = sb("ht_e", [P, R * P])
        y_e = sb("y_e", [P, R, D])
        het = sb("het", [P, R, D])
        gate = sb("gate", [P, R, D])
        mix = sb("mix", [P, R, D])
        elu = sb("elu", [P, R, D])
        deg = sb("deg", [P, 12])
        degc = sb("degc", [P, 12])
        scl = sb("scl", [P, 12])
        s_in_out = sb("s_in_out", [P, 8])
        neg_s_out = sb("neg_s_out", [P, R])
        u1 = sb("u1", [P, R, D])
        pre = sb("pre", [P, R, D])
        softp = sb("softp", [P, R, D])

        st_l = sb("st_l", [P, R, 6])
        mv_l = sb("mv_l", [P, R, 2])
        lv_l = sb("lv_l", [P, R])
        rs_l = sb("rs_l", [P, R])
        xn_l = sb("xn_l", [P, R, D])
        h2 = sb("h2", [P, R, D])
        zt = sb("zt", [P, R * P])
        hid = sb("hid", [P, HB, R * P])
        sq = sb("sq", [P, HB, R * P])
        rms_b = sb("rms_b", [P, R * P])
        x_b2 = sb("x_b2", [P, R, D])
        ht_l = sb("ht_l", [P, R * P])
        qk_f = sb("qk_f", [QROWS, 2 * N])
        qk_r = sb("qk_r", [QROWS, 2 * N])
        qk_s = sb("qk_s", [QROWS, 2 * N], bf16)

        S = [sb(f"S{i}", [P, 2, HALVES, N]) for i in range(SB)]
        mx = [sb(f"mx{i}", [P, 4]) for i in range(SB)]
        ng = [sb(f"ng{i}", [P, 4]) for i in range(SB)]
        nm = [sb(f"nm{i}", [P, 4]) for i in range(SB)]
        sm = [sb(f"sm{i}", [P, 4]) for i in range(SB)]
        rc = [sb(f"rc{i}", [P, 4]) for i in range(SB)]
        ET = [sb(f"ET{i}", [P, HALVES, N]) for i in range(2)]
        zf = [sb(f"zf{i}", [P, HALVES, D]) for i in range(2)]
        res = [sb(f"res{i}", [P, HALVES, D]) for i in range(2)]

        fc_sb = hid[:, 0:2, :].rearrange("p a n -> p (a n)")
        fct = hid[:, 2:4, :].rearrange("p a n -> p (a n)")
        fp_sb = sq[:, 0:2, :].rearrange("p a n -> p (a n)").rearrange("p (h d) -> p h d", d=D)
        fcb_cols = sq[:, 2:4, :].rearrange("p a n -> p (a n)").rearrange("p (h d) -> p h d", d=D)
        ws_sb = xn_l[:, 0, :]

        def bank(name):
            return ctx.enter_context(nc.psum_tensor(name, [P, 512], fp32))

        ps_e, ps_l = bank("ps_e"), bank("ps_l")
        ps_s = [bank(f"ps_s{i}") for i in range(2)]
        ps_t = [bank(f"ps_t{i}") for i in range(2)]
        ps_o = [bank(f"ps_o{i}") for i in range(2)]

        p_load = sem("p_load")
        p_pool = sem("p_pool")
        p_pe = sem("p_pe")
        p_zeroed = sem("p_zeroed")
        p_products = sem("p_products")
        p_rows = sem("p_rows")
        p_fct = sem("p_fct")
        p_weights = sem("p_weights")
        adj_in = [sem(f"adj_in{i}") for i in range(2)]
        x_loaded = signal("x_loaded", LOADED)
        stored = [signal(f"stored{i}", LOADED) for i in range(2)]
        e_adj_tr = signal("e_adj_tr", 2)
        e_at = signal("e_at", 2)
        e_deg_ps = signal("e_deg_ps")
        e_deg = signal("e_deg")
        e_degc = signal("e_degc")
        e_scl = signal("e_scl", 2)
        e_masked = signal("e_masked")
        e_norms = signal("e_norms")
        e_bn = signal("e_bn", 3)
        e_mv = signal("e_mv", 3)
        e_lv = signal("e_lv", 3)
        e_rs = signal("e_rs", 3)
        e_xn = signal("e_xn", 3)
        e_h1 = signal("e_h1")
        e_tr0 = signal("e_tr0")
        e_ht0 = signal("e_ht0")
        e_proj_ps = signal("e_proj_ps", 4)
        e_proj = signal("e_proj", 4)
        e_clamped = signal("e_clamped")
        e_gate = signal("e_gate", 3)
        e_hop0 = signal("e_hop0")
        e_dif = signal("e_dif")
        e_gated = signal("e_gated")
        e_mix = signal("e_mix")
        e_min = signal("e_min")
        e_expm = signal("e_expm")
        e_elu = signal("e_elu")
        e_x0 = signal("e_x0")
        e_tr1 = signal("e_tr1")
        e_ht1 = signal("e_ht1")
        e_u_ps = signal("e_u_ps", 2)
        e_u = signal("e_u", 2)
        e_hop1 = signal("e_hop1")
        e_pre = signal("e_pre")
        e_sp = signal("e_sp", 3)
        e_part = signal("e_part")
        e_x1 = signal("e_x1")
        l_mask = signal("l_mask")
        l_bn = signal("l_bn", 2)
        l_mv = signal("l_mv", 2)
        l_lv = signal("l_lv", 2)
        l_rs = signal("l_rs", 2)
        l_xn = signal("l_xn", 2)
        l_h2 = signal("l_h2")
        l_z_ps = signal("l_z_ps")
        l_zt = signal("l_zt")
        l_hid_ps = signal("l_hid_ps", 4)
        l_hid = signal("l_hid", 4)
        l_sq = signal("l_sq", 4)
        l_sum = signal("l_sum", 3)
        l_ss_ps = signal("l_ss_ps")
        l_rms = signal("l_rms", 2)
        l_g = signal("l_g", 4)
        l_cl = signal("l_cl", 4)
        l_sig = signal("l_sig", 6)
        l_act_p = signal("l_act_p", 2)
        l_act_v = signal("l_act_v", 2)
        l_w2_ps = signal("l_w2_ps")
        l_xb = signal("l_xb")
        l_x2 = signal("l_x2")
        l_tr = signal("l_tr")
        l_ht = signal("l_ht")
        l_zh = signal("l_zh")
        l_qk_ps = signal("l_qk_ps")
        l_split = signal("l_split", 5)
        l_rows = signal("l_rows")
        l_g_ps = signal("l_g_ps", 8)
        l_ga = signal("l_ga", 4)
        l_gv = signal("l_gv", 4)
        h_qk = signal("h_qk", 16)
        h_max = signal("h_max", 16)
        h_neg = signal("h_neg", 8)
        h_leaky = signal("h_leaky", 8)
        h_exp = signal("h_exp", 8)
        h_rc = signal("h_rc", 8)
        h_norm = signal("h_norm", 8)
        h_tr = signal("h_tr", 16)
        h_et = signal("h_et", 16)
        h_av = signal("h_av", 16)
        f_z = signal("f_z", 2)
        f_c = signal("f_c", 2)
        f_s = signal("f_s", 6)
        f_res = signal("f_res", 2)

        AT_E = dict(adj0=0, adj1=1, deg=2, deg2=3, ln0=0, rs0=1, xn0=2, tr0=3, ht0=4, proj0=5, proj1=6,
                    proj2=7, proj3=8, gate=9, hop0=9, dif=10, mix=11, expm=12, x0=12, rs1=13, h1=14,
                    rs2=15, xn1=16, tr1=17, ht1=18, u0=19, u1=20, hop1=21, pre=22, sp=23, x1=24)
        AT_L = dict(mask=0, ln2=0, rs2=1, h2=2, z=3, zt=4, hid0=5, hid1=6, hid2=7, hid3=8, ss=10,
                    rms=11, g0=12, g1=12, g2=13, g3=13, sig0=13, sig1=14, act=15, w2=17, x2=18,
                    rs3=19, xn3=20, tr=21, ht=22, qk=23, split=23, rows=26,
                    g_0=24, g_1=25, g_2=26, g_3=27, g_4=28, g_5=29, g_6=30, g_7=31)

        def group(th, s, lag, p):
            if s >= lag:
                return th, s - lag, p
            return th - 1, s - lag + GROUPS, 1 - p

        def iterations(engine, body):
            for t in range(5):
                body(t, t % 2, t)
            with engine.Fori(5, PAIRS - 2, 2) as t:
                body(t, 1, None)
                body(t + 1, 0, None)
            for t in range(PAIRS - 1, PAIRS + 3):
                body(t, t % 2, t)

        def mine(known, back):
            return known is None or 0 <= known - back < PAIRS

        block = ctx.enter_context(nc.Block())

        @block.sync
        def _(sp):
            for dst, src in (
                (w_proj[:, 0:D], theta), (w_proj[:, D:2 * D], w_h), (w_proj[:, 2 * D:3 * D], w_t),
                (ws_sb, w_self), (w_l1[:, D:2 * D], w_neigh), (w1_sb[:, :], w1),
                (w2_sb[:, :, :], w2.rearrange("(b p) d -> p b d", p=P)),
                (fc_sb, fc_w), (fp_sb, fp_w.rearrange("(h e) d -> e h d", e=P)),
                (gamma_sb[:, :], gamma.rearrange("(p a) -> p a", a=1)),
                (beta_sb[:, :], beta.rearrange("(p a) -> p a", a=1)),
                (qkw_sb[:, 0:1], q_w), (qkw_sb[:, 1:2], k_w),
                (qkb_sb[:, 0:1], q_b.rearrange("(a n) -> a n", a=1)),
                (qkb_sb[:, 1:2], k_b.rearrange("(a n) -> a n", a=1)),
                (bias_row[:, 0:D], b_t.rearrange("(a n) -> a n", a=1)),
                (bias_row[:, D:2 * D], b2.rearrange("(a n) -> a n", a=1)),
                (bias_row[:, 2 * D:3 * D], fp_b.rearrange("(a n) -> a n", a=1)),
                (bias_row[:, 3 * D:3 * D + 1], epsilon),
                (select[:, :], row_select),
            ):
                sp.dma_start(dst, src).then_inc(p_load, 16)
            with nc.allow_non_contiguous_dma(reason="three short vectors, once"):
                sp.dma_start(b1_sb[:, :], b1.rearrange("(b p) -> p b", p=P)).then_inc(p_load, 16)
                sp.dma_start(rmsw_sb[:, :], rms_w.rearrange("(b p) -> p b", p=P)).then_inc(p_load, 16)
                sp.dma_start(fcb_sb[:, :], fc_b.rearrange("(h e) -> e h", e=P)).then_inc(p_load, 16)

            def load_adj(t, p, k):
                sp.dma_start(A[p][:, :, :], adj_v[t]).then_inc(adj_in[p], 16)

            load_adj(0, 0, 0)
            sp.dma_start(x_in[:, :, :], x_v[0]).then_inc(x_loaded.semaphore, 16)

            def store(pair, g):
                sp.wait_ge(f_res.semaphore, f_res.at(pair, g + 1))
                sp.dma_start(out_v[pair * 2 + g], res[g][:, :, :]).then_inc(stored[g].semaphore, 16)

            def body(t, p, known):
                if mine(known, 3):
                    store(t - 3, 1)
                if known is None or known + 1 < PAIRS:
                    if due(l_mask.at(t - 1)):
                        sp.wait_ge(l_mask.semaphore, l_mask.at(t - 1))
                    if due(e_deg_ps.at(t - 1)):
                        sp.wait_ge(e_deg_ps.semaphore, e_deg_ps.at(t - 1))
                    load_adj(t + 1, 1 - p, None)
                    sp.wait_ge(e_x0.semaphore, e_x0.at(t))
                    sp.dma_start(x_in[:, :, :], x_v[t + 1]).then_inc(x_loaded.semaphore, 16)
                if mine(known, 2):
                    store(t - 2, 0)

            iterations(sp, body)
            for g in range(2):
                sp.wait_ge(stored[g].semaphore, stored[g].at(PAIRS - 1))

        @block.gpsimd
        def _(pool):
            pool.memset(ident[:, :], 0.0).then_inc(p_pool, 1)
            pool.memset(ones[:, :], 1.0).then_inc(p_pool, 1)
            pool.memset(fence_pool[:, :], 0.0).then_inc(p_pool, 1)
            pool.wait_ge(p_pool, 3)
            pool.affine_select(out=ident[:, :], in_=ident[:, :], compare_op=ALU.not_equal, fill=1.0,
                               base=0, pattern=[[-1, P]], channel_multiplier=1).then_inc(p_pool, 1)
            pool.wait_ge(p_weights, 5)

            def residual_bias(tl, q):
                pool.wait_ge(e_x1.semaphore, e_x1.at(tl))
                if due(l_x2.at(tl - 1)):
                    pool.wait_ge(l_x2.semaphore, l_x2.at(tl - 1))
                pool.tensor_tensor(x_b2[:, 0, :], X[q][:, 0, :], b2_rows[:, :], ALU.add)
                for r in range(1, R):
                    last = pool.tensor_tensor(x_b2[:, r, :], X[q][:, r, :], b2_rows[:, :], ALU.add)
                last.then_inc(l_xb.semaphore, 1)

            def sum_squares(tl):
                pool.wait_ge(l_sq.semaphore, l_sq.at(tl, 2))
                pool.tensor_tensor(sq[:, 0, :], sq[:, 0, :], sq[:, 1, :], ALU.add).then_inc(l_sum.semaphore, 1)
                pool.wait_ge(l_sq.semaphore, l_sq.at(tl, 4))
                pool.tensor_tensor(sq[:, 2, :], sq[:, 2, :], sq[:, 3, :], ALU.add).then_inc(l_sum.semaphore, 1)
                pool.wait_ge(l_sum.semaphore, l_sum.at(tl, 2))
                pool.tensor_tensor(sq[:, 0, :], sq[:, 0, :], sq[:, 2, :], ALU.add).then_inc(l_sum.semaphore, 1)

            def silu_blocks(tl):
                for b in range(2):
                    pool.wait_ge(l_sig.semaphore, l_sig.at(tl, 5))
                    pool.tensor_tensor(hid[:, b, :], hid[:, b, :], sq[:, b, :], ALU.mult)\
                        .then_inc(l_act_p.semaphore, 1)

            def normalise(th, s, p):
                pair, u, _ = group(th, s, 1, p)
                pool.wait_ge(h_rc.semaphore, h_rc.at(pair, u + 1))
                pool.tensor_tensor(fence_pool[:, 0:1], fence_pool[:, 1:2], fence_pool[:, 2:3], ALU.add)
                for k in range(4):
                    row = S[u % SB][:, k // 2, k % 2, :]
                    last = pool.tensor_scalar(row, row, rc[u % SB][:, k:k + 1], 1.0, ALU.mult, ALU.mult)
                last.then_inc(h_norm.semaphore, 1)

            def body(t, p, known):
                tl, th = t - 1, t - 2
                if mine(known, 1):
                    residual_bias(tl, 1 - p)
                for s in range(GROUPS):
                    if mine(known, 2) if s >= 1 else mine(known, 3):
                        normalise(th, s, p)
                    if mine(known, 1):
                        if s == AT_L["ss"] // 4:
                            sum_squares(tl)
                        if s == AT_L["act"] // 4:
                            silu_blocks(tl)

            iterations(pool, body)

        @block.scalar
        def _(act):
            act.preload_act_table_set("natural_log_exp_and_others")
            act.wait_ge(p_weights, 5)

            def adj_evac(t, p, g):
                act.wait_ge(e_adj_tr.semaphore, e_adj_tr.at(t, g + 1))
                act.activation(AT[p][:, g, :, :].rearrange("p a n -> p (a n)"), ps_e[:, :], ACT.Copy)\
                    .then_inc(e_at.semaphore, 1)

            def degree_roots(t):
                act.wait_ge(e_degc.semaphore, e_degc.at(t))
                act.activation(degc[:, :], degc[:, :], ACT.Ln).then_inc(e_scl.semaphore, 1)
                act.wait_ge(e_scl.semaphore, e_scl.at(t, 1))
                act.activation(scl[:, :], degc[:, :], ACT.Exp, scale=-0.5).then_inc(e_scl.semaphore, 1)

            def rstd(t, k, mv, lv, rs, s_mv, s_lv, s_rs):
                act.wait_ge(s_mv.semaphore, s_mv.at(t, k))
                act.activation(lv[:, :], mv[:, :, 1], ACT.Ln, bias=ln_guard[:, 0:1]).then_inc(s_lv.semaphore, 1)
                act.wait_ge(s_lv.semaphore, s_lv.at(t, k))
                act.activation(rs[:, :], lv[:, :], ACT.Exp, scale=-0.5).then_inc(s_rs.semaphore, 1)

            def rstd_e(t, k):
                rstd(t, k, mv_e, lv_e, rs_e, e_mv, e_lv, e_rs)

            def rstd_l(t, k):
                rstd(t, k, mv_l, lv_l, rs_l, l_mv, l_lv, l_rs)

            def relu_t0(t):
                act.wait_ge(e_tr0.semaphore, e_tr0.at(t))
                act.activation(ht_e[:, :], ps_e[:, :], ACT.Relu).then_inc(e_ht0.semaphore, 1)

            def gate_sigmoid(t):
                flat = gate[:, :, :].rearrange("p r d -> p (r d)")
                act.wait_ge(e_clamped.semaphore, e_clamped.at(t))
                act.activation(flat, flat, ACT.Exp, scale=-1.0).then_inc(e_gate.semaphore, 1)
                act.wait_ge(e_gate.semaphore, e_gate.at(t, 1))
                act.activation(flat, flat, ACT.Ln, bias=1.0).then_inc(e_gate.semaphore, 1)
                act.wait_ge(e_gate.semaphore, e_gate.at(t, 2))
                act.activation(flat, flat, ACT.Exp, scale=-1.0).then_inc(e_gate.semaphore, 1)

            def elu_exp(t):
                flat = elu[:, :, :].rearrange("p r d -> p (r d)")
                act.wait_ge(e_min.semaphore, e_min.at(t))
                act.activation(flat, flat, ACT.Exp).then_inc(e_expm.semaphore, 1)

            def softplus(t):
                flat = softp[:, :, :].rearrange("p r d -> p (r d)")
                act.wait_ge(e_pre.semaphore, e_pre.at(t))
                act.activation(flat, pre[:, :, :].rearrange("p r d -> p (r d)"), ACT.Abs).then_inc(e_sp.semaphore, 1)
                act.wait_ge(e_sp.semaphore, e_sp.at(t, 1))
                act.activation(flat, flat, ACT.Exp, scale=-1.0).then_inc(e_sp.semaphore, 1)
                act.wait_ge(e_sp.semaphore, e_sp.at(t, 2))
                act.activation(flat, flat, ACT.Ln, bias=1.0).then_inc(e_sp.semaphore, 1)

            def zt_evac(t):
                act.wait_ge(l_z_ps.semaphore, l_z_ps.at(t))
                act.activation(zt[:, :], ps_l[:, :], ACT.Copy).then_inc(l_zt.semaphore, 1)

            def square(t, b):
                act.wait_ge(l_hid.semaphore, l_hid.at(t, b + 1))
                act.activation(sq[:, b, :], hid[:, b, :], ACT.Square).then_inc(l_sq.semaphore, 1)

            def rms(t):
                act.wait_ge(l_ss_ps.semaphore, l_ss_ps.at(t))
                act.activation(rms_b[:, :], ps_l[:, :], ACT.Ln, bias=rms_guard[:, 0:1], scale=1.0 / HID)\
                    .then_inc(l_rms.semaphore, 1)
                act.wait_ge(l_rms.semaphore, l_rms.at(t, 1))
                act.activation(rms_b[:, :], rms_b[:, :], ACT.Exp, scale=-0.5).then_inc(l_rms.semaphore, 1)

            def half(i):
                return sq[:, 2 * i:2 * i + 2, :].rearrange("p b n -> p (b n)")

            def silu_exp(t, i):
                act.wait_ge(l_cl.semaphore, l_cl.at(t, 2 * i + 2))
                act.activation(half(i), half(i), ACT.Exp, scale=-1.0).then_inc(l_sig.semaphore, 1)

            def silu_rest(t):
                for i in range(2):
                    act.wait_ge(l_sig.semaphore, l_sig.at(t, 1 + i))
                    act.activation(half(i), half(i), ACT.Ln, bias=1.0).then_inc(l_sig.semaphore, 1)
                for i in range(2):
                    act.wait_ge(l_sig.semaphore, l_sig.at(t, 3 + i))
                    act.activation(half(i), half(i), ACT.Exp, scale=-1.0).then_inc(l_sig.semaphore, 1)

            def relu_t3(t):
                act.wait_ge(l_tr.semaphore, l_tr.at(t))
                act.activation(ht_l[:, :], ps_l[:, :], ACT.Relu).then_inc(l_ht.semaphore, 1)

            def g_evac(t, q, k):
                act.wait_ge(l_g_ps.semaphore, l_g_ps.at(t, k + 1))
                if k == 0:
                    if due(h_av.at(t - 2)):
                        act.wait_ge(h_av.semaphore, h_av.at(t - 2))
                act.activation(G[q][:, k // 2, 4 * (k % 2):4 * (k % 2) + 4, :].rearrange("p h d -> p (h d)"),
                                    ps_l[:, :], ACT.Copy)\
                    .then_inc(l_ga.semaphore, 1)

            def exp(pair, u, k):
                if k == 0:
                    act.wait_ge(h_leaky.semaphore, h_leaky.at(pair, u + 1))
                row = S[u % SB][:, k // 2, k % 2, :]
                ins = act.activation(row, row, ACT.Exp, bias=nm[u % SB][:, k:k + 1],
                                     accum_out=sm[u % SB][:, k:k + 1])
                if k == 3:
                    ins.then_inc(h_exp.semaphore, 1)

            def et_evac(pair, u, j):
                act.wait_ge(h_tr.semaphore, h_tr.at(pair, 2 * u + j + 1))
                if due(h_av.at(pair, 2 * u + j - 1)):
                    act.wait_ge(h_av.semaphore, h_av.at(pair, 2 * u + j - 1))
                act.activation(ET[j][:, :, :].rearrange("p a n -> p (a n)"), ps_t[j][:, :], ACT.Copy)\
                    .then_inc(h_et.semaphore, 1)

            def final_sigmoid(pair, g):
                flat = zf[g][:, :, :].rearrange("p r d -> p (r d)")
                act.wait_ge(f_c.semaphore, f_c.at(pair, g + 1))
                act.activation(flat, flat, ACT.Exp, scale=-1.0).then_inc(f_s.semaphore, 1)
                act.wait_ge(f_s.semaphore, f_s.at(pair, 3 * g + 1))
                act.activation(flat, flat, ACT.Ln, bias=1.0).then_inc(f_s.semaphore, 1)
                act.wait_ge(f_s.semaphore, f_s.at(pair, 3 * g + 2))
                act.activation(flat, flat, ACT.Exp, scale=-1.0).then_inc(f_s.semaphore, 1)

            def early(t, p, at):
                E = AT_E
                if at == E["adj0"]:
                    adj_evac(t, p, 0)
                if at == E["rs0"]:
                    rstd_e(t, 1)
                if at == E["adj1"]:
                    adj_evac(t, p, 1)
                if at == E["deg2"]:
                    degree_roots(t)
                if at == E["ht0"]:
                    relu_t0(t)
                if at == E["gate"]:
                    gate_sigmoid(t)
                if at == E["expm"]:
                    elu_exp(t)
                if at == E["rs1"]:
                    rstd_e(t, 2)
                if at == E["rs2"]:
                    rstd_e(t, 3)
                if at == E["sp"]:
                    softplus(t)

            def late(t, q, at):
                L = AT_L
                if at == L["rs2"]:
                    rstd_l(t, 1)
                if at == L["zt"]:
                    zt_evac(t)
                for b in range(4):
                    if at == L[f"hid{b}"]:
                        square(t, b)
                if at == L["rms"]:
                    rms(t)
                if at == L["sig0"]:
                    silu_exp(t, 0)
                if at == L["sig1"]:
                    silu_exp(t, 1)
                    silu_rest(t)
                if at == L["rs3"]:
                    rstd_l(t, 2)
                if at == L["ht"]:
                    relu_t3(t)
                for k in range(0, 8, 2):
                    if at == L[f"g_{k}"]:
                        g_evac(t, q, k)

            def body(t, p, known):
                th = t - 2
                for s in range(GROUPS):
                    lag1 = mine(known, 2) if s >= 1 else mine(known, 3)
                    lag2 = mine(known, 2) if s >= 2 else mine(known, 3)
                    pair1, u1_, _ = group(th, s, 1, p)
                    pair2, u2_, _ = group(th, s, 2, p)
                    for k in range(4):
                        if lag1:
                            exp(pair1, u1_, k)
                        if lag2 and k in (1, 3):
                            et_evac(pair2, u2_, k // 2)
                        if mine(known, 0):
                            early(t, p, 4 * s + k)
                        if mine(known, 1):
                            late(t - 1, 1 - p, 4 * s + k)
                        if k == 1:
                            if s == 2 and mine(known, 3):
                                final_sigmoid(t - 3, 1)
                            if s == 6 and mine(known, 2):
                                final_sigmoid(t - 2, 0)

            iterations(act, body)

        @block.vector
        def _(dve):
            dve.memset(w_qk[:, :, :], 0.0).then_inc(p_zeroed, 1)
            dve.memset(bq_prod[:, :, :], 0.0).then_inc(p_zeroed, 1)
            dve.memset(qkb_row[:, :, :], 0.0).then_inc(p_zeroed, 1)
            dve.memset(ln_guard[:, :], 1e-5)
            dve.memset(rms_guard[:, :], 1e-6)
            dve.memset(fcb_cols, 0.0).then_inc(p_zeroed, 1)
            dve.wait_ge(p_load, 16 * 23)
            dve.wait_ge(p_zeroed, 4)
            dve.tensor_tensor(w_l1[:, 0:D], ws_sb, w_l1[:, D:2 * D], ALU.add)
            for part in range(3):
                for kind in range(2):
                    dve.tensor_scalar(bq_prod[:, part, 8 * kind:8 * kind + 8], fcb_sb[:, :],
                                      qkw_sb[:, kind:kind + 1], None, ALU.mult)
                    dve.tensor_scalar(qkb_row[:, part, 8 * kind:8 * kind + 8], qkb_row[:, part, 8 * kind:8 * kind + 8],
                                      qkb_sb[:, kind:kind + 1], None, ALU.add)
            for h in range(HEADS):
                last = dve.tensor_scalar(fcb_cols[:, h, :], fcb_cols[:, h, :], fcb_sb[:, h:h + 1], None, ALU.add)
            last.then_inc(p_products, 1)
            dve.wait_ge(p_pe, 1)
            dve.tensor_copy(bt_rows[:, :], ps_e[:, 0:D])
            dve.tensor_copy(b2_rows[:, :], ps_e[:, D:2 * D])
            dve.tensor_copy(eps_col[:, :], ps_e[:, 3 * D:3 * D + 1]).then_inc(p_rows, 1)
            dve.wait_ge(p_rows, 1)
            dve.wait_ge(p_pool, 4)
            dve.tensor_scalar(eps_ident[:, :], ident[:, :], eps_col[:, 0:1], None, ALU.mult).then_inc(p_weights, 1)
            dve.wait_ge(p_pe, 2)
            dve.tensor_copy(bfin_rows[:, :], ps_l[:, 0:D]).then_inc(p_weights, 1)
            dve.wait_ge(p_pe, 3)
            for i in range(2):
                last = dve.tensor_copy(fct[:, 512 * i:512 * i + 512], ps_t[i][:, :])
            last.then_inc(p_fct, 1)
            dve.wait_ge(p_pe, 4)
            for i in range(2):
                last = dve.tensor_copy(w_head[:, 512 * i:512 * i + 512], ps_s[i][:, :])
            last.then_inc(p_weights, 1)
            for part in range(3):
                for kind in range(2):
                    last = dve.tensor_copy(w_qk[:, part, 8 * kind:8 * kind + 8], ps_o[0][:, kind:16:2])
            last.then_inc(p_weights, 1)
            dve.tensor_copy(b_qk[:, :], ps_o[1][0:QROWS, 0:1]).then_inc(p_weights, 1)

            carried = [0]

            def carrier():
                carried[0] += 1
                return fence[:, carried[0] % 16:carried[0] % 16 + 1]

            def stats(t, k, src, st, mv, s_bn, s_mv):
                for r in range(R):
                    last = dve.bn_stats(st[:, r, :], src[:, r, :])
                last.then_inc(s_bn.semaphore, 1)
                dve.wait_ge(s_bn.semaphore, s_bn.at(t, k))
                dve.memset(carrier(), 0.0)
                for r in range(R):
                    last = dve.bn_aggr(mv[:, r, :], st[:, r, :])
                last.then_inc(s_mv.semaphore, 1)

            def apply(t, k, dst, src, mv, rs, s_rs, sig):
                dve.wait_ge(s_rs.semaphore, s_rs.at(t, k))
                for r in range(R):
                    last = dve.tensor_scalar(dst[:, r, :], src[:, r, :], mv[:, r, 0:1], rs[:, r:r + 1],
                                             ALU.subtract, ALU.mult)
                last.then_inc(sig.semaphore, 1)

            def stats_e(t, k, src):
                stats(t, k, src, st_e, mv_e, e_bn, e_mv)

            def stats_l(t, k, src):
                stats(t, k, src, st_l, mv_l, l_bn, l_mv)

            def degrees(t):
                dve.wait_ge(e_deg_ps.semaphore, e_deg_ps.at(t))
                dve.tensor_scalar(deg[:, 0:4], ps_e[:, 0:4], 1e-6, None, ALU.add)
                dve.tensor_copy(deg[:, 4:12], ps_e[:, 0:8]).then_inc(e_deg.semaphore, 1)
                dve.wait_ge(e_deg.semaphore, e_deg.at(t))
                dve.tensor_scalar(degc[:, :], deg[:, :], 1e-19, None, ALU.max).then_inc(e_degc.semaphore, 1)

            def degree_masks(t):
                dve.wait_ge(e_scl.semaphore, e_scl.at(t))
                dve.scalar_tensor_tensor(out=s_in_out[:, :], in0=deg[:, 4:12], scalar=0.0,
                                              in1=scl[:, 4:12], op0=ALU.not_equal, op1=ALU.mult)\
                    .then_inc(e_masked.semaphore, 1)
                dve.wait_ge(e_masked.semaphore, e_masked.at(t))
                dve.tensor_scalar(neg_s_out[:, :], s_in_out[:, 4:8], -1.0, None, ALU.mult).then_inc(e_norms.semaphore, 1)

            def proj_evac(t, r):
                dve.wait_ge(e_proj_ps.semaphore, e_proj_ps.at(t, r + 1))
                dve.tensor_scalar(y_e[:, r, :], ps_e[:, 0:D], scl[:, r:r + 1], None, ALU.mult)
                dve.tensor_copy(het[:, r, :], ps_e[:, D:2 * D])
                dve.tensor_tensor(gate[:, r, :], ps_e[:, 2 * D:3 * D], bt_rows[:, :], ALU.add)\
                    .then_inc(e_proj.semaphore, 1)

            def gate_clamp(t):
                dve.wait_ge(e_proj.semaphore, e_proj.at(t))
                dve.tensor_scalar(gate[:, :, :], gate[:, :, :], FLOOR, None, ALU.max).then_inc(e_clamped.semaphore, 1)

            def hop0_evac(t):
                dve.wait_ge(e_hop0.semaphore, e_hop0.at(t))
                for r in range(R):
                    last = dve.scalar_tensor_tensor(out=mix[:, r, :], in0=ps_e[:, r * D:(r + 1) * D],
                                                    scalar=scl[:, r:r + 1], in1=het[:, r, :],
                                                    op0=ALU.mult, op1=ALU.subtract)
                last.then_inc(e_dif.semaphore, 1)

            def mix_up(t):
                dve.wait_ge(e_dif.semaphore, e_dif.at(t))
                dve.wait_ge(e_gate.semaphore, e_gate.at(t))
                dve.tensor_tensor(mix[:, :, :], mix[:, :, :], gate[:, :, :], ALU.mult).then_inc(e_gated.semaphore, 1)
                dve.wait_ge(e_gated.semaphore, e_gated.at(t))
                dve.tensor_tensor(mix[:, :, :], mix[:, :, :], het[:, :, :], ALU.add).then_inc(e_mix.semaphore, 1)
                dve.wait_ge(e_mix.semaphore, e_mix.at(t))
                dve.tensor_scalar(elu[:, :, :], mix[:, :, :], 0.0, None, ALU.min).then_inc(e_min.semaphore, 1)

            def residual0(t, p):
                dve.wait_ge(e_expm.semaphore, e_expm.at(t))
                dve.scalar_tensor_tensor(out=mix[:, :, :], in0=elu[:, :, :], scalar=-1.0,
                                              in1=mix[:, :, :], op0=ALU.add, op1=ALU.max)\
                    .then_inc(e_elu.semaphore, 1)
                dve.wait_ge(e_elu.semaphore, e_elu.at(t))
                if due(l_xb.at(t - 2)):
                    dve.wait_ge(l_xb.semaphore, l_xb.at(t - 2))
                dve.tensor_tensor(X[p][:, :, :], x_in[:, :, :], mix[:, :, :], ALU.add).then_inc(e_x0.semaphore, 1)
                dve.wait_ge(e_x0.semaphore, e_x0.at(t))
                stats_e(t, 2, X[p])

            def h1_relu(t, p):
                apply(t, 2, h1_e, X[p], mv_e, rs_e, e_rs, e_xn)
                dve.wait_ge(e_xn.semaphore, e_xn.at(t, 2))
                dve.tensor_scalar(h1_e[:, :, :], h1_e[:, :, :], 0.0, None, ALU.max).then_inc(e_h1.semaphore, 1)
                dve.wait_ge(e_h1.semaphore, e_h1.at(t))
                stats_e(t, 3, h1_e)

            def ht1_evac(t):
                dve.wait_ge(e_tr1.semaphore, e_tr1.at(t))
                dve.tensor_scalar(ht_e[:, :], ps_e[:, :], gamma_sb[:, 0:1], beta_sb[:, 0:1],
                                       ALU.mult, ALU.add)\
                    .then_inc(e_ht1.semaphore, 1)

            def u_evac(t, i):
                dve.wait_ge(e_u_ps.semaphore, e_u_ps.at(t, i + 1))
                if i == 0:
                    dve.wait_ge(e_norms.semaphore, e_norms.at(t))
                for n in range(2):
                    r = 2 * i + n
                    dve.tensor_scalar(y_e[:, r, :], ps_e[:, n * 2 * D + D:(n + 1) * 2 * D],
                                      s_in_out[:, r:r + 1], None, ALU.mult)
                dve.tensor_copy(u1[:, 2 * i:2 * i + 2, :],
                                     ps_e[:, :].rearrange("p (n c) -> p n c", n=2)[:, :, 0:D])\
                    .then_inc(e_u.semaphore, 1)

            def hop1_evac(t):
                dve.wait_ge(e_hop1.semaphore, e_hop1.at(t))
                for r in range(R):
                    last = dve.scalar_tensor_tensor(out=pre[:, r, :], in0=ps_e[:, r * D:(r + 1) * D],
                                                    scalar=neg_s_out[:, r:r + 1], in1=u1[:, r, :],
                                                    op0=ALU.mult, op1=ALU.add)
                last.then_inc(e_pre.semaphore, 1)

            def residual1(t, p):
                dve.wait_ge(e_sp.semaphore, e_sp.at(t, 1))
                dve.scalar_tensor_tensor(out=pre[:, :, :], in0=pre[:, :, :], scalar=0.0,
                                              in1=X[p][:, :, :], op0=ALU.max, op1=ALU.add)\
                    .then_inc(e_part.semaphore, 1)
                dve.wait_ge(e_part.semaphore, e_part.at(t))
                dve.wait_ge(e_sp.semaphore, e_sp.at(t))
                dve.tensor_tensor(X[p][:, :, :], pre[:, :, :], softp[:, :, :], ALU.add).then_inc(e_x1.semaphore, 1)

            def mask(t, q):
                dve.tensor_scalar(M[q][:, :, :], A[q][:, :, :], 1.0, -NEG, ALU.subtract, ALU.mult)\
                    .then_inc(l_mask.semaphore, 1)

            def h2_relu(t, q):
                apply(t, 1, xn_l, X[q], mv_l, rs_l, l_rs, l_xn)
                dve.wait_ge(l_xn.semaphore, l_xn.at(t, 1))
                dve.tensor_scalar(h2[:, :, :], xn_l[:, :, :], 0.0, None, ALU.max).then_inc(l_h2.semaphore, 1)

            def hid_evac(t, b):
                dve.wait_ge(l_hid_ps.semaphore, l_hid_ps.at(t, b + 1))
                dve.tensor_scalar(hid[:, b, :], ps_l[:, :], b1_sb[:, b:b + 1], None, ALU.add)\
                    .then_inc(l_hid.semaphore, 1)

            def rms_scale(t, b):
                if b == 0:
                    dve.wait_ge(l_rms.semaphore, l_rms.at(t))
                dve.scalar_tensor_tensor(out=hid[:, b, :], in0=hid[:, b, :], scalar=rmsw_sb[:, b:b + 1],
                                              in1=rms_b[:, :], op0=ALU.mult, op1=ALU.mult)\
                    .then_inc(l_g.semaphore, 1)

            def silu_clamp(t, b):
                dve.wait_ge(l_g.semaphore, l_g.at(t, b + 1))
                dve.tensor_scalar(sq[:, b, :], hid[:, b, :], FLOOR, None, ALU.max).then_inc(l_cl.semaphore, 1)

            def silu_blocks(t):
                dve.wait_ge(l_sig.semaphore, l_sig.at(t))
                for b in range(2, 4):
                    dve.tensor_tensor(hid[:, b, :], hid[:, b, :], sq[:, b, :], ALU.mult).then_inc(l_act_v.semaphore, 1)

            def residual2(t, q):
                dve.wait_ge(l_w2_ps.semaphore, l_w2_ps.at(t))
                dve.wait_ge(l_xb.semaphore, l_xb.at(t))
                dve.tensor_tensor(XH[q][:, :, :].rearrange("p r d -> p (r d)"), ps_l[:, :],
                                       x_b2[:, :, :].rearrange("p r d -> p (r d)"), ALU.add)\
                    .then_inc(l_x2.semaphore, 1)
                dve.wait_ge(l_x2.semaphore, l_x2.at(t))
                stats_l(t, 2, XH[q])

            def h3(t, q):
                apply(t, 2, xn_l, XH[q], mv_l, rs_l, l_rs, l_xn)

            def h3_bias(t, q):
                dve.wait_ge(l_xn.semaphore, l_xn.at(t, 2))
                for r in range(R):
                    last = dve.scalar_tensor_tensor(out=ZH[q][:, r, :], in0=xn_l[:, r, :], scalar=0.0,
                                                    in1=bfin_rows[:, :], op0=ALU.max, op1=ALU.add)
                last.then_inc(l_zh.semaphore, 1)

            def qk_split(t):
                dve.wait_ge(l_qk_ps.semaphore, l_qk_ps.at(t))
                dve.tensor_scalar(qk_f[:, :], ps_l[0:QROWS, :], b_qk[:, 0:1], None, ALU.add)\
                    .then_inc(l_split.semaphore, 1)
                dve.wait_ge(l_split.semaphore, l_split.at(t, 1))
                dve.tensor_copy(qk_s[:, :], qk_f[:, :]).then_inc(l_split.semaphore, 1)
                dve.wait_ge(l_split.semaphore, l_split.at(t, 2))
                dve.tensor_tensor(qk_r[:, :], qk_f[:, :], qk_s[:, :], ALU.subtract).then_inc(l_split.semaphore, 1)
                dve.wait_ge(l_split.semaphore, l_split.at(t, 3))
                dve.tensor_copy(qk_s[32:64, :], qk_r[32:64, :])
                dve.tensor_copy(qk_s[64:96, :], qk_r[64:96, :]).then_inc(l_split.semaphore, 1)
                dve.wait_ge(l_split.semaphore, l_split.at(t, 4))
                dve.tensor_tensor(qk_s[64:96, :], qk_r[64:96, :], qk_s[64:96, :], ALU.subtract)\
                    .then_inc(l_split.semaphore, 1)

            def qk_rows(t, q):
                dve.wait_ge(l_split.semaphore, l_split.at(t))
                if due(h_qk.at(t - 2)):
                    dve.wait_ge(h_qk.semaphore, h_qk.at(t - 2))
                dve.tensor_scalar(q_rows[q][:, :], qk_s[:, :], select[:, 0:1], select[:, 1:2], ALU.mult, ALU.add)
                for h in range(HEADS):
                    last = dve.tensor_scalar(k_rows[q][:, h, :], qk_s[:, :], select[:, 2 + h:3 + h],
                                             select[:, 2 + HEADS + h:3 + HEADS + h], ALU.mult, ALU.add)
                last.then_inc(l_rows.semaphore, 1)

            def g_evac(t, q, k):
                dve.wait_ge(l_g_ps.semaphore, l_g_ps.at(t, k + 1))
                if k == 1:
                    if due(h_av.at(t - 2)):
                        dve.wait_ge(h_av.semaphore, h_av.at(t - 2))
                dve.tensor_copy(G[q][:, k // 2, 4 * (k % 2):4 * (k % 2) + 4, :].rearrange("p h d -> p (h d)"),
                                     ps_l[:, :])\
                    .then_inc(l_gv.semaphore, 1)

            def head_max(pair, u, j, q):
                if j == 0:
                    if due(h_tr.at(pair, 2 * (u - SB) + 2)):
                        dve.wait_ge(h_tr.semaphore, h_tr.at(pair, 2 * (u - SB) + 2))
                dve.wait_ge(h_qk.semaphore, h_qk.at(pair, 2 * u + j + 1))
                dve.memset(carrier(), 0.0)
                g = u // GPG
                for i in range(HALVES):
                    last = dve.tensor_tensor_reduce(S[u % SB][:, j, i, :], ps_s[j][:, i * N:(i + 1) * N],
                                                    M[q][:, HALVES * g + i, :], 1.0, -3e38, ALU.add, ALU.max,
                                                    mx[u % SB][:, 2 * j + i:2 * j + i + 1])
                last.then_inc(h_max.semaphore, 1)

            def head_leaky(pair, u):
                b = u % SB
                dve.wait_ge(h_max.semaphore, h_max.at(pair, 2 * u + 2))
                dve.tensor_scalar(ng[b][:, :], mx[b][:, :], -1.0, None, ALU.mult).then_inc(h_neg.semaphore, 1)
                flat = S[b][:, :, :, :].rearrange("p j i n -> p (j i n)")
                dve.scalar_tensor_tensor(out=flat, in0=flat, scalar=SLOPE, in1=flat, op0=ALU.mult, op1=ALU.max)
                dve.wait_ge(h_neg.semaphore, h_neg.at(pair, u + 1))
                dve.scalar_tensor_tensor(out=nm[b][:, :], in0=mx[b][:, :], scalar=-SLOPE, in1=ng[b][:, :],
                                              op0=ALU.mult, op1=ALU.min)\
                    .then_inc(h_leaky.semaphore, 1)

            def head_recip(pair, u):
                dve.wait_ge(h_exp.semaphore, h_exp.at(pair, u + 1))
                dve.reciprocal(rc[u % SB][:, :], sm[u % SB][:, :]).then_inc(h_rc.semaphore, 1)

            def final_in(pair, g, q):
                dve.wait_ge(h_av.semaphore, h_av.at(pair, 8 * (g + 1)))
                flat = zf[g][:, :, :].rearrange("p r d -> p (r d)")
                dve.tensor_tensor(flat, ps_o[g][:, 0:HALVES * D],
                                       ZH[q][:, HALVES * g:HALVES * g + HALVES, :].rearrange("p r d -> p (r d)"),
                                       ALU.add)\
                    .then_inc(f_z.semaphore, 1)
                dve.wait_ge(f_z.semaphore, f_z.at(pair, g + 1))
                dve.tensor_scalar(flat, flat, FLOOR, None, ALU.max).then_inc(f_c.semaphore, 1)

            def final_out(pair, g, q):
                dve.wait_ge(f_s.semaphore, f_s.at(pair, 3 * g + 3))
                if due(stored[g].at(pair - 1)):
                    dve.wait_ge(stored[g].semaphore, stored[g].at(pair - 1))
                dve.tensor_tensor(res[g][:, :, :], XH[q][:, HALVES * g:HALVES * g + HALVES, :], zf[g][:, :, :],
                                       ALU.add)\
                    .then_inc(f_res.semaphore, 1)

            def early(t, p, at, adj_count):
                E = AT_E
                if at == E["ln0"]:
                    dve.wait_ge(x_loaded.semaphore, x_loaded.at(t))
                    stats_e(t, 1, x_in)
                if at == E["deg"]:
                    degrees(t)
                if at == E["xn0"]:
                    apply(t, 1, xn_e, x_in, mv_e, rs_e, e_rs, e_xn)
                if at == E["deg2"] + 1:
                    degree_masks(t)
                for r in range(R):
                    if at == E[f"proj{r}"]:
                        proj_evac(t, r)
                if at == E["gate"]:
                    gate_clamp(t)
                if at == E["dif"]:
                    hop0_evac(t)
                if at == E["mix"]:
                    mix_up(t)
                if at == E["x0"]:
                    residual0(t, p)
                if at == E["h1"]:
                    h1_relu(t, p)
                if at == E["xn1"]:
                    apply(t, 3, xn_e, h1_e, mv_e, rs_e, e_rs, e_xn)
                if at == E["ht1"]:
                    ht1_evac(t)
                for i in range(2):
                    if at == E[f"u{i}"]:
                        u_evac(t, i)
                if at == E["pre"]:
                    hop1_evac(t)
                if at == E["x1"]:
                    residual1(t, p)

            def late(t, q, at):
                L = AT_L
                if at == L["mask"]:
                    mask(t, q)
                if at == L["ln2"]:
                    dve.wait_ge(e_x1.semaphore, e_x1.at(t))
                    stats_l(t, 1, X[q])
                if at == L["h2"]:
                    h2_relu(t, q)
                for b in range(HB):
                    if at == L[f"hid{b}"]:
                        hid_evac(t, b)
                for b in range(HB):
                    if at == L[f"g{b}"]:
                        rms_scale(t, b)
                for b in range(HB):
                    if at == L[f"g{b}"]:
                        silu_clamp(t, b)
                if at == L["act"]:
                    silu_blocks(t)
                if at == L["x2"]:
                    residual2(t, q)
                if at == L["xn3"]:
                    h3(t, q)
                if at == L["xn3"] + 1:
                    h3_bias(t, q)
                if at == L["split"]:
                    qk_split(t)
                if at == L["rows"]:
                    qk_rows(t, q)
                for k in range(1, 8, 2):
                    if at == L[f"g_{k}"]:
                        g_evac(t, q, k)

            def body(t, p, known):
                th = t - 2
                for s in range(GROUPS):
                    lag0 = mine(known, 2)
                    lag1 = mine(known, 2) if s >= 1 else mine(known, 3)
                    pair1, ug1, _ = group(th, s, 1, p)
                    for k in range(4):
                        if lag0 and k < 2:
                            head_max(th, s, k, p)
                        if lag0 and k == 2:
                            head_leaky(th, s)
                        if lag1 and k == 3:
                            head_recip(pair1, ug1)
                        if mine(known, 0):
                            early(t, p, 4 * s + k, None)
                        if mine(known, 1):
                            late(t - 1, 1 - p, 4 * s + k)
                        if k == 0:
                            if s == 2 and mine(known, 3):
                                final_in(t - 3, 1, 1 - p)
                            if s == 6 and mine(known, 2):
                                final_in(t - 2, 0, p)
                        if k == 3:
                            if s == 2 and mine(known, 3):
                                final_out(t - 3, 1, 1 - p)
                            if s == 6 and mine(known, 2):
                                final_out(t - 2, 0, p)

            iterations(dve, body)

        @block.tensor
        def _(pe):
            def mm(dst, left, right, start=True, stop=True):
                return pe.matmul(dst, left, right, start=start, stop=stop)

            pe.wait_ge(p_pool, 4)
            pe.wait_ge(p_load, 16 * 23)
            mm(ps_e[:, 0:3 * D + 1], ones[0:1, :], bias_row[:, :]).then_inc(p_pe, 1)
            pe.wait_ge(p_products, 1)
            mm(ps_l[:, 0:D], ones[0:1, :], bias_row[:, 2 * D:3 * D], stop=False)
            for h in range(HEADS):
                last = mm(ps_l[:, 0:D], fcb_cols[:, h, :], fp_sb[:, h, :], start=False, stop=(h == HEADS - 1))
            last.then_inc(p_pe, 1)
            for h in range(HEADS):
                last = pe.transpose(ps_t[h // 4][:, (h % 4) * P:(h % 4 + 1) * P], fc_sb[:, h * P:(h + 1) * P],
                                    ident[:, :])
            last.then_inc(p_pe, 1)
            pe.wait_ge(p_fct, 1)
            for h in range(HEADS):
                mm(ps_s[h // 4][:, (h % 4) * P:(h % 4 + 1) * P], fct[:, h * P:(h + 1) * P], fp_sb[:, h, :])
                mm(ps_o[0][:, 2 * h:2 * h + 2], fct[:, h * P:(h + 1) * P], qkw_sb[:, :])
            mm(ps_o[1][0:QROWS, 0:1], bq_prod[:, :, :].rearrange("p a n -> p (a n)"), ones[:, 0:1], stop=False)
            mm(ps_o[1][0:QROWS, 0:1], qkb_row[:, :, :].rearrange("p a n -> p (a n)"), ones[0:1, 0:1],
               start=False).then_inc(p_pe, 1)
            pe.wait_ge(p_weights, 5)

            def transposes(dst, src):
                for r in range(R):
                    last = pe.transpose(dst[:, r * P:(r + 1) * P], src[:, r, :], ident[:, :])
                return last

            def adj_transpose(t, p, g, known):
                if g == 0:
                    arrived(t, p, known)
                    if due(e_pre.at(t - 1)):
                        pe.wait_ge(e_pre.semaphore, e_pre.at(t - 1))
                else:
                    pe.wait_ge(e_at.semaphore, e_at.at(t, 1))
                for m in range(HALVES):
                    for i in range(HALVES):
                        last = pe.transpose(ps_e[:, m * N + i * P:m * N + (i + 1) * P],
                                            A[p][:, HALVES * g + i, m * P:(m + 1) * P], ident[:, :])
                last.then_inc(e_adj_tr.semaphore, 1)

            def arrived(t, p, known):
                pe.wait_ge(adj_in[p], (t - p) * 8 + 16)

            def degree_sums(t, p):
                pe.wait_ge(e_at.semaphore, e_at.at(t, 2))
                for r in range(R):
                    g, i = divmod(r, HALVES)
                    for m in range(HALVES):
                        mm(ps_e[:, r:r + 1], AT[p][:, g, m, i * P:(i + 1) * P], ones[:, 0:1],
                           start=(m == 0), stop=(m == HALVES - 1))
                    for m in range(HALVES):
                        last = mm(ps_e[:, R + r:R + r + 1], A[p][:, HALVES * g + m, i * P:(i + 1) * P], ones[:, 0:1],
                                  start=(m == 0), stop=(m == HALVES - 1))
                last.then_inc(e_deg_ps.semaphore, 1)

            def transpose0(t):
                pe.wait_ge(e_xn.semaphore, e_xn.at(t, 1))
                pe.wait_ge(e_deg.semaphore, e_deg.at(t))
                transposes(ps_e, xn_e).then_inc(e_tr0.semaphore, 1)

            def project(t, r):
                if r == 0:
                    pe.wait_ge(e_ht0.semaphore, e_ht0.at(t))
                else:
                    pe.wait_ge(e_proj.semaphore, e_proj.at(t, r))
                mm(ps_e[:, 0:3 * D], ht_e[:, r * P:(r + 1) * P], w_proj[:, :]).then_inc(e_proj_ps.semaphore, 1)

            def hop(t, p, sig):
                for r in range(R):
                    g, i = divmod(r, HALVES)
                    for m in range(HALVES):
                        last = mm(ps_e[:, r * D:(r + 1) * D], AT[p][:, g, m, i * P:(i + 1) * P],
                                  y_e[:, HALVES * g + m, :], start=(m == 0), stop=(m == HALVES - 1))
                last.then_inc(sig.semaphore, 1)

            def hop0(t, p):
                pe.wait_ge(e_proj.semaphore, e_proj.at(t, 4))
                hop(t, p, e_hop0)

            def transpose1(t):
                pe.wait_ge(e_xn.semaphore, e_xn.at(t, 3))
                transposes(ps_e, xn_e).then_inc(e_tr1.semaphore, 1)

            def mix1(t, i):
                if i == 0:
                    pe.wait_ge(e_ht1.semaphore, e_ht1.at(t))
                else:
                    pe.wait_ge(e_u.semaphore, e_u.at(t, 1))
                for n in range(2):
                    r = 2 * i + n
                    last = mm(ps_e[:, n * 2 * D:(n + 1) * 2 * D], ht_e[:, r * P:(r + 1) * P], w_l1[:, :])
                last.then_inc(e_u_ps.semaphore, 1)

            def hop1(t, p):
                pe.wait_ge(e_u.semaphore, e_u.at(t, 2))
                hop(t, p, e_hop1)

            def neighbour_sum(t, q):
                pe.wait_ge(l_h2.semaphore, l_h2.at(t))
                if due(l_ga.at(t - 1)):
                    pe.wait_ge(l_ga.semaphore, l_ga.at(t - 1))
                if due(l_gv.at(t - 1)):
                    pe.wait_ge(l_gv.semaphore, l_gv.at(t - 1))
                for g in range(2):
                    for m in range(HALVES):
                        pe.matmul(ps_l[:, g * N:(g + 1) * N], h2[:, HALVES * g + m, :], AT[q][:, g, m, :],
                                  start=(m == 0), stop=False, skip_group_check=True)
                    for i in range(HALVES):
                        last = pe.matmul(ps_l[:, g * N + i * P:g * N + (i + 1) * P], h2[:, HALVES * g + i, :],
                                         eps_ident[:, :], start=False, stop=(i == HALVES - 1),
                                         skip_group_check=True)
                last.then_inc(l_z_ps.semaphore, 1)

            def hidden(t, b):
                if b == 0:
                    pe.wait_ge(l_zt.semaphore, l_zt.at(t))
                else:
                    pe.wait_ge(l_hid.semaphore, l_hid.at(t, b))
                mm(ps_l[:, :], w1_sb[:, b * P:(b + 1) * P], zt[:, :]).then_inc(l_hid_ps.semaphore, 1)

            def squares_sum(t):
                pe.wait_ge(l_sum.semaphore, l_sum.at(t))
                pe.wait_ge(l_hid.semaphore, l_hid.at(t))
                mm(ps_l[:, :], ones[:, :], sq[:, 0, :]).then_inc(l_ss_ps.semaphore, 1)

            def down(t):
                pe.wait_ge(l_act_p.semaphore, l_act_p.at(t))
                pe.wait_ge(l_act_v.semaphore, l_act_v.at(t))
                for r in range(R):
                    for b in range(HB):
                        last = mm(ps_l[:, r * D:(r + 1) * D], hid[:, b, r * P:(r + 1) * P], w2_sb[:, b, :],
                                  start=(b == 0), stop=(b == HB - 1))
                last.then_inc(l_w2_ps.semaphore, 1)

            def transpose3(t):
                pe.wait_ge(l_xn.semaphore, l_xn.at(t, 2))
                transposes(ps_l, xn_l).then_inc(l_tr.semaphore, 1)

            def queries_keys(t):
                pe.wait_ge(l_ht.semaphore, l_ht.at(t))
                mm(ps_l[0:QROWS, :], w_qk[:, :, :].rearrange("p a n -> p (a n)"), ht_l[:, :])\
                    .then_inc(l_qk_ps.semaphore, 1)

            def head_features(t, k):
                if k == 0:
                    pe.wait_ge(l_split.semaphore, l_split.at(t, 1))
                elif k % 2:
                    pe.wait_ge(l_ga.semaphore, l_ga.at(t, k // 2 + 1))
                else:
                    pe.wait_ge(l_gv.semaphore, l_gv.at(t, k // 2))
                mm(ps_l[:, :], ht_l[:, (k // 2) * P:(k // 2 + 1) * P], w_head[:, 512 * (k % 2):512 * (k % 2) + 512])\
                    .then_inc(l_g_ps.semaphore, 1)

            def scores(pair, u, j, q):
                if u == 0 and j == 0:
                    pe.wait_ge(l_rows.semaphore, l_rows.at(pair))
                if due(h_max.at(pair, 2 * u + j - 1)):
                    pe.wait_ge(h_max.semaphore, h_max.at(pair, 2 * u + j - 1))
                g, h = u // GPG, 2 * (u % GPG) + j
                for i in range(HALVES):
                    last = mm(ps_s[j][:, i * N:(i + 1) * N], q_rows[q][:, g * N + i * P:g * N + (i + 1) * P],
                              k_rows[q][:, h, g * N:(g + 1) * N])
                last.then_inc(h_qk.semaphore, 1)

            def head_transpose(pair, u, j):
                pe.wait_ge(h_norm.semaphore, h_norm.at(pair, u + 1))
                if due(h_et.at(pair, 2 * u + j - 1)):
                    pe.wait_ge(h_et.semaphore, h_et.at(pair, 2 * u + j - 1))
                for m in range(HALVES):
                    for i in range(HALVES):
                        last = pe.transpose(ps_t[j][:, m * N + i * P:m * N + (i + 1) * P],
                                            S[u % SB][:, j, i, m * P:(m + 1) * P], ident[:, :])
                last.then_inc(h_tr.semaphore, 1)

            def attend(pair, u, j, q):
                g, h = u // GPG, 2 * (u % GPG) + j
                pe.wait_ge(h_et.semaphore, h_et.at(pair, 2 * u + j + 1))
                if u == 0 and j == 0:
                    pe.wait_ge(l_ga.semaphore, l_ga.at(pair))
                    pe.wait_ge(l_gv.semaphore, l_gv.at(pair))
                if h == 0:
                    if due(f_z.at(pair - 1, g + 1)):
                        pe.wait_ge(f_z.semaphore, f_z.at(pair - 1, g + 1))
                for i in range(HALVES):
                    for m in range(HALVES):
                        last = pe.matmul(ps_o[g][:, i * D:(i + 1) * D], ET[j][:, m, i * P:(i + 1) * P],
                                         G[q][:, HALVES * g + m, h, :],
                                         start=(h == 0 and i == 0 and m == 0),
                                         stop=(h == HEADS - 1 and m == HALVES - 1), skip_group_check=True)
                last.then_inc(h_av.semaphore, 1)

            def early(t, p, at, known):
                E = AT_E
                for g in range(2):
                    if at == E[f"adj{g}"]:
                        adj_transpose(t, p, g, known)
                if at == E["deg"]:
                    degree_sums(t, p)
                if at == E["tr0"]:
                    transpose0(t)
                for r in range(R):
                    if at == E[f"proj{r}"]:
                        project(t, r)
                if at == E["hop0"]:
                    hop0(t, p)
                if at == E["tr1"]:
                    transpose1(t)
                for i in range(2):
                    if at == E[f"u{i}"]:
                        mix1(t, i)
                if at == E["hop1"]:
                    hop1(t, p)

            def late(t, q, at):
                L = AT_L
                if at == L["z"]:
                    neighbour_sum(t, q)
                for b in range(HB):
                    if at == L[f"hid{b}"]:
                        hidden(t, b)
                if at == L["ss"]:
                    squares_sum(t)
                if at == L["w2"]:
                    down(t)
                if at == L["tr"]:
                    transpose3(t)
                if at == L["qk"]:
                    queries_keys(t)
                for k in range(8):
                    if at == L[f"g_{k}"]:
                        head_features(t, k)

            def body(t, p, known):
                th = t - 2
                for s in range(GROUPS):
                    lag0 = mine(known, 2)
                    lag2 = mine(known, 2) if s >= 2 else mine(known, 3)
                    pair2, ug2, q2 = group(th, s, 2, p)
                    for k in range(4):
                        if lag0 and k == 0:
                            scores(th, s, 0, p)
                            scores(th, s, 1, p)
                        if lag2 and k == 1:
                            head_transpose(pair2, ug2, 0)
                            head_transpose(pair2, ug2, 1)
                        if lag2 and k >= 2:
                            attend(pair2, ug2, k - 2, q2)
                        if mine(known, 0):
                            early(t, p, 4 * s + k, known)
                        if mine(known, 1):
                            late(t - 1, 1 - p, 4 * s + k)

            iterations(pe, body)


_INS = ['x', 'adj', 'L0_gnn_theta', 'L0_gnn_W_h', 'L0_gnn_W_t', 'L0_gnn_b_t', 'L1_gnn_gamma', 'L1_gnn_beta',
        'L1_gnn_W_self', 'L1_gnn_W_neigh', 'L2_gnn_epsilon', 'L2_gnn_W1', 'L2_gnn_b1', 'L2_gnn_rms_weight',
        'L2_gnn_W2', 'L2_gnn_b2', 'L3_gnn_fc_w', 'L3_gnn_fc_b', 'L3_gnn_q_w', 'L3_gnn_q_b', 'L3_gnn_k_w',
        'L3_gnn_k_b', 'L3_gnn_fp_w', 'L3_gnn_fp_b']


def row_select(heads):
    import numpy as _np
    select = _np.zeros((96, 2 + 2 * heads), _np.float32)
    for part in range(3):
        for h in range(heads):
            q, k = 32 * part + h, 32 * part + heads + h
            select[q, 0] = 1.0
            select[k, 1] = 1.0
            select[k, 2 + h] = 1.0
            select[q, 2 + heads + h] = 1.0
    return select


def kernel(**inputs):
    import numpy as _np
    import concourse.bacc as _bacc
    from concourse import mybir as _mybir
    from concourse.bass_utils import run_bass_kernel_spmd as _run

    nc = _bacc.Bacc("TRN2", target_bir_lowering=False, num_devices=1)
    arrays, args = {}, []
    for name in _INS:
        a = _np.ascontiguousarray(inputs[name])
        if a.ndim == 0:
            a = a.reshape(1, 1)
        if name == 'L2_gnn_epsilon':
            a = a.reshape(1, 1)
        arrays[f"in_{name}_dram"] = a
        args.append(nc.dram_tensor(f"in_{name}_dram", a.shape, _mybir.dt.from_np(a.dtype), kind="ExternalInput").ap())
    select = row_select(8)
    arrays["row_select_dram"] = select
    args.append(nc.dram_tensor("row_select_dram", select.shape, _mybir.dt.float32, kind="ExternalInput").ap())
    shape = tuple(inputs['x'].shape)
    args.append(nc.dram_tensor("out_0_dram", shape, _mybir.dt.float32, kind="ExternalOutput").ap())
    four_layer_gnn_kernel(nc, *args)
    r = _run(nc, [arrays], core_ids=[0])
    return r.results[0]["out_0_dram"]
```

```python
import concourse.bass as bass
from concourse import mybir
from contextlib import ExitStack


class Signal:

    def __init__(self, semaphore, per_pair):
        self.semaphore = semaphore
        self.per_pair = per_pair

    def at(self, pair, k=None):
        return pair * self.per_pair + (self.per_pair if k is None else k)


def due(count):
    return not isinstance(count, int) or count > 0


def four_layer_gnn_kernel(nc, x, adj, theta, w_h, w_t, b_t, gamma, beta, w_self, w_neigh, epsilon,
                          w1, b1, rms_w, w2, b2, fc_w, fc_b, q_w, q_b, k_w, k_b, fp_w, fp_b,
                          row_select, out):
    fp32 = mybir.dt.float32
    bf16 = mybir.dt.bfloat16
    ALU = mybir.AluOpType
    ACT = mybir.ActivationFunctionType

    B, N, D = x.shape
    P = 128
    HALVES = N // P
    R = 2 * HALVES
    PAIRS = B // 2
    HID = w1.shape[1]
    HB = HID // P
    HEADS = fc_w.shape[1] // D
    GROUPS = 2 * HEADS // 2
    GPG = GROUPS // 2
    QROWS = 96
    SLOPE = 0.01
    NEG = -1e9
    FLOOR = -40.0
    HUGE = 3e38
    SB = 4
    LOADED = 16

    adj_v = adj.rearrange("b n m -> (b n) m").rearrange("(t r p) m -> t p r m", r=R, p=P)
    x_v = x.rearrange("b n d -> (b n) d").rearrange("(t r p) d -> t p r d", r=R, p=P)
    out_v = out.rearrange("b n d -> (b n) d").rearrange("(b r p) d -> b p r d", r=HALVES, p=P)

    ctx = ExitStack()
    with ctx:
        def sb(name, shape, dt=fp32):
            return ctx.enter_context(nc.sbuf_tensor(name, shape, dt))

        def sem(name):
            return ctx.enter_context(nc.semaphore(name))

        def signal(name, per_pair=1):
            return Signal(sem(name), per_pair)

        ident = sb("ident", [P, P])
        ones = sb("ones", [P, P])
        eps_ident = sb("eps_ident", [P, P])
        w_proj = sb("w_proj", [P, 3 * D])
        w_l1 = sb("w_l1", [P, 2 * D])
        w1_sb = sb("w1_sb", [P, HID])
        w2_sb = sb("w2_sb", [P, HB, D])
        b1_sb = sb("b1_sb", [P, HB])
        rmsw_sb = sb("rmsw_sb", [P, HB])
        gamma_sb = sb("gamma_sb", [P, 1])
        beta_sb = sb("beta_sb", [P, 1])
        w_head = sb("w_head", [P, HEADS * D])
        w_qk = sb("w_qk", [P, 3, 32])
        b_qk = sb("b_qk", [QROWS, 1])
        select = sb("select", [QROWS, 2 + 2 * HEADS])
        bt_rows = sb("bt_rows", [P, D])
        b2_rows = sb("b2_rows", [P, D])
        bfin_rows = sb("bfin_rows", [P, D])
        eps_col = sb("eps_col", [P, 1])
        bias_row = sb("bias_row", [1, 3 * D + 1])
        qkw_sb = sb("qkw_sb", [P, 2])
        qkb_sb = sb("qkb_sb", [1, 2])
        qkb_row = sb("qkb_row", [1, 3, 32])
        fcb_sb = sb("fcb_sb", [P, HEADS])
        bq_prod = sb("bq_prod", [P, 3, 32])
        ln_guard = sb("ln_guard", [P, 1])
        rms_guard = sb("rms_guard", [P, 1])
        fence = sb("fence", [P, 16])
        fence_pool = sb("fence_pool", [P, 32])

        A = [sb(f"A{i}", [P, R, N]) for i in range(2)]
        AT = [sb(f"AT{i}", [P, 2, HALVES, N]) for i in range(2)]
        M = [sb(f"M{i}", [P, R, N]) for i in range(2)]
        x_in = sb("x_in", [P, R, D])
        X = [sb(f"X{i}", [P, R, D]) for i in range(2)]
        XH = [sb(f"XH{i}", [P, R, D]) for i in range(2)]
        ZH = [sb(f"ZH{i}", [P, R, D]) for i in range(2)]
        G = [sb(f"G{i}", [P, R, HEADS, D]) for i in range(2)]
        q_rows = [sb(f"q_rows{i}", [QROWS, 2 * N], bf16) for i in range(2)]
        k_rows = [sb(f"k_rows{i}", [QROWS, HEADS, 2 * N], bf16) for i in range(2)]

        st_e = sb("st_e", [P, R, 6])
        mv_e = sb("mv_e", [P, R, 2])
        lv_e = sb("lv_e", [P, R])
        rs_e = sb("rs_e", [P, R])
        xn_e = sb("xn_e", [P, R, D])
        h1_e = sb("h1_e", [P, R, D])
        ht_e = sb("ht_e", [P, R * P])
        y_e = sb("y_e", [P, R, D])
        het = sb("het", [P, R, D])
        gate = sb("gate", [P, R, D])
        mix = sb("mix", [P, R, D])
        elu = sb("elu", [P, R, D])
        deg = sb("deg", [P, 12])
        degc = sb("degc", [P, 12])
        scl = sb("scl", [P, 12])
        s_in_out = sb("s_in_out", [P, 8])
        neg_s_out = sb("neg_s_out", [P, R])
        u1 = sb("u1", [P, R, D])
        pre = sb("pre", [P, R, D])
        softp = sb("softp", [P, R, D])

        st_l = sb("st_l", [P, R, 6])
        mv_l = sb("mv_l", [P, R, 2])
        lv_l = sb("lv_l", [P, R])
        rs_l = sb("rs_l", [P, R])
        xn_l = sb("xn_l", [P, R, D])
        h2 = sb("h2", [P, R, D])
        zt = sb("zt", [P, R * P])
        hid = sb("hid", [P, HB, R * P])
        sq = sb("sq", [P, HB, R * P])
        rms_b = sb("rms_b", [P, R * P])
        x_b2 = sb("x_b2", [P, R, D])
        ht_l = sb("ht_l", [P, R * P])
        qk_f = sb("qk_f", [QROWS, 2 * N])
        qk_r = sb("qk_r", [QROWS, 2 * N])
        qk_s = sb("qk_s", [QROWS, 2 * N], bf16)

        S = [sb(f"S{i}", [P, 2, HALVES, N]) for i in range(SB)]
        mx = [sb(f"mx{i}", [P, 4]) for i in range(SB)]
        ng = [sb(f"ng{i}", [P, 4]) for i in range(SB)]
        nm = [sb(f"nm{i}", [P, 4]) for i in range(SB)]
        sm = [sb(f"sm{i}", [P, 4]) for i in range(SB)]
        rc = [sb(f"rc{i}", [P, 4]) for i in range(SB)]
        ET = [sb(f"ET{i}", [P, HALVES, N]) for i in range(2)]
        zf = [sb(f"zf{i}", [P, HALVES, D]) for i in range(2)]
        res = [sb(f"res{i}", [P, HALVES, D]) for i in range(2)]

        fc_sb = hid[:, 0:2, :].rearrange("p a n -> p (a n)")
        fct = hid[:, 2:4, :].rearrange("p a n -> p (a n)")
        fp_sb = sq[:, 0:2, :].rearrange("p a n -> p (a n)").rearrange("p (h d) -> p h d", d=D)
        fcb_cols = sq[:, 2:4, :].rearrange("p a n -> p (a n)").rearrange("p (h d) -> p h d", d=D)
        ws_sb = xn_l[:, 0, :]

        def bank(name):
            return ctx.enter_context(nc.psum_tensor(name, [P, 512], fp32))

        ps_e, ps_l = bank("ps_e"), bank("ps_l")
        ps_s = [bank(f"ps_s{i}") for i in range(2)]
        ps_t = [bank(f"ps_t{i}") for i in range(2)]
        ps_o = [bank(f"ps_o{i}") for i in range(2)]

        p_load = sem("p_load")
        p_pool = sem("p_pool")
        p_pe = sem("p_pe")
        p_zeroed = sem("p_zeroed")
        p_products = sem("p_products")
        p_rows = sem("p_rows")
        p_fct = sem("p_fct")
        p_weights = sem("p_weights")
        adj_in = [sem(f"adj_in{i}") for i in range(2)]
        x_loaded = signal("x_loaded", LOADED)
        stored = [signal(f"stored{i}", LOADED) for i in range(2)]
        e_adj_tr = signal("e_adj_tr", 2)
        e_at = signal("e_at", 2)
        e_deg_ps = signal("e_deg_ps")
        e_deg = signal("e_deg")
        e_degc = signal("e_degc")
        e_scl = signal("e_scl", 2)
        e_masked = signal("e_masked")
        e_norms = signal("e_norms")
        e_bn = signal("e_bn", 3)
        e_mv = signal("e_mv", 3)
        e_lv = signal("e_lv", 3)
        e_rs = signal("e_rs", 3)
        e_xn = signal("e_xn", 3)
        e_h1 = signal("e_h1")
        e_tr0 = signal("e_tr0")
        e_ht0 = signal("e_ht0")
        e_proj_ps = signal("e_proj_ps", 4)
        e_proj = signal("e_proj", 4)
        e_clamped = signal("e_clamped")
        e_gate = signal("e_gate", 3)
        e_hop0 = signal("e_hop0")
        e_dif = signal("e_dif")
        e_gated = signal("e_gated")
        e_mix = signal("e_mix")
        e_min = signal("e_min")
        e_expm = signal("e_expm")
        e_elu = signal("e_elu")
        e_x0 = signal("e_x0")
        e_tr1 = signal("e_tr1")
        e_ht1 = signal("e_ht1")
        e_u_ps = signal("e_u_ps", 2)
        e_u = signal("e_u", 2)
        e_hop1 = signal("e_hop1")
        e_pre = signal("e_pre")
        e_sp = signal("e_sp", 3)
        e_part = signal("e_part")
        e_x1 = signal("e_x1")
        l_mask = signal("l_mask")
        l_bn = signal("l_bn", 2)
        l_mv = signal("l_mv", 2)
        l_lv = signal("l_lv", 2)
        l_rs = signal("l_rs", 2)
        l_xn = signal("l_xn", 2)
        l_h2 = signal("l_h2")
        l_z_ps = signal("l_z_ps")
        l_zt = signal("l_zt")
        l_hid_ps = signal("l_hid_ps", 4)
        l_hid = signal("l_hid", 4)
        l_sq = signal("l_sq", 4)
        l_sum = signal("l_sum", 3)
        l_ss_ps = signal("l_ss_ps")
        l_rms = signal("l_rms", 2)
        l_g = signal("l_g", 4)
        l_cl = signal("l_cl", 4)
        l_sig = signal("l_sig", 6)
        l_act = signal("l_act", 4)
        l_w2_ps = signal("l_w2_ps")
        l_xb = signal("l_xb")
        l_x2 = signal("l_x2")
        l_tr = signal("l_tr")
        l_ht = signal("l_ht")
        l_zh = signal("l_zh")
        l_qk_ps = signal("l_qk_ps")
        l_split = signal("l_split", 5)
        l_rows = signal("l_rows")
        l_g_ps = signal("l_g_ps", 8)
        l_features = signal("l_features", 8)
        h_qk = signal("h_qk", 16)
        h_max = signal("h_max", 16)
        h_neg = signal("h_neg", 8)
        h_leaky = signal("h_leaky", 8)
        h_exp = signal("h_exp", 8)
        h_rc = signal("h_rc", 8)
        h_norm = signal("h_norm", 8)
        h_tr = signal("h_tr", 16)
        h_et = signal("h_et", 16)
        h_av = signal("h_av", 16)
        f_z = signal("f_z", 2)
        f_c = signal("f_c", 2)
        f_s = signal("f_s", 6)
        f_res = signal("f_res", 2)

        def iterations(engine, body):
            for t in range(5):
                body(t, t % 2, t)
            with engine.Fori(5, PAIRS - 2, 2) as t:
                body(t, 1, None)
                body(t + 1, 0, None)
            for t in range(PAIRS - 1, PAIRS + 3):
                body(t, t % 2, t)

        def mine(known, back):
            return known is None or 0 <= known - back < PAIRS

        block = ctx.enter_context(nc.Block())

        @block.sync
        def _(sp):
            for dst, src in (
                (w_proj[:, 0:D], theta), (w_proj[:, D:2 * D], w_h), (w_proj[:, 2 * D:3 * D], w_t),
                (ws_sb, w_self), (w_l1[:, D:2 * D], w_neigh), (w1_sb[:, :], w1),
                (w2_sb[:, :, :], w2.rearrange("(b p) d -> p b d", p=P)),
                (fc_sb, fc_w), (fp_sb, fp_w.rearrange("(h e) d -> e h d", e=P)),
                (gamma_sb[:, :], gamma.rearrange("(p a) -> p a", a=1)),
                (beta_sb[:, :], beta.rearrange("(p a) -> p a", a=1)),
                (qkw_sb[:, 0:1], q_w), (qkw_sb[:, 1:2], k_w),
                (qkb_sb[:, 0:1], q_b.rearrange("(a n) -> a n", a=1)),
                (qkb_sb[:, 1:2], k_b.rearrange("(a n) -> a n", a=1)),
                (bias_row[:, 0:D], b_t.rearrange("(a n) -> a n", a=1)),
                (bias_row[:, D:2 * D], b2.rearrange("(a n) -> a n", a=1)),
                (bias_row[:, 2 * D:3 * D], fp_b.rearrange("(a n) -> a n", a=1)),
                (bias_row[:, 3 * D:3 * D + 1], epsilon),
                (select[:, :], row_select),
            ):
                sp.dma_start(dst, src).then_inc(p_load, 16)
            with nc.allow_non_contiguous_dma(reason="three short vectors, once"):
                sp.dma_start(b1_sb[:, :], b1.rearrange("(b p) -> p b", p=P)).then_inc(p_load, 16)
                sp.dma_start(rmsw_sb[:, :], rms_w.rearrange("(b p) -> p b", p=P)).then_inc(p_load, 16)
                sp.dma_start(fcb_sb[:, :], fc_b.rearrange("(h e) -> e h", e=P)).then_inc(p_load, 16)

            def load_adj(t, p, k):
                sp.dma_start(A[p][:, :, :], adj_v[t]).then_inc(adj_in[p], 16)

            load_adj(0, 0, 0)
            sp.dma_start(x_in[:, :, :], x_v[0]).then_inc(x_loaded.semaphore, 16)

            def store(pair, g):
                sp.wait_ge(f_res.semaphore, f_res.at(pair, g + 1))
                sp.dma_start(out_v[pair * 2 + g], res[g][:, :, :]).then_inc(stored[g].semaphore, 16)

            def body(t, p, known):
                if mine(known, 3):
                    store(t - 3, 1)
                if known is None or known + 1 < PAIRS:
                    if due(l_mask.at(t - 1)):
                        sp.wait_ge(l_mask.semaphore, l_mask.at(t - 1))
                    if due(e_deg_ps.at(t - 1)):
                        sp.wait_ge(e_deg_ps.semaphore, e_deg_ps.at(t - 1))
                    load_adj(t + 1, 1 - p, None)
                    sp.wait_ge(e_x0.semaphore, e_x0.at(t))
                    sp.dma_start(x_in[:, :, :], x_v[t + 1]).then_inc(x_loaded.semaphore, 16)
                if mine(known, 2):
                    store(t - 2, 0)

            iterations(sp, body)
            for g in range(2):
                sp.wait_ge(stored[g].semaphore, stored[g].at(PAIRS - 1))

        @block.gpsimd
        def _(pool):
            pool.memset(ident[:, :], 0.0).then_inc(p_pool, 1)
            pool.memset(ones[:, :], 1.0).then_inc(p_pool, 1)
            pool.memset(fence_pool[:, :], 0.0).then_inc(p_pool, 1)
            pool.wait_ge(p_pool, 3)
            pool.affine_select(out=ident[:, :], in_=ident[:, :], compare_op=ALU.not_equal, fill=1.0,
                               base=0, pattern=[[-1, P]], channel_multiplier=1).then_inc(p_pool, 1)
            pool.wait_ge(p_weights, 5)

            def residual_bias(tl, q):
                pool.wait_ge(e_x1.semaphore, e_x1.at(tl))
                if due(l_x2.at(tl - 1)):
                    pool.wait_ge(l_x2.semaphore, l_x2.at(tl - 1))
                pool.tensor_tensor(x_b2[:, 0, :], X[q][:, 0, :], b2_rows[:, :], ALU.add)
                for r in range(1, R):
                    last = pool.tensor_tensor(x_b2[:, r, :], X[q][:, r, :], b2_rows[:, :], ALU.add)
                last.then_inc(l_xb.semaphore, 1)

            carried = [0]

            def carrier():
                carried[0] += 1
                column = 4 + carried[0] % 28
                return fence_pool[:, column:column + 1], fence_pool[:, 0:1], fence_pool[:, 1:2]

            def residual0(t, p):
                pool.wait_ge(e_elu.semaphore, e_elu.at(t))
                pool.tensor_tensor(X[p][:, :, :], x_in[:, :, :], mix[:, :, :], ALU.add)\
                    .then_inc(e_x0.semaphore, 1)

            def residual1(t, p):
                pool.wait_ge(e_part.semaphore, e_part.at(t))
                pool.wait_ge(e_sp.semaphore, e_sp.at(t))
                pool.tensor_tensor(X[p][:, :, :], pre[:, :, :], softp[:, :, :], ALU.add)\
                    .then_inc(e_x1.semaphore, 1)

            def gate_clamp(t):
                pool.wait_ge(e_proj.semaphore, e_proj.at(t))
                pool.tensor_tensor(*carrier(), ALU.add)
                pool.tensor_scalar(gate[:, :, :], gate[:, :, :], HUGE, FLOOR, ALU.min, ALU.max)\
                    .then_inc(e_clamped.semaphore, 1)

            def mask(t, q):
                if due(h_max.at(t - 2)):
                    pool.wait_ge(h_max.semaphore, h_max.at(t - 2))
                    pool.tensor_tensor(*carrier(), ALU.add)
                pool.wait_ge(e_deg_ps.semaphore, e_deg_ps.at(t))
                pool.tensor_tensor(*carrier(), ALU.add)
                pool.tensor_scalar(M[q][:, :, :], A[q][:, :, :], -1.0, -NEG, ALU.add, ALU.mult)\
                    .then_inc(l_mask.semaphore, 1)

            def sum_squares(t, n):
                a, b = ((0, 1), (2, 3), (0, 2))[n]
                if n < 2:
                    pool.wait_ge(l_sq.semaphore, l_sq.at(t, 2 * n + 2))
                else:
                    pool.wait_ge(l_sum.semaphore, l_sum.at(t, 2))
                pool.tensor_tensor(sq[:, a, :], sq[:, a, :], sq[:, b, :], ALU.add)\
                    .then_inc(l_sum.semaphore, 1)

            def silu_clamp(t, b):
                pool.wait_ge(l_g.semaphore, l_g.at(t, b + 1))
                pool.tensor_tensor(*carrier(), ALU.add)
                pool.tensor_scalar(sq[:, b, :], hid[:, b, :], HUGE, FLOOR, ALU.min, ALU.max)\
                    .then_inc(l_cl.semaphore, 1)

            def silu_block(t, b):
                pool.wait_ge(l_sig.semaphore, l_sig.at(t, 5 + b // 2))
                pool.tensor_tensor(hid[:, b, :], hid[:, b, :], sq[:, b, :], ALU.mult)\
                    .then_inc(l_act.semaphore, 1)

            def final_clamp(pair, g):
                flat = zf[g][:, :, :].rearrange("p r d -> p (r d)")
                pool.wait_ge(f_z.semaphore, f_z.at(pair, g + 1))
                pool.tensor_tensor(*carrier(), ALU.add)
                pool.tensor_scalar(flat, flat, HUGE, FLOOR, ALU.min, ALU.max).then_inc(f_c.semaphore, 1)

            def normalise(pair, u):
                pool.wait_ge(h_rc.semaphore, h_rc.at(pair, u + 1))
                pool.tensor_tensor(*carrier(), ALU.add)
                for k in range(4):
                    row = S[u % SB][:, k // 2, k % 2, :]
                    last = pool.tensor_scalar(row, row, rc[u % SB][:, k:k + 1], 1.0, ALU.mult, ALU.mult)
                last.then_inc(h_norm.semaphore, 1)

            def body(t, p, known):
                early, late, heads, tail = (mine(known, back) for back in range(4))
                if tail:
                    normalise(t - 3, 3)
                    normalise(t - 3, 4)
                    normalise(t - 3, 5)
                if late:
                    residual1(t - 1, 1 - p)
                    mask(t - 1, 1 - p)
                    residual_bias(t - 1, 1 - p)
                if tail:
                    normalise(t - 3, 6)
                    final_clamp(t - 3, 0)
                    normalise(t - 3, 7)
                if late:
                    sum_squares(t - 1, 0)
                if early:
                    gate_clamp(t)
                if late:
                    sum_squares(t - 1, 1)
                    sum_squares(t - 1, 2)
                if heads:
                    normalise(t - 2, 0)
                if early:
                    residual0(t, p)
                if late:
                    silu_clamp(t - 1, 0)
                    silu_clamp(t - 1, 1)
                    silu_clamp(t - 1, 2)
                    silu_clamp(t - 1, 3)
                if heads:
                    normalise(t - 2, 1)
                    normalise(t - 2, 2)
                if late:
                    silu_block(t - 1, 0)
                    silu_block(t - 1, 1)
                    silu_block(t - 1, 2)
                    silu_block(t - 1, 3)
                if tail:
                    final_clamp(t - 3, 1)

            iterations(pool, body)

        @block.scalar
        def _(act):
            act.preload_act_table_set("natural_log_exp_and_others")
            act.wait_ge(p_weights, 5)

            def adj_evac(t, p, g):
                act.wait_ge(e_adj_tr.semaphore, e_adj_tr.at(t, g + 1))
                act.activation(AT[p][:, g, :, :].rearrange("p a n -> p (a n)"), ps_e[:, :], ACT.Copy)\
                    .then_inc(e_at.semaphore, 1)

            def degree_roots(t):
                act.wait_ge(e_degc.semaphore, e_degc.at(t))
                act.activation(degc[:, :], degc[:, :], ACT.Ln).then_inc(e_scl.semaphore, 1)
                act.wait_ge(e_scl.semaphore, e_scl.at(t, 1))
                act.activation(scl[:, :], degc[:, :], ACT.Exp, scale=-0.5).then_inc(e_scl.semaphore, 1)

            def rstd(t, k, mv, lv, rs, s_mv, s_lv, s_rs):
                act.wait_ge(s_mv.semaphore, s_mv.at(t, k))
                act.activation(lv[:, :], mv[:, :, 1], ACT.Ln, bias=ln_guard[:, 0:1]).then_inc(s_lv.semaphore, 1)
                act.wait_ge(s_lv.semaphore, s_lv.at(t, k))
                act.activation(rs[:, :], lv[:, :], ACT.Exp, scale=-0.5).then_inc(s_rs.semaphore, 1)

            def rstd_e(t, k):
                rstd(t, k, mv_e, lv_e, rs_e, e_mv, e_lv, e_rs)

            def rstd_l(t, k):
                rstd(t, k, mv_l, lv_l, rs_l, l_mv, l_lv, l_rs)

            def relu_t0(t):
                act.wait_ge(e_tr0.semaphore, e_tr0.at(t))
                act.activation(ht_e[:, :], ps_e[:, :], ACT.Relu).then_inc(e_ht0.semaphore, 1)

            def gate_sigmoid(t):
                flat = gate[:, :, :].rearrange("p r d -> p (r d)")
                act.wait_ge(e_clamped.semaphore, e_clamped.at(t))
                act.activation(flat, flat, ACT.Exp, scale=-1.0).then_inc(e_gate.semaphore, 1)
                act.wait_ge(e_gate.semaphore, e_gate.at(t, 1))
                act.activation(flat, flat, ACT.Ln, bias=1.0).then_inc(e_gate.semaphore, 1)
                act.wait_ge(e_gate.semaphore, e_gate.at(t, 2))
                act.activation(flat, flat, ACT.Exp, scale=-1.0).then_inc(e_gate.semaphore, 1)

            def elu_exp(t):
                flat = elu[:, :, :].rearrange("p r d -> p (r d)")
                act.wait_ge(e_min.semaphore, e_min.at(t))
                act.activation(flat, flat, ACT.Exp).then_inc(e_expm.semaphore, 1)

            def softplus(t):
                flat = softp[:, :, :].rearrange("p r d -> p (r d)")
                act.wait_ge(e_pre.semaphore, e_pre.at(t))
                act.activation(flat, pre[:, :, :].rearrange("p r d -> p (r d)"), ACT.Abs).then_inc(e_sp.semaphore, 1)
                act.wait_ge(e_sp.semaphore, e_sp.at(t, 1))
                act.activation(flat, flat, ACT.Exp, scale=-1.0).then_inc(e_sp.semaphore, 1)
                act.wait_ge(e_sp.semaphore, e_sp.at(t, 2))
                act.activation(flat, flat, ACT.Ln, bias=1.0).then_inc(e_sp.semaphore, 1)

            def zt_evac(t):
                act.wait_ge(l_z_ps.semaphore, l_z_ps.at(t))
                act.activation(zt[:, :], ps_l[:, :], ACT.Copy).then_inc(l_zt.semaphore, 1)

            def hid_evac(t, b):
                act.wait_ge(l_hid_ps.semaphore, l_hid_ps.at(t, b + 1))
                act.activation(hid[:, b, :], ps_l[:, :], ACT.Identity, bias=b1_sb[:, b:b + 1])\
                    .then_inc(l_hid.semaphore, 1)

            def square(t, b):
                act.wait_ge(l_hid.semaphore, l_hid.at(t, b + 1))
                act.activation(sq[:, b, :], hid[:, b, :], ACT.Square).then_inc(l_sq.semaphore, 1)

            def rms(t):
                act.wait_ge(l_ss_ps.semaphore, l_ss_ps.at(t))
                act.activation(rms_b[:, :], ps_l[:, :], ACT.Ln, bias=rms_guard[:, 0:1], scale=1.0 / HID)\
                    .then_inc(l_rms.semaphore, 1)
                act.wait_ge(l_rms.semaphore, l_rms.at(t, 1))
                act.activation(rms_b[:, :], rms_b[:, :], ACT.Exp, scale=-0.5).then_inc(l_rms.semaphore, 1)

            def half(i):
                return sq[:, 2 * i:2 * i + 2, :].rearrange("p b n -> p (b n)")

            def silu_exp(t, i):
                act.wait_ge(l_cl.semaphore, l_cl.at(t, 2 * i + 2))
                act.activation(half(i), half(i), ACT.Exp, scale=-1.0).then_inc(l_sig.semaphore, 1)

            def silu_ln(t, i):
                act.wait_ge(l_sig.semaphore, l_sig.at(t, 1 + i))
                act.activation(half(i), half(i), ACT.Ln, bias=1.0).then_inc(l_sig.semaphore, 1)

            def silu_sig(t, i):
                act.wait_ge(l_sig.semaphore, l_sig.at(t, 3 + i))
                act.activation(half(i), half(i), ACT.Exp, scale=-1.0).then_inc(l_sig.semaphore, 1)

            def relu_t3(t):
                act.wait_ge(l_tr.semaphore, l_tr.at(t))
                act.activation(ht_l[:, :], ps_l[:, :], ACT.Relu).then_inc(l_ht.semaphore, 1)

            def g_evac(t, q, k):
                act.wait_ge(l_g_ps.semaphore, l_g_ps.at(t, k + 1))
                if k == 0:
                    if due(h_av.at(t - 2)):
                        act.wait_ge(h_av.semaphore, h_av.at(t - 2))
                act.activation(G[q][:, k // 2, 4 * (k % 2):4 * (k % 2) + 4, :].rearrange("p h d -> p (h d)"),
                                    ps_l[:, :], ACT.Copy)\
                    .then_inc(l_features.semaphore, 1)

            def exp(pair, u, k):
                if k == 0:
                    act.wait_ge(h_leaky.semaphore, h_leaky.at(pair, u + 1))
                row = S[u % SB][:, k // 2, k % 2, :]
                ins = act.activation(row, row, ACT.Exp, bias=nm[u % SB][:, k:k + 1],
                                     accum_out=sm[u % SB][:, k:k + 1])
                if k == 3:
                    ins.then_inc(h_exp.semaphore, 1)

            def et_evac(pair, u, j):
                act.wait_ge(h_tr.semaphore, h_tr.at(pair, 2 * u + j + 1))
                if due(h_av.at(pair, 2 * u + j - 1)):
                    act.wait_ge(h_av.semaphore, h_av.at(pair, 2 * u + j - 1))
                act.activation(ET[j][:, :, :].rearrange("p a n -> p (a n)"), ps_t[j][:, :], ACT.Copy)\
                    .then_inc(h_et.semaphore, 1)

            def final_sigmoid(pair, g):
                flat = zf[g][:, :, :].rearrange("p r d -> p (r d)")
                act.wait_ge(f_c.semaphore, f_c.at(pair, g + 1))
                act.activation(flat, flat, ACT.Exp, scale=-1.0).then_inc(f_s.semaphore, 1)
                act.wait_ge(f_s.semaphore, f_s.at(pair, 3 * g + 1))
                act.activation(flat, flat, ACT.Ln, bias=1.0).then_inc(f_s.semaphore, 1)
                act.wait_ge(f_s.semaphore, f_s.at(pair, 3 * g + 2))
                act.activation(flat, flat, ACT.Exp, scale=-1.0).then_inc(f_s.semaphore, 1)

            def body(t, p, known):
                early, late, heads, tail = (mine(known, back) for back in range(4))
                if tail:
                    et_evac(t - 3, 3, 0)
                    exp(t - 3, 5, 1)
                    exp(t - 3, 5, 2)
                if heads:
                    relu_t3(t - 2)
                if late:
                    softplus(t - 1)
                if tail:
                    exp(t - 3, 5, 3)
                    et_evac(t - 3, 3, 1)
                if heads:
                    g_evac(t - 2, p, 0)
                if tail:
                    et_evac(t - 3, 4, 0)
                    exp(t - 3, 6, 0)
                if heads:
                    g_evac(t - 2, p, 1)
                if tail:
                    exp(t - 3, 6, 1)
                    exp(t - 3, 6, 2)
                if heads:
                    g_evac(t - 2, p, 2)
                if tail:
                    exp(t - 3, 6, 3)
                if early:
                    adj_evac(t, p, 0)
                if heads:
                    g_evac(t - 2, p, 3)
                if tail:
                    et_evac(t - 3, 4, 1)
                    exp(t - 3, 7, 0)
                if heads:
                    g_evac(t - 2, p, 4)
                if early:
                    rstd_e(t, 1)
                    adj_evac(t, p, 1)
                if heads:
                    g_evac(t - 2, p, 5)
                if tail:
                    et_evac(t - 3, 5, 0)
                    exp(t - 3, 7, 1)
                if heads:
                    g_evac(t - 2, p, 6)
                if tail:
                    exp(t - 3, 7, 2)
                    exp(t - 3, 7, 3)
                if heads:
                    g_evac(t - 2, p, 7)
                if late:
                    rstd_l(t - 1, 1)
                if tail:
                    et_evac(t - 3, 5, 1)
                if early:
                    degree_roots(t)
                    relu_t0(t)
                if heads:
                    exp(t - 2, 0, 0)
                    exp(t - 2, 0, 1)
                if tail:
                    et_evac(t - 3, 6, 0)
                if late:
                    zt_evac(t - 1)
                if tail:
                    final_sigmoid(t - 3, 0)
                if late:
                    hid_evac(t - 1, 0)
                if heads:
                    exp(t - 2, 0, 2)
                if late:
                    square(t - 1, 0)
                    hid_evac(t - 1, 1)
                    square(t - 1, 1)
                if heads:
                    exp(t - 2, 0, 3)
                if late:
                    hid_evac(t - 1, 2)
                    square(t - 1, 2)
                    hid_evac(t - 1, 3)
                    square(t - 1, 3)
                if early:
                    gate_sigmoid(t)
                if tail:
                    et_evac(t - 3, 6, 1)
                    et_evac(t - 3, 7, 0)
                if early:
                    elu_exp(t)
                if late:
                    rms(t - 1)
                if heads:
                    exp(t - 2, 1, 0)
                    exp(t - 2, 1, 1)
                    exp(t - 2, 1, 2)
                    exp(t - 2, 1, 3)
                if tail:
                    et_evac(t - 3, 7, 1)
                if heads:
                    exp(t - 2, 2, 0)
                    et_evac(t - 2, 0, 0)
                if early:
                    rstd_e(t, 2)
                if heads:
                    exp(t - 2, 2, 1)
                    exp(t - 2, 2, 2)
                    exp(t - 2, 2, 3)
                if late:
                    silu_exp(t - 1, 0)
                if early:
                    rstd_e(t, 3)
                if heads:
                    et_evac(t - 2, 0, 1)
                    exp(t - 2, 3, 0)
                if late:
                    silu_exp(t - 1, 1)
                    silu_ln(t - 1, 0)
                    silu_ln(t - 1, 1)
                    silu_sig(t - 1, 0)
                if heads:
                    et_evac(t - 2, 1, 0)
                    exp(t - 2, 3, 1)
                if late:
                    silu_sig(t - 1, 1)
                if heads:
                    exp(t - 2, 3, 2)
                    exp(t - 2, 3, 3)
                    et_evac(t - 2, 1, 1)
                    exp(t - 2, 4, 0)
                    exp(t - 2, 4, 1)
                    et_evac(t - 2, 2, 0)
                    exp(t - 2, 4, 2)
                    exp(t - 2, 4, 3)
                    et_evac(t - 2, 2, 1)
                    exp(t - 2, 5, 0)
                if tail:
                    final_sigmoid(t - 3, 1)
                if late:
                    rstd_l(t - 1, 2)

            iterations(act, body)

        @block.vector
        def _(dve):
            dve.memset(w_qk[:, :, :], 0.0).then_inc(p_zeroed, 1)
            dve.memset(bq_prod[:, :, :], 0.0).then_inc(p_zeroed, 1)
            dve.memset(qkb_row[:, :, :], 0.0).then_inc(p_zeroed, 1)
            dve.memset(ln_guard[:, :], 1e-5)
            dve.memset(rms_guard[:, :], 1e-6)
            dve.memset(fcb_cols, 0.0).then_inc(p_zeroed, 1)
            dve.wait_ge(p_load, 16 * 23)
            dve.wait_ge(p_zeroed, 4)
            dve.tensor_tensor(w_l1[:, 0:D], ws_sb, w_l1[:, D:2 * D], ALU.add)
            for part in range(3):
                for kind in range(2):
                    dve.tensor_scalar(bq_prod[:, part, 8 * kind:8 * kind + 8], fcb_sb[:, :],
                                      qkw_sb[:, kind:kind + 1], None, ALU.mult)
                    dve.tensor_scalar(qkb_row[:, part, 8 * kind:8 * kind + 8], qkb_row[:, part, 8 * kind:8 * kind + 8],
                                      qkb_sb[:, kind:kind + 1], None, ALU.add)
            for h in range(HEADS):
                last = dve.tensor_scalar(fcb_cols[:, h, :], fcb_cols[:, h, :], fcb_sb[:, h:h + 1], None, ALU.add)
            last.then_inc(p_products, 1)
            dve.wait_ge(p_pe, 1)
            dve.tensor_copy(bt_rows[:, :], ps_e[:, 0:D])
            dve.tensor_copy(b2_rows[:, :], ps_e[:, D:2 * D])
            dve.tensor_copy(eps_col[:, :], ps_e[:, 3 * D:3 * D + 1]).then_inc(p_rows, 1)
            dve.wait_ge(p_rows, 1)
            dve.wait_ge(p_pool, 4)
            dve.tensor_scalar(eps_ident[:, :], ident[:, :], eps_col[:, 0:1], None, ALU.mult).then_inc(p_weights, 1)
            dve.wait_ge(p_pe, 2)
            dve.tensor_copy(bfin_rows[:, :], ps_l[:, 0:D]).then_inc(p_weights, 1)
            dve.wait_ge(p_pe, 3)
            for i in range(2):
                last = dve.tensor_copy(fct[:, 512 * i:512 * i + 512], ps_t[i][:, :])
            last.then_inc(p_fct, 1)
            dve.wait_ge(p_pe, 4)
            for i in range(2):
                last = dve.tensor_copy(w_head[:, 512 * i:512 * i + 512], ps_s[i][:, :])
            last.then_inc(p_weights, 1)
            for part in range(3):
                for kind in range(2):
                    last = dve.tensor_copy(w_qk[:, part, 8 * kind:8 * kind + 8], ps_o[0][:, kind:16:2])
            last.then_inc(p_weights, 1)
            dve.tensor_copy(b_qk[:, :], ps_o[1][0:QROWS, 0:1]).then_inc(p_weights, 1)

            carried = [0]

            def carrier():
                carried[0] += 1
                return fence[:, carried[0] % 16:carried[0] % 16 + 1]

            def stats(t, k, src, st, mv, s_bn, s_mv):
                for r in range(R):
                    last = dve.bn_stats(st[:, r, :], src[:, r, :])
                last.then_inc(s_bn.semaphore, 1)
                dve.wait_ge(s_bn.semaphore, s_bn.at(t, k))
                dve.memset(carrier(), 0.0)
                for r in range(R):
                    last = dve.bn_aggr(mv[:, r, :], st[:, r, :])
                last.then_inc(s_mv.semaphore, 1)

            def apply(t, k, dst, src, mv, rs, s_rs, sig):
                dve.wait_ge(s_rs.semaphore, s_rs.at(t, k))
                for r in range(R):
                    last = dve.tensor_scalar(dst[:, r, :], src[:, r, :], mv[:, r, 0:1], rs[:, r:r + 1],
                                             ALU.subtract, ALU.mult)
                last.then_inc(sig.semaphore, 1)

            def stats_e(t, k, src):
                stats(t, k, src, st_e, mv_e, e_bn, e_mv)

            def stats_l(t, k, src):
                stats(t, k, src, st_l, mv_l, l_bn, l_mv)

            def degrees(t):
                dve.wait_ge(e_deg_ps.semaphore, e_deg_ps.at(t))
                dve.tensor_scalar(deg[:, 0:4], ps_e[:, 0:4], 1e-6, None, ALU.add)
                dve.tensor_copy(deg[:, 4:12], ps_e[:, 0:8]).then_inc(e_deg.semaphore, 1)
                dve.wait_ge(e_deg.semaphore, e_deg.at(t))
                dve.tensor_scalar(degc[:, :], deg[:, :], 1e-19, None, ALU.max).then_inc(e_degc.semaphore, 1)

            def degree_masks(t):
                dve.wait_ge(e_scl.semaphore, e_scl.at(t))
                dve.scalar_tensor_tensor(out=s_in_out[:, :], in0=deg[:, 4:12], scalar=0.0,
                                              in1=scl[:, 4:12], op0=ALU.not_equal, op1=ALU.mult)\
                    .then_inc(e_masked.semaphore, 1)
                dve.wait_ge(e_masked.semaphore, e_masked.at(t))
                dve.tensor_scalar(neg_s_out[:, :], s_in_out[:, 4:8], -1.0, None, ALU.mult).then_inc(e_norms.semaphore, 1)

            def proj_evac(t, r):
                dve.wait_ge(e_proj_ps.semaphore, e_proj_ps.at(t, r + 1))
                dve.tensor_scalar(y_e[:, r, :], ps_e[:, 0:D], scl[:, r:r + 1], None, ALU.mult)
                dve.tensor_copy(het[:, r, :], ps_e[:, D:2 * D])
                dve.tensor_tensor(gate[:, r, :], ps_e[:, 2 * D:3 * D], bt_rows[:, :], ALU.add)\
                    .then_inc(e_proj.semaphore, 1)

            def hop0_evac(t):
                dve.wait_ge(e_hop0.semaphore, e_hop0.at(t))
                for r in range(R):
                    last = dve.scalar_tensor_tensor(out=mix[:, r, :], in0=ps_e[:, r * D:(r + 1) * D],
                                                    scalar=scl[:, r:r + 1], in1=het[:, r, :],
                                                    op0=ALU.mult, op1=ALU.subtract)
                last.then_inc(e_dif.semaphore, 1)

            def mix_up(t):
                dve.wait_ge(e_dif.semaphore, e_dif.at(t))
                dve.wait_ge(e_gate.semaphore, e_gate.at(t))
                dve.tensor_tensor(mix[:, :, :], mix[:, :, :], gate[:, :, :], ALU.mult).then_inc(e_gated.semaphore, 1)
                dve.wait_ge(e_gated.semaphore, e_gated.at(t))
                dve.tensor_tensor(mix[:, :, :], mix[:, :, :], het[:, :, :], ALU.add).then_inc(e_mix.semaphore, 1)
                dve.wait_ge(e_mix.semaphore, e_mix.at(t))
                dve.tensor_scalar(elu[:, :, :], mix[:, :, :], 0.0, None, ALU.min).then_inc(e_min.semaphore, 1)

            def elu_out(t):
                dve.wait_ge(e_expm.semaphore, e_expm.at(t))
                dve.scalar_tensor_tensor(out=mix[:, :, :], in0=elu[:, :, :], scalar=-1.0,
                                         in1=mix[:, :, :], op0=ALU.add, op1=ALU.max)\
                    .then_inc(e_elu.semaphore, 1)

            def stats0(t):
                dve.wait_ge(x_loaded.semaphore, x_loaded.at(t))
                if due(e_xn.at(t - 1)):
                    dve.wait_ge(e_xn.semaphore, e_xn.at(t - 1))
                stats_e(t, 1, x_in)

            def stats1(t, p):
                dve.wait_ge(e_x0.semaphore, e_x0.at(t))
                stats_e(t, 2, X[p])

            def h1_relu(t, p):
                apply(t, 2, h1_e, X[p], mv_e, rs_e, e_rs, e_xn)
                dve.wait_ge(e_xn.semaphore, e_xn.at(t, 2))
                dve.tensor_scalar(h1_e[:, :, :], h1_e[:, :, :], 0.0, None, ALU.max).then_inc(e_h1.semaphore, 1)
                dve.wait_ge(e_h1.semaphore, e_h1.at(t))
                stats_e(t, 3, h1_e)

            def normed0(t):
                apply(t, 1, xn_e, x_in, mv_e, rs_e, e_rs, e_xn)

            def normed1(t):
                apply(t, 3, xn_e, h1_e, mv_e, rs_e, e_rs, e_xn)

            def ht1_evac(t):
                dve.wait_ge(e_tr1.semaphore, e_tr1.at(t))
                dve.tensor_scalar(ht_e[:, :], ps_e[:, :], gamma_sb[:, 0:1], beta_sb[:, 0:1],
                                       ALU.mult, ALU.add)\
                    .then_inc(e_ht1.semaphore, 1)

            def u_evac(t, i):
                dve.wait_ge(e_u_ps.semaphore, e_u_ps.at(t, i + 1))
                if i == 0:
                    dve.wait_ge(e_norms.semaphore, e_norms.at(t))
                for n in range(2):
                    r = 2 * i + n
                    dve.tensor_scalar(y_e[:, r, :], ps_e[:, n * 2 * D + D:(n + 1) * 2 * D],
                                      s_in_out[:, r:r + 1], None, ALU.mult)
                dve.tensor_copy(u1[:, 2 * i:2 * i + 2, :],
                                     ps_e[:, :].rearrange("p (n c) -> p n c", n=2)[:, :, 0:D])\
                    .then_inc(e_u.semaphore, 1)

            def hop1_evac(t):
                dve.wait_ge(e_hop1.semaphore, e_hop1.at(t))
                for r in range(R):
                    last = dve.scalar_tensor_tensor(out=pre[:, r, :], in0=ps_e[:, r * D:(r + 1) * D],
                                                    scalar=neg_s_out[:, r:r + 1], in1=u1[:, r, :],
                                                    op0=ALU.mult, op1=ALU.add)
                last.then_inc(e_pre.semaphore, 1)

            def softplus_part(t, p):
                dve.wait_ge(e_sp.semaphore, e_sp.at(t, 1))
                dve.scalar_tensor_tensor(out=pre[:, :, :], in0=pre[:, :, :], scalar=0.0,
                                         in1=X[p][:, :, :], op0=ALU.max, op1=ALU.add)\
                    .then_inc(e_part.semaphore, 1)

            def stats2(t, q):
                dve.wait_ge(e_x1.semaphore, e_x1.at(t))
                stats_l(t, 1, X[q])

            def h2_relu(t, q):
                if due(l_zh.at(t - 1)):
                    dve.wait_ge(l_zh.semaphore, l_zh.at(t - 1))
                apply(t, 1, xn_l, X[q], mv_l, rs_l, l_rs, l_xn)
                dve.wait_ge(l_xn.semaphore, l_xn.at(t, 1))
                dve.tensor_scalar(h2[:, :, :], xn_l[:, :, :], 0.0, None, ALU.max).then_inc(l_h2.semaphore, 1)

            def rms_scale(t, b):
                if b == 0:
                    dve.wait_ge(l_rms.semaphore, l_rms.at(t))
                dve.scalar_tensor_tensor(out=hid[:, b, :], in0=hid[:, b, :], scalar=rmsw_sb[:, b:b + 1],
                                              in1=rms_b[:, :], op0=ALU.mult, op1=ALU.mult)\
                    .then_inc(l_g.semaphore, 1)

            def residual2(t, q):
                dve.wait_ge(l_w2_ps.semaphore, l_w2_ps.at(t))
                dve.wait_ge(l_xb.semaphore, l_xb.at(t))
                if due(f_res.at(t - 2)):
                    dve.wait_ge(f_res.semaphore, f_res.at(t - 2))
                dve.tensor_tensor(XH[q][:, :, :].rearrange("p r d -> p (r d)"), ps_l[:, :],
                                       x_b2[:, :, :].rearrange("p r d -> p (r d)"), ALU.add)\
                    .then_inc(l_x2.semaphore, 1)
                dve.wait_ge(l_x2.semaphore, l_x2.at(t))
                stats_l(t, 2, XH[q])

            def h3(t, q):
                apply(t, 2, xn_l, XH[q], mv_l, rs_l, l_rs, l_xn)

            def h3_bias(t, q):
                dve.wait_ge(l_xn.semaphore, l_xn.at(t, 2))
                if due(f_z.at(t - 2)):
                    dve.wait_ge(f_z.semaphore, f_z.at(t - 2))
                for r in range(R):
                    last = dve.scalar_tensor_tensor(out=ZH[q][:, r, :], in0=xn_l[:, r, :], scalar=0.0,
                                                    in1=bfin_rows[:, :], op0=ALU.max, op1=ALU.add)
                last.then_inc(l_zh.semaphore, 1)

            def qk_split(t):
                dve.wait_ge(l_qk_ps.semaphore, l_qk_ps.at(t))
                dve.tensor_scalar(qk_f[:, :], ps_l[0:QROWS, :], b_qk[:, 0:1], None, ALU.add)\
                    .then_inc(l_split.semaphore, 1)
                dve.wait_ge(l_split.semaphore, l_split.at(t, 1))
                dve.tensor_copy(qk_s[:, :], qk_f[:, :]).then_inc(l_split.semaphore, 1)
                dve.wait_ge(l_split.semaphore, l_split.at(t, 2))
                dve.tensor_tensor(qk_r[:, :], qk_f[:, :], qk_s[:, :], ALU.subtract).then_inc(l_split.semaphore, 1)
                dve.wait_ge(l_split.semaphore, l_split.at(t, 3))
                dve.tensor_copy(qk_s[32:64, :], qk_r[32:64, :])
                dve.tensor_copy(qk_s[64:96, :], qk_r[64:96, :]).then_inc(l_split.semaphore, 1)
                dve.wait_ge(l_split.semaphore, l_split.at(t, 4))
                dve.tensor_tensor(qk_s[64:96, :], qk_r[64:96, :], qk_s[64:96, :], ALU.subtract)\
                    .then_inc(l_split.semaphore, 1)

            def qk_rows(t, q):
                dve.wait_ge(l_split.semaphore, l_split.at(t))
                if due(h_qk.at(t - 2)):
                    dve.wait_ge(h_qk.semaphore, h_qk.at(t - 2))
                dve.tensor_scalar(q_rows[q][:, :], qk_s[:, :], select[:, 0:1], select[:, 1:2], ALU.mult, ALU.add)
                for h in range(HEADS):
                    last = dve.tensor_scalar(k_rows[q][:, h, :], qk_s[:, :], select[:, 2 + h:3 + h],
                                             select[:, 2 + HEADS + h:3 + HEADS + h], ALU.mult, ALU.add)
                last.then_inc(l_rows.semaphore, 1)

            def head_max(pair, u, j, q):
                if j == 0:
                    if due(h_tr.at(pair, 2 * (u - SB) + 2)):
                        dve.wait_ge(h_tr.semaphore, h_tr.at(pair, 2 * (u - SB) + 2))
                    dve.wait_ge(h_qk.semaphore, h_qk.at(pair, 2 * u + 2))
                    dve.memset(carrier(), 0.0)
                g = u // GPG
                for i in range(HALVES):
                    last = dve.tensor_tensor_reduce(S[u % SB][:, j, i, :], ps_s[j][:, i * N:(i + 1) * N],
                                                    M[q][:, HALVES * g + i, :], 1.0, -3e38, ALU.add, ALU.max,
                                                    mx[u % SB][:, 2 * j + i:2 * j + i + 1])
                last.then_inc(h_max.semaphore, 1)

            def head_leaky(pair, u):
                b = u % SB
                dve.wait_ge(h_max.semaphore, h_max.at(pair, 2 * u + 2))
                dve.tensor_scalar(ng[b][:, :], mx[b][:, :], -1.0, None, ALU.mult).then_inc(h_neg.semaphore, 1)
                flat = S[b][:, :, :, :].rearrange("p j i n -> p (j i n)")
                dve.scalar_tensor_tensor(out=flat, in0=flat, scalar=SLOPE, in1=flat, op0=ALU.mult, op1=ALU.max)
                dve.wait_ge(h_neg.semaphore, h_neg.at(pair, u + 1))
                dve.scalar_tensor_tensor(out=nm[b][:, :], in0=mx[b][:, :], scalar=-SLOPE, in1=ng[b][:, :],
                                              op0=ALU.mult, op1=ALU.min)\
                    .then_inc(h_leaky.semaphore, 1)

            def head_recip(pair, u):
                dve.wait_ge(h_exp.semaphore, h_exp.at(pair, u + 1))
                dve.reciprocal(rc[u % SB][:, :], sm[u % SB][:, :]).then_inc(h_rc.semaphore, 1)

            def final_in(pair, g, q):
                dve.wait_ge(l_zh.semaphore, l_zh.at(pair))
                dve.wait_ge(h_av.semaphore, h_av.at(pair, 8 * (g + 1)))
                flat = zf[g][:, :, :].rearrange("p r d -> p (r d)")
                dve.tensor_tensor(flat, ps_o[g][:, 0:HALVES * D],
                                       ZH[q][:, HALVES * g:HALVES * g + HALVES, :].rearrange("p r d -> p (r d)"),
                                       ALU.add)\
                    .then_inc(f_z.semaphore, 1)

            def final_out(pair, g, q):
                dve.wait_ge(f_s.semaphore, f_s.at(pair, 3 * g + 3))
                if due(stored[g].at(pair - 1)):
                    dve.wait_ge(stored[g].semaphore, stored[g].at(pair - 1))
                dve.tensor_tensor(res[g][:, :, :], XH[q][:, HALVES * g:HALVES * g + HALVES, :], zf[g][:, :, :],
                                       ALU.add)\
                    .then_inc(f_res.semaphore, 1)

            def body(t, p, known):
                early, late, heads, tail = (mine(known, back) for back in range(4))
                if early:
                    stats0(t)
                if late:
                    softplus_part(t - 1, 1 - p)
                if tail:
                    head_recip(t - 3, 5)
                    head_leaky(t - 3, 7)
                if heads:
                    qk_rows(t - 2, p)
                if late:
                    stats2(t - 1, 1 - p)
                if tail:
                    head_recip(t - 3, 6)
                if heads:
                    h3_bias(t - 2, p)
                if early:
                    degrees(t)
                if heads:
                    head_max(t - 2, 0, 0, p)
                    head_max(t - 2, 0, 1, p)
                if early:
                    normed0(t)
                if late:
                    h2_relu(t - 1, 1 - p)
                if heads:
                    head_leaky(t - 2, 0)
                if tail:
                    final_in(t - 3, 0, 1 - p)
                if heads:
                    head_max(t - 2, 1, 0, p)
                    head_max(t - 2, 1, 1, p)
                if tail:
                    head_recip(t - 3, 7)
                if early:
                    degree_masks(t)
                    proj_evac(t, 0)
                if heads:
                    head_leaky(t - 2, 1)
                if early:
                    proj_evac(t, 1)
                    proj_evac(t, 2)
                    proj_evac(t, 3)
                if heads:
                    head_max(t - 2, 2, 0, p)
                    head_max(t - 2, 2, 1, p)
                    head_recip(t - 2, 0)
                    head_leaky(t - 2, 2)
                if early:
                    hop0_evac(t)
                    mix_up(t)
                if heads:
                    head_max(t - 2, 3, 0, p)
                if early:
                    elu_out(t)
                if heads:
                    head_max(t - 2, 3, 1, p)
                if late:
                    rms_scale(t - 1, 0)
                    rms_scale(t - 1, 1)
                if early:
                    stats1(t, p)
                if late:
                    rms_scale(t - 1, 2)
                    rms_scale(t - 1, 3)
                if heads:
                    head_recip(t - 2, 1)
                if early:
                    h1_relu(t, p)
                if heads:
                    head_leaky(t - 2, 3)
                if early:
                    normed1(t)
                if tail:
                    final_out(t - 3, 0, 1 - p)
                    final_in(t - 3, 1, 1 - p)
                if heads:
                    head_recip(t - 2, 2)
                if early:
                    ht1_evac(t)
                if heads:
                    head_max(t - 2, 4, 0, p)
                    head_max(t - 2, 4, 1, p)
                if early:
                    u_evac(t, 0)
                if heads:
                    head_leaky(t - 2, 4)
                    head_max(t - 2, 5, 0, p)
                    head_max(t - 2, 5, 1, p)
                    head_recip(t - 2, 3)
                    head_leaky(t - 2, 5)
                if early:
                    u_evac(t, 1)
                if heads:
                    head_max(t - 2, 6, 0, p)
                    head_recip(t - 2, 4)
                    head_max(t - 2, 6, 1, p)
                    head_leaky(t - 2, 6)
                if tail:
                    final_out(t - 3, 1, 1 - p)
                if late:
                    residual2(t - 1, 1 - p)
                    h3(t - 1, 1 - p)
                if early:
                    hop1_evac(t)
                if heads:
                    head_max(t - 2, 7, 0, p)
                    head_max(t - 2, 7, 1, p)
                if late:
                    qk_split(t - 1)

            iterations(dve, body)

        @block.tensor
        def _(pe):
            def mm(dst, left, right, start=True, stop=True):
                return pe.matmul(dst, left, right, start=start, stop=stop)

            pe.wait_ge(p_pool, 4)
            pe.wait_ge(p_load, 16 * 23)
            mm(ps_e[:, 0:3 * D + 1], ones[0:1, :], bias_row[:, :]).then_inc(p_pe, 1)
            pe.wait_ge(p_products, 1)
            mm(ps_l[:, 0:D], ones[0:1, :], bias_row[:, 2 * D:3 * D], stop=False)
            for h in range(HEADS):
                last = mm(ps_l[:, 0:D], fcb_cols[:, h, :], fp_sb[:, h, :], start=False, stop=(h == HEADS - 1))
            last.then_inc(p_pe, 1)
            for h in range(HEADS):
                last = pe.transpose(ps_t[h // 4][:, (h % 4) * P:(h % 4 + 1) * P], fc_sb[:, h * P:(h + 1) * P],
                                    ident[:, :])
            last.then_inc(p_pe, 1)
            pe.wait_ge(p_fct, 1)
            for h in range(HEADS):
                mm(ps_s[h // 4][:, (h % 4) * P:(h % 4 + 1) * P], fct[:, h * P:(h + 1) * P], fp_sb[:, h, :])
                mm(ps_o[0][:, 2 * h:2 * h + 2], fct[:, h * P:(h + 1) * P], qkw_sb[:, :])
            mm(ps_o[1][0:QROWS, 0:1], bq_prod[:, :, :].rearrange("p a n -> p (a n)"), ones[:, 0:1], stop=False)
            mm(ps_o[1][0:QROWS, 0:1], qkb_row[:, :, :].rearrange("p a n -> p (a n)"), ones[0:1, 0:1],
               start=False).then_inc(p_pe, 1)
            pe.wait_ge(p_weights, 5)

            def transposes(dst, src):
                for r in range(R):
                    last = pe.transpose(dst[:, r * P:(r + 1) * P], src[:, r, :], ident[:, :])
                return last

            def adj_transpose(t, p, g):
                if g == 0:
                    pe.wait_ge(adj_in[p], (t - p) * 8 + 16)
                    if due(e_pre.at(t - 1)):
                        pe.wait_ge(e_pre.semaphore, e_pre.at(t - 1))
                else:
                    pe.wait_ge(e_at.semaphore, e_at.at(t, 1))
                for m in range(HALVES):
                    for i in range(HALVES):
                        last = pe.transpose(ps_e[:, m * N + i * P:m * N + (i + 1) * P],
                                            A[p][:, HALVES * g + i, m * P:(m + 1) * P], ident[:, :])
                last.then_inc(e_adj_tr.semaphore, 1)

            def degree_sums(t, p):
                pe.wait_ge(e_at.semaphore, e_at.at(t, 2))
                for r in range(R):
                    g, i = divmod(r, HALVES)
                    for m in range(HALVES):
                        mm(ps_e[:, r:r + 1], AT[p][:, g, m, i * P:(i + 1) * P], ones[:, 0:1],
                           start=(m == 0), stop=(m == HALVES - 1))
                    for m in range(HALVES):
                        last = mm(ps_e[:, R + r:R + r + 1], A[p][:, HALVES * g + m, i * P:(i + 1) * P], ones[:, 0:1],
                                  start=(m == 0), stop=(m == HALVES - 1))
                last.then_inc(e_deg_ps.semaphore, 1)

            def transpose0(t):
                pe.wait_ge(e_xn.semaphore, e_xn.at(t, 1))
                pe.wait_ge(e_deg.semaphore, e_deg.at(t))
                transposes(ps_e, xn_e).then_inc(e_tr0.semaphore, 1)

            def project(t, r):
                if r == 0:
                    pe.wait_ge(e_ht0.semaphore, e_ht0.at(t))
                else:
                    pe.wait_ge(e_proj.semaphore, e_proj.at(t, r))
                mm(ps_e[:, 0:3 * D], ht_e[:, r * P:(r + 1) * P], w_proj[:, :]).then_inc(e_proj_ps.semaphore, 1)

            def hop(t, p, sig):
                for r in range(R):
                    g, i = divmod(r, HALVES)
                    for m in range(HALVES):
                        last = mm(ps_e[:, r * D:(r + 1) * D], AT[p][:, g, m, i * P:(i + 1) * P],
                                  y_e[:, HALVES * g + m, :], start=(m == 0), stop=(m == HALVES - 1))
                last.then_inc(sig.semaphore, 1)

            def hop0(t, p):
                pe.wait_ge(e_proj.semaphore, e_proj.at(t, 4))
                hop(t, p, e_hop0)

            def transpose1(t):
                pe.wait_ge(e_xn.semaphore, e_xn.at(t, 3))
                transposes(ps_e, xn_e).then_inc(e_tr1.semaphore, 1)

            def mix1(t, i):
                if i == 0:
                    pe.wait_ge(e_ht1.semaphore, e_ht1.at(t))
                else:
                    pe.wait_ge(e_u.semaphore, e_u.at(t, 1))
                for n in range(2):
                    r = 2 * i + n
                    last = mm(ps_e[:, n * 2 * D:(n + 1) * 2 * D], ht_e[:, r * P:(r + 1) * P], w_l1[:, :])
                last.then_inc(e_u_ps.semaphore, 1)

            def hop1(t, p):
                pe.wait_ge(e_u.semaphore, e_u.at(t, 2))
                hop(t, p, e_hop1)

            def neighbour_sum(t, q):
                pe.wait_ge(l_h2.semaphore, l_h2.at(t))
                if due(l_features.at(t - 1)):
                    pe.wait_ge(l_features.semaphore, l_features.at(t - 1))
                for g in range(2):
                    for m in range(HALVES):
                        pe.matmul(ps_l[:, g * N:(g + 1) * N], h2[:, HALVES * g + m, :], AT[q][:, g, m, :],
                                  start=(m == 0), stop=False, skip_group_check=True)
                    for i in range(HALVES):
                        last = pe.matmul(ps_l[:, g * N + i * P:g * N + (i + 1) * P], h2[:, HALVES * g + i, :],
                                         eps_ident[:, :], start=False, stop=(i == HALVES - 1),
                                         skip_group_check=True)
                last.then_inc(l_z_ps.semaphore, 1)

            def hidden(t, b):
                if b == 0:
                    pe.wait_ge(l_zt.semaphore, l_zt.at(t))
                else:
                    pe.wait_ge(l_hid.semaphore, l_hid.at(t, b))
                mm(ps_l[:, :], w1_sb[:, b * P:(b + 1) * P], zt[:, :]).then_inc(l_hid_ps.semaphore, 1)

            def squares_sum(t):
                pe.wait_ge(l_sum.semaphore, l_sum.at(t))
                pe.wait_ge(l_hid.semaphore, l_hid.at(t))
                mm(ps_l[:, :], ones[:, :], sq[:, 0, :]).then_inc(l_ss_ps.semaphore, 1)

            def down(t):
                pe.wait_ge(l_act.semaphore, l_act.at(t))
                for r in range(R):
                    for b in range(HB):
                        last = mm(ps_l[:, r * D:(r + 1) * D], hid[:, b, r * P:(r + 1) * P], w2_sb[:, b, :],
                                  start=(b == 0), stop=(b == HB - 1))
                last.then_inc(l_w2_ps.semaphore, 1)

            def transpose3(t):
                pe.wait_ge(l_xn.semaphore, l_xn.at(t, 2))
                transposes(ps_l, xn_l).then_inc(l_tr.semaphore, 1)

            def queries_keys(t):
                pe.wait_ge(l_ht.semaphore, l_ht.at(t))
                mm(ps_l[0:QROWS, :], w_qk[:, :, :].rearrange("p a n -> p (a n)"), ht_l[:, :])\
                    .then_inc(l_qk_ps.semaphore, 1)

            def head_features(t, k):
                if k == 0:
                    pe.wait_ge(l_split.semaphore, l_split.at(t, 1))
                else:
                    pe.wait_ge(l_features.semaphore, l_features.at(t, k))
                mm(ps_l[:, :], ht_l[:, (k // 2) * P:(k // 2 + 1) * P], w_head[:, 512 * (k % 2):512 * (k % 2) + 512])\
                    .then_inc(l_g_ps.semaphore, 1)

            def scores(pair, u, j, q):
                if u == 0 and j == 0:
                    pe.wait_ge(l_rows.semaphore, l_rows.at(pair))
                if due(h_max.at(pair, 2 * u + j - 1)):
                    pe.wait_ge(h_max.semaphore, h_max.at(pair, 2 * u + j - 1))
                g, h = u // GPG, 2 * (u % GPG) + j
                for i in range(HALVES):
                    last = mm(ps_s[j][:, i * N:(i + 1) * N], q_rows[q][:, g * N + i * P:g * N + (i + 1) * P],
                              k_rows[q][:, h, g * N:(g + 1) * N])
                last.then_inc(h_qk.semaphore, 1)

            def head_transpose(pair, u, j):
                pe.wait_ge(h_norm.semaphore, h_norm.at(pair, u + 1))
                if due(h_et.at(pair, 2 * u + j - 1)):
                    pe.wait_ge(h_et.semaphore, h_et.at(pair, 2 * u + j - 1))
                for m in range(HALVES):
                    for i in range(HALVES):
                        last = pe.transpose(ps_t[j][:, m * N + i * P:m * N + (i + 1) * P],
                                            S[u % SB][:, j, i, m * P:(m + 1) * P], ident[:, :])
                last.then_inc(h_tr.semaphore, 1)

            def attend(pair, u, j, q):
                g, h = u // GPG, 2 * (u % GPG) + j
                pe.wait_ge(h_et.semaphore, h_et.at(pair, 2 * u + j + 1))
                if u == 0 and j == 0:
                    pe.wait_ge(l_features.semaphore, l_features.at(pair))
                if h == 0:
                    if due(f_z.at(pair - 1, g + 1)):
                        pe.wait_ge(f_z.semaphore, f_z.at(pair - 1, g + 1))
                for i in range(HALVES):
                    for m in range(HALVES):
                        last = pe.matmul(ps_o[g][:, i * D:(i + 1) * D], ET[j][:, m, i * P:(i + 1) * P],
                                         G[q][:, HALVES * g + m, h, :],
                                         start=(h == 0 and i == 0 and m == 0),
                                         stop=(h == HEADS - 1 and m == HALVES - 1), skip_group_check=True)
                last.then_inc(h_av.semaphore, 1)

            def body(t, p, known):
                early, late, heads, tail = (mine(known, back) for back in range(4))
                if tail:
                    head_transpose(t - 3, 3, 0)
                if late:
                    hop1(t - 1, 1 - p)
                if tail:
                    scores(t - 3, 7, 0, 1 - p)
                    head_transpose(t - 3, 3, 1)
                    scores(t - 3, 7, 1, 1 - p)
                if heads:
                    transpose3(t - 2)
                if tail:
                    attend(t - 3, 2, 1, 1 - p)
                if heads:
                    queries_keys(t - 2)
                if tail:
                    attend(t - 3, 3, 0, 1 - p)
                if heads:
                    head_features(t - 2, 0)
                if early:
                    adj_transpose(t, p, 0)
                if tail:
                    head_transpose(t - 3, 4, 0)
                if heads:
                    head_features(t - 2, 1)
                if tail:
                    attend(t - 3, 3, 1, 1 - p)
                if heads:
                    head_features(t - 2, 2)
                if tail:
                    attend(t - 3, 4, 0, 1 - p)
                if heads:
                    head_features(t - 2, 3)
                if tail:
                    head_transpose(t - 3, 4, 1)
                if heads:
                    head_features(t - 2, 4)
                if tail:
                    head_transpose(t - 3, 5, 0)
                if early:
                    adj_transpose(t, p, 1)
                if heads:
                    head_features(t - 2, 5)
                if early:
                    degree_sums(t, p)
                if heads:
                    scores(t - 2, 0, 0, p)
                    scores(t - 2, 0, 1, p)
                    head_features(t - 2, 6)
                if tail:
                    attend(t - 3, 4, 1, 1 - p)
                if heads:
                    head_features(t - 2, 7)
                    scores(t - 2, 1, 0, p)
                if tail:
                    head_transpose(t - 3, 5, 1)
                if heads:
                    scores(t - 2, 1, 1, p)
                if tail:
                    attend(t - 3, 5, 0, 1 - p)
                    head_transpose(t - 3, 6, 0)
                if early:
                    transpose0(t)
                if late:
                    neighbour_sum(t - 1, 1 - p)
                if early:
                    project(t, 0)
                if late:
                    hidden(t - 1, 0)
                if heads:
                    scores(t - 2, 2, 0, p)
                if early:
                    project(t, 1)
                if late:
                    hidden(t - 1, 1)
                if early:
                    project(t, 2)
                if late:
                    hidden(t - 1, 2)
                if early:
                    project(t, 3)
                if heads:
                    scores(t - 2, 2, 1, p)
                if tail:
                    head_transpose(t - 3, 6, 1)
                if late:
                    hidden(t - 1, 3)
                if early:
                    hop0(t, p)
                if tail:
                    attend(t - 3, 5, 1, 1 - p)
                    attend(t - 3, 6, 0, 1 - p)
                    head_transpose(t - 3, 7, 0)
                    head_transpose(t - 3, 7, 1)
                if heads:
                    scores(t - 2, 3, 0, p)
                    scores(t - 2, 3, 1, p)
                if late:
                    squares_sum(t - 1)
                if tail:
                    attend(t - 3, 6, 1, 1 - p)
                    attend(t - 3, 7, 0, 1 - p)
                if heads:
                    head_transpose(t - 2, 0, 0)
                    head_transpose(t - 2, 0, 1)
                    scores(t - 2, 4, 0, p)
                    scores(t - 2, 4, 1, p)
                if tail:
                    attend(t - 3, 7, 1, 1 - p)
                if heads:
                    attend(t - 2, 0, 0, p)
                if early:
                    transpose1(t)
                    mix1(t, 0)
                if heads:
                    head_transpose(t - 2, 1, 0)
                    head_transpose(t - 2, 1, 1)
                    scores(t - 2, 5, 0, p)
                    scores(t - 2, 5, 1, p)
                    attend(t - 2, 0, 1, p)
                    attend(t - 2, 1, 0, p)
                if early:
                    mix1(t, 1)
                if heads:
                    head_transpose(t - 2, 2, 0)
                    scores(t - 2, 6, 0, p)
                    head_transpose(t - 2, 2, 1)
                    attend(t - 2, 1, 1, p)
                    scores(t - 2, 6, 1, p)
                if late:
                    down(t - 1)
                if heads:
                    attend(t - 2, 2, 0, p)

            iterations(pe, body)


_INS = ['x', 'adj', 'L0_gnn_theta', 'L0_gnn_W_h', 'L0_gnn_W_t', 'L0_gnn_b_t', 'L1_gnn_gamma', 'L1_gnn_beta',
        'L1_gnn_W_self', 'L1_gnn_W_neigh', 'L2_gnn_epsilon', 'L2_gnn_W1', 'L2_gnn_b1', 'L2_gnn_rms_weight',
        'L2_gnn_W2', 'L2_gnn_b2', 'L3_gnn_fc_w', 'L3_gnn_fc_b', 'L3_gnn_q_w', 'L3_gnn_q_b', 'L3_gnn_k_w',
        'L3_gnn_k_b', 'L3_gnn_fp_w', 'L3_gnn_fp_b']


def row_select(heads):
    import numpy as _np
    select = _np.zeros((96, 2 + 2 * heads), _np.float32)
    for part in range(3):
        for h in range(heads):
            q, k = 32 * part + h, 32 * part + heads + h
            select[q, 0] = 1.0
            select[k, 1] = 1.0
            select[k, 2 + h] = 1.0
            select[q, 2 + heads + h] = 1.0
    return select


def kernel(**inputs):
    import numpy as _np
    import concourse.bacc as _bacc
    from concourse import mybir as _mybir
    from concourse.bass_utils import run_bass_kernel_spmd as _run

    nc = _bacc.Bacc("TRN2", target_bir_lowering=False, num_devices=1)
    arrays, args = {}, []
    for name in _INS:
        a = _np.ascontiguousarray(inputs[name])
        if a.ndim == 0:
            a = a.reshape(1, 1)
        if name == 'L2_gnn_epsilon':
            a = a.reshape(1, 1)
        arrays[f"in_{name}_dram"] = a
        args.append(nc.dram_tensor(f"in_{name}_dram", a.shape, _mybir.dt.from_np(a.dtype), kind="ExternalInput").ap())
    select = row_select(8)
    arrays["row_select_dram"] = select
    args.append(nc.dram_tensor("row_select_dram", select.shape, _mybir.dt.float32, kind="ExternalInput").ap())
    shape = tuple(inputs['x'].shape)
    args.append(nc.dram_tensor("out_0_dram", shape, _mybir.dt.float32, kind="ExternalOutput").ap())
    four_layer_gnn_kernel(nc, *args)
    r = _run(nc, [arrays], core_ids=[0])
    return r.results[0]["out_0_dram"]
```

```python
import concourse.bass as bass
from concourse import mybir
from contextlib import ExitStack


class Signal:

    def __init__(self, semaphore, per_pair):
        self.semaphore = semaphore
        self.per_pair = per_pair

    def at(self, pair, k=None):
        return pair * self.per_pair + (self.per_pair if k is None else k)


def due(count):
    return not isinstance(count, int) or count > 0


def four_layer_gnn_kernel(nc, x, adj, theta, w_h, w_t, b_t, gamma, beta, w_self, w_neigh, epsilon,
                          w1, b1, rms_w, w2, b2, fc_w, fc_b, q_w, q_b, k_w, k_b, fp_w, fp_b,
                          row_select, out):
    fp32 = mybir.dt.float32
    bf16 = mybir.dt.bfloat16
    ALU = mybir.AluOpType
    ACT = mybir.ActivationFunctionType

    B, N, D = x.shape
    P = 128
    HALVES = N // P
    R = 2 * HALVES
    PAIRS = B // 2
    HID = w1.shape[1]
    HB = HID // P
    HEADS = fc_w.shape[1] // D
    GROUPS = 2 * HEADS // 2
    GPG = GROUPS // 2
    QROWS = 96
    SLOPE = 0.01
    NEG = -1e9
    FLOOR = -40.0
    SB = 4
    LOADED = 16

    adj_v = adj.rearrange("b n m -> (b n) m").rearrange("(t r p) m -> t p r m", r=R, p=P)
    x_v = x.rearrange("b n d -> (b n) d").rearrange("(t r p) d -> t p r d", r=R, p=P)
    out_v = out.rearrange("b n d -> (b n) d").rearrange("(b r p) d -> b p r d", r=HALVES, p=P)

    ctx = ExitStack()
    with ctx:
        def sb(name, shape, dt=fp32):
            return ctx.enter_context(nc.sbuf_tensor(name, shape, dt))

        def sem(name):
            return ctx.enter_context(nc.semaphore(name))

        def signal(name, per_pair=1):
            return Signal(sem(name), per_pair)

        ident = sb("ident", [P, P])
        ones = sb("ones", [P, P])
        eps_ident = sb("eps_ident", [P, P])
        w_proj = sb("w_proj", [P, 3 * D])
        w_l1 = sb("w_l1", [P, 2 * D])
        w1_sb = sb("w1_sb", [P, HID])
        w2_sb = sb("w2_sb", [P, HB, D])
        b1_sb = sb("b1_sb", [P, HB])
        rmsw_sb = sb("rmsw_sb", [P, HB])
        gamma_sb = sb("gamma_sb", [P, 1])
        beta_sb = sb("beta_sb", [P, 1])
        w_head = sb("w_head", [P, HEADS * D])
        w_qk = sb("w_qk", [P, 3, 32])
        b_qk = sb("b_qk", [QROWS, 1])
        select = sb("select", [QROWS, 2 + 2 * HEADS])
        bt_rows = sb("bt_rows", [P, D])
        b2_rows = sb("b2_rows", [P, D])
        bfin_rows = sb("bfin_rows", [P, D])
        eps_col = sb("eps_col", [P, 1])
        bias_row = sb("bias_row", [1, 3 * D + 1])
        qkw_sb = sb("qkw_sb", [P, 2])
        qkb_sb = sb("qkb_sb", [1, 2])
        qkb_row = sb("qkb_row", [1, 3, 32])
        fcb_sb = sb("fcb_sb", [P, HEADS])
        bq_prod = sb("bq_prod", [P, 3, 32])
        fence = sb("fence", [P, 16])
        fence_pool = sb("fence_pool", [P, 32])
        ln_guard = sb("ln_guard", [P, 1])
        rms_guard = sb("rms_guard", [P, 1])

        A = [sb(f"A{i}", [P, R, N]) for i in range(2)]
        AT = [sb(f"AT{i}", [P, 2, HALVES, N]) for i in range(2)]
        M = [sb(f"M{i}", [P, R, N]) for i in range(2)]
        x_in = sb("x_in", [P, R, D])
        X = [sb(f"X{i}", [P, R, D]) for i in range(2)]
        XH = [sb(f"XH{i}", [P, R, D]) for i in range(2)]
        ZH = [sb(f"ZH{i}", [P, R, D]) for i in range(2)]
        G = [sb(f"G{i}", [P, R, HEADS, D]) for i in range(2)]
        q_rows = [sb(f"q_rows{i}", [QROWS, 2 * N], bf16) for i in range(2)]
        k_rows = [sb(f"k_rows{i}", [QROWS, HEADS, 2 * N], bf16) for i in range(2)]

        st_e = sb("st_e", [P, R, 6])
        mv_e = sb("mv_e", [P, R, 2])
        lv_e = sb("lv_e", [P, R])
        rs_e = sb("rs_e", [P, R])
        xn_e = sb("xn_e", [P, R, D])
        h1_e = sb("h1_e", [P, R, D])
        ht_e = sb("ht_e", [P, R * P])
        y_e = sb("y_e", [P, R, D])
        het = sb("het", [P, R, D])
        gate = sb("gate", [P, R, D])
        mix = sb("mix", [P, R, D])
        elu = sb("elu", [P, R, D])
        sums = sb("sums", [P, 8])
        row_copy = sb("row_copy", [P, R, N])
        degc = sb("degc", [P, 12])
        scl = sb("scl", [P, 12])
        s_in_out = sb("s_in_out", [P, 8])
        neg_s_out = sb("neg_s_out", [P, R])
        u1 = sb("u1", [P, R, D])
        pre = sb("pre", [P, R, D])
        softp = sb("softp", [P, R, D])

        st_l = sb("st_l", [P, R, 6])
        mv_l = sb("mv_l", [P, R, 2])
        lv_l = sb("lv_l", [P, R])
        rs_l = sb("rs_l", [P, R])
        xn_l = sb("xn_l", [P, R, D])
        h2 = sb("h2", [P, R, D])
        zt = sb("zt", [P, R * P])
        hid = sb("hid", [P, HB, R * P])
        sq = sb("sq", [P, HB, R * P])
        rms_b = sb("rms_b", [P, R * P])
        x_b2 = sb("x_b2", [P, R, D])
        ht_l = sb("ht_l", [P, R * P])
        qk_f = sb("qk_f", [QROWS, 2 * N])
        qk_r = sb("qk_r", [QROWS, 2 * N])
        qk_s = sb("qk_s", [QROWS, 2 * N], bf16)

        S = [sb(f"S{i}", [P, 2, HALVES, N]) for i in range(SB)]
        mx = [sb(f"mx{i}", [P, 4]) for i in range(SB)]
        ng = [sb(f"ng{i}", [P, 4]) for i in range(SB)]
        nm = [sb(f"nm{i}", [P, 4]) for i in range(SB)]
        sm = [sb(f"sm{i}", [P, 4]) for i in range(SB)]
        rc = [sb(f"rc{i}", [P, 4]) for i in range(SB)]
        ET = [sb(f"ET{i}", [P, HALVES, N]) for i in range(2)]
        zf = [sb(f"zf{i}", [P, HALVES, D]) for i in range(2)]
        res = [sb(f"res{i}", [P, HALVES, D]) for i in range(2)]

        fc_sb = hid[:, 0:2, :].rearrange("p a n -> p (a n)")
        fct = hid[:, 2:4, :].rearrange("p a n -> p (a n)")
        fp_sb = sq[:, 0:2, :].rearrange("p a n -> p (a n)").rearrange("p (h d) -> p h d", d=D)
        fcb_cols = sq[:, 2:4, :].rearrange("p a n -> p (a n)").rearrange("p (h d) -> p h d", d=D)
        ws_sb = xn_l[:, 0, :]

        def bank(name):
            return ctx.enter_context(nc.psum_tensor(name, [P, 512], fp32))

        ps_e = bank("ps_e")
        ps_l = [bank(f"ps_l{i}") for i in range(2)]
        ps_s = [bank(f"ps_s{i}") for i in range(2)]
        ps_t = [bank(f"ps_t{i}") for i in range(2)]
        ps_o = bank("ps_o")

        p_first = sem("p_first")
        p_load = sem("p_load")
        p_early = sem("p_early")
        p_pool = sem("p_pool")
        p_pe = sem("p_pe")
        p_zeroed = sem("p_zeroed")
        p_products = sem("p_products")
        p_fct = sem("p_fct")
        p_weights = sem("p_weights")
        adj_in = [sem(f"adj_in{i}") for i in range(2)]
        x_loaded = signal("x_loaded", LOADED)
        stored = [signal(f"stored{i}", LOADED) for i in range(2)]
        e_adj_tr = signal("e_adj_tr", 2)
        e_at = signal("e_at", 2)
        e_sums = signal("e_sums")
        e_degc = signal("e_degc")
        e_scl = signal("e_scl", 2)
        e_masked = signal("e_masked")
        e_norms = signal("e_norms")
        e_bn = signal("e_bn", 3)
        e_mv = signal("e_mv", 3)
        e_lv = signal("e_lv", 3)
        e_rs = signal("e_rs", 3)
        e_xn = signal("e_xn", 3)
        e_h1 = signal("e_h1")
        e_tr0 = signal("e_tr0")
        e_ht0 = signal("e_ht0")
        e_proj_ps = signal("e_proj_ps", 4)
        e_proj = signal("e_proj", 4)
        e_clamped = signal("e_clamped")
        e_gate = signal("e_gate", 3)
        e_hop0 = signal("e_hop0")
        e_dif = signal("e_dif")
        e_gated = signal("e_gated")
        e_mix = signal("e_mix")
        e_min = signal("e_min")
        e_expm = signal("e_expm")
        e_elu = signal("e_elu")
        e_x0 = signal("e_x0")
        e_tr1 = signal("e_tr1")
        e_ht1 = signal("e_ht1")
        e_u_ps = signal("e_u_ps", 2)
        e_u = signal("e_u", 2)
        e_hop1 = signal("e_hop1")
        e_pre = signal("e_pre")
        e_sp = signal("e_sp", 3)
        e_part = signal("e_part")
        e_x1 = signal("e_x1")
        l_mask = signal("l_mask")
        l_bn = signal("l_bn", 2)
        l_mv = signal("l_mv", 2)
        l_lv = signal("l_lv", 2)
        l_rs = signal("l_rs", 2)
        l_xn = signal("l_xn", 2)
        l_h2 = signal("l_h2")
        l_z_ps = signal("l_z_ps")
        l_zt = signal("l_zt")
        l_hid_ps = signal("l_hid_ps", 4)
        l_hid = signal("l_hid", 4)
        l_sq = signal("l_sq", 4)
        l_sum = signal("l_sum", 3)
        l_ss_ps = signal("l_ss_ps")
        l_rms = signal("l_rms", 2)
        l_g = signal("l_g", 4)
        l_cl = signal("l_cl", 4)
        l_sig = signal("l_sig", 6)
        l_act = signal("l_act", 4)
        l_w2_ps = signal("l_w2_ps")
        l_xb = signal("l_xb")
        l_x2 = signal("l_x2")
        l_tr = signal("l_tr")
        l_ht = signal("l_ht")
        l_zh = signal("l_zh")
        l_qk_ps = signal("l_qk_ps")
        l_split = signal("l_split", 4)
        l_rest = signal("l_rest")
        l_rows = signal("l_rows")
        l_late_rows = signal("l_late_rows")
        l_g_ps = signal("l_g_ps", 8)
        l_features = signal("l_features", 8)
        h_qk = signal("h_qk", 16)
        h_max = signal("h_max", 16)
        h_neg = signal("h_neg", 8)
        h_leaky = signal("h_leaky", 8)
        h_exp = signal("h_exp", 8)
        h_rc = signal("h_rc", 8)
        h_norm = signal("h_norm", 8)
        h_tr = signal("h_tr", 16)
        h_et = signal("h_et", 16)
        h_av = signal("h_av", 16)
        f_z = signal("f_z", 2)
        f_c = signal("f_c", 2)
        f_s = signal("f_s", 6)
        f_res = signal("f_res", 2)

        def iterations(engine, body):
            for t in range(5):
                body(t, t % 2, t)
            with engine.Fori(5, PAIRS - 2, 2) as t:
                body(t, 1, None)
                body(t + 1, 0, None)
            for t in range(PAIRS - 1, PAIRS + 3):
                body(t, t % 2, t)

        def mine(known, back):
            return known is None or 0 <= known - back < PAIRS

        block = ctx.enter_context(nc.Block())

        @block.sync
        def _(sp):
            def load_adj(t, p, k):
                sp.dma_start(A[p][:, :, :], adj_v[t]).then_inc(adj_in[p], 16)

            load_adj(0, 0, 0)
            sp.dma_start(x_in[:, :, :], x_v[0]).then_inc(x_loaded.semaphore, 16)
            for dst, src in (
                (w_proj[:, 0:D], theta), (w_proj[:, D:2 * D], w_h), (w_proj[:, 2 * D:3 * D], w_t),
                (bias_row[:, 0:D], b_t.rearrange("(a n) -> a n", a=1)),
                (bias_row[:, D:2 * D], b2.rearrange("(a n) -> a n", a=1)),
                (bias_row[:, 2 * D:3 * D], fp_b.rearrange("(a n) -> a n", a=1)),
                (bias_row[:, 3 * D:3 * D + 1], epsilon),
                (ws_sb, w_self), (w_l1[:, D:2 * D], w_neigh),
                (gamma_sb[:, :], gamma.rearrange("(p a) -> p a", a=1)),
                (beta_sb[:, :], beta.rearrange("(p a) -> p a", a=1)),
            ):
                sp.dma_start(dst, src).then_inc(p_first, 16)
            for dst, src in (
                (fc_sb, fc_w), (fp_sb, fp_w.rearrange("(h e) d -> e h d", e=P)),
                (qkw_sb[:, 0:1], q_w), (qkw_sb[:, 1:2], k_w),
                (qkb_sb[:, 0:1], q_b.rearrange("(a n) -> a n", a=1)),
                (qkb_sb[:, 1:2], k_b.rearrange("(a n) -> a n", a=1)),
                (w1_sb[:, :], w1), (w2_sb[:, :, :], w2.rearrange("(b p) d -> p b d", p=P)),
                (select[:, :], row_select),
            ):
                sp.dma_start(dst, src).then_inc(p_load, 16)
            with nc.allow_non_contiguous_dma(reason="three short vectors, once"):
                sp.dma_start(b1_sb[:, :], b1.rearrange("(b p) -> p b", p=P)).then_inc(p_load, 16)
                sp.dma_start(rmsw_sb[:, :], rms_w.rearrange("(b p) -> p b", p=P)).then_inc(p_load, 16)
                sp.dma_start(fcb_sb[:, :], fc_b.rearrange("(h e) -> e h", e=P)).then_inc(p_load, 16)

            def store(pair, g):
                sp.wait_ge(f_res.semaphore, f_res.at(pair, g + 1))
                sp.dma_start(out_v[pair * 2 + g], res[g][:, :, :]).then_inc(stored[g].semaphore, 16)

            def body(t, p, known):
                if mine(known, 3):
                    store(t - 3, 1)
                if known is None or known + 1 < PAIRS:
                    if due(l_mask.at(t - 1)):
                        sp.wait_ge(l_mask.semaphore, l_mask.at(t - 1))
                    if due(e_sums.at(t - 1)):
                        sp.wait_ge(e_sums.semaphore, e_sums.at(t - 1))
                    load_adj(t + 1, 1 - p, None)
                    sp.wait_ge(e_x0.semaphore, e_x0.at(t))
                    sp.dma_start(x_in[:, :, :], x_v[t + 1]).then_inc(x_loaded.semaphore, 16)
                if mine(known, 2):
                    store(t - 2, 0)

            iterations(sp, body)
            for g in range(2):
                sp.wait_ge(stored[g].semaphore, stored[g].at(PAIRS - 1))

        @block.gpsimd
        def _(pool):
            pool.memset(ident[:, :], 0.0).then_inc(p_pool, 1)
            pool.memset(ones[:, :], 1.0).then_inc(p_pool, 1)
            pool.memset(fence_pool[:, :], 0.0).then_inc(p_pool, 1)
            pool.wait_ge(p_pool, 3)
            pool.affine_select(out=ident[:, :], in_=ident[:, :], compare_op=ALU.not_equal, fill=1.0,
                               base=0, pattern=[[-1, P]], channel_multiplier=1).then_inc(p_pool, 1)
            pool.wait_ge(p_early, 1)

            def residual_bias(tl, q):
                pool.wait_ge(e_x1.semaphore, e_x1.at(tl))
                if due(l_x2.at(tl - 1)):
                    pool.wait_ge(l_x2.semaphore, l_x2.at(tl - 1))
                pool.tensor_tensor(x_b2[:, 0, :], X[q][:, 0, :], b2_rows[:, :], ALU.add)
                for r in range(1, R):
                    last = pool.tensor_tensor(x_b2[:, r, :], X[q][:, r, :], b2_rows[:, :], ALU.add)
                last.then_inc(l_xb.semaphore, 1)

            carried = [0]

            def carrier():
                carried[0] += 1
                column = 4 + carried[0] % 28
                return fence_pool[:, column:column + 1], fence_pool[:, 0:1], fence_pool[:, 1:2]

            def residual0(t, p):
                pool.wait_ge(e_elu.semaphore, e_elu.at(t))
                pool.tensor_tensor(X[p][:, :, :], x_in[:, :, :], mix[:, :, :], ALU.add)\
                    .then_inc(e_x0.semaphore, 1)

            def residual1(t, p):
                pool.wait_ge(e_part.semaphore, e_part.at(t))
                pool.wait_ge(e_sp.semaphore, e_sp.at(t))
                pool.tensor_tensor(X[p][:, :, :], pre[:, :, :], softp[:, :, :], ALU.add)\
                    .then_inc(e_x1.semaphore, 1)

            def mix_up(t):
                pool.wait_ge(e_dif.semaphore, e_dif.at(t))
                pool.wait_ge(e_gate.semaphore, e_gate.at(t))
                pool.tensor_tensor(mix[:, :, :], mix[:, :, :], gate[:, :, :], ALU.mult).then_inc(e_gated.semaphore, 1)
                pool.wait_ge(e_gated.semaphore, e_gated.at(t))
                pool.tensor_tensor(mix[:, :, :], mix[:, :, :], het[:, :, :], ALU.add).then_inc(e_mix.semaphore, 1)

            def mask(t, q):
                if due(h_max.at(t - 2)):
                    pool.wait_ge(h_max.semaphore, h_max.at(t - 2))
                pool.wait_ge(e_sums.semaphore, e_sums.at(t))
                pool.tensor_tensor(*carrier(), ALU.add)
                pool.tensor_scalar(M[q][:, :, :], A[q][:, :, :], -1.0, -NEG, ALU.add, ALU.mult)\
                    .then_inc(l_mask.semaphore, 1)

            def sum_squares(t, n):
                a, b = ((0, 1), (2, 3), (0, 2))[n]
                if n < 2:
                    pool.wait_ge(l_sq.semaphore, l_sq.at(t, 2 * n + 2))
                else:
                    pool.wait_ge(l_sum.semaphore, l_sum.at(t, 2))
                pool.tensor_tensor(sq[:, a, :], sq[:, a, :], sq[:, b, :], ALU.add)\
                    .then_inc(l_sum.semaphore, 1)

            def rms_scale(t, b):
                pool.wait_ge(l_rms.semaphore, l_rms.at(t))
                pool.tensor_tensor(hid[:, b, :], hid[:, b, :], rms_b[:, :], ALU.mult).then_inc(l_g.semaphore, 1)

            def silu_block(t, b):
                pool.wait_ge(l_sig.semaphore, l_sig.at(t, 5 + b // 2))
                pool.tensor_tensor(hid[:, b, :], hid[:, b, :], sq[:, b, :], ALU.mult)\
                    .then_inc(l_act.semaphore, 1)

            def qk_rest(t):
                pool.wait_ge(l_split.semaphore, l_split.at(t, 2))
                pool.tensor_tensor(qk_r[:, :], qk_f[:, :], qk_s[:, :], ALU.subtract).then_inc(l_rest.semaphore, 1)

            def key_rows(t, q):
                if due(h_qk.at(t - 2)):
                    pool.wait_ge(h_qk.semaphore, h_qk.at(t - 2))
                pool.wait_ge(l_split.semaphore, l_split.at(t))
                pool.tensor_tensor(*carrier(), ALU.add)
                for h in range(HEADS - HEADS // 2, HEADS):
                    last = pool.tensor_scalar(k_rows[q][:, h, :], qk_s[:, :], select[:, 2 + h:3 + h],
                                              select[:, 2 + HEADS + h:3 + HEADS + h], ALU.mult, ALU.add)
                last.then_inc(l_late_rows.semaphore, 1)

            def normalise(pair, u):
                pool.wait_ge(h_rc.semaphore, h_rc.at(pair, u + 1))
                pool.tensor_tensor(*carrier(), ALU.add)
                for k in range(4):
                    row = S[u % SB][:, k // 2, k % 2, :]
                    last = pool.tensor_scalar(row, row, rc[u % SB][:, k:k + 1], 1.0, ALU.mult, ALU.mult)
                last.then_inc(h_norm.semaphore, 1)

            def final_out(pair, g, q):
                pool.wait_ge(f_s.semaphore, f_s.at(pair, 3 * g + 3))
                if due(stored[g].at(pair - 1)):
                    pool.wait_ge(stored[g].semaphore, stored[g].at(pair - 1))
                pool.tensor_tensor(res[g][:, :, :], XH[q][:, HALVES * g:HALVES * g + HALVES, :], zf[g][:, :, :],
                                   ALU.add)\
                    .then_inc(f_res.semaphore, 1)

            def body(t, p, known):
                early, late, heads, tail = (mine(known, back) for back in range(4))
                if heads:
                    silu_block(t - 2, 0)
                    silu_block(t - 2, 1)
                    silu_block(t - 2, 2)
                    silu_block(t - 2, 3)
                if tail:
                    normalise(t - 3, 3)
                    normalise(t - 3, 4)
                if late:
                    residual1(t - 1, 1 - p)
                if tail:
                    normalise(t - 3, 5)
                if late:
                    mask(t - 1, 1 - p)
                if heads:
                    qk_rest(t - 2)
                    key_rows(t - 2, p)
                if late:
                    residual_bias(t - 1, 1 - p)
                if tail:
                    normalise(t - 3, 6)
                    normalise(t - 3, 7)
                if early:
                    mix_up(t)
                if heads:
                    normalise(t - 2, 0)
                if early:
                    residual0(t, p)
                if late:
                    sum_squares(t - 1, 0)
                    sum_squares(t - 1, 1)
                    sum_squares(t - 1, 2)
                if heads:
                    normalise(t - 2, 1)
                if late:
                    rms_scale(t - 1, 0)
                    rms_scale(t - 1, 1)
                    rms_scale(t - 1, 2)
                    rms_scale(t - 1, 3)
                if heads:
                    normalise(t - 2, 2)
                if tail:
                    final_out(t - 3, 0, 1 - p)
                    final_out(t - 3, 1, 1 - p)

            iterations(pool, body)

        @block.scalar
        def _(act):
            act.preload_act_table_set("natural_log_exp_and_others")
            act.wait_ge(p_early, 1)

            def adj_evac(t, p, g):
                act.wait_ge(e_adj_tr.semaphore, e_adj_tr.at(t, g + 1))
                if g == 0:
                    if due(e_masked.at(t - 1)):
                        act.wait_ge(e_masked.semaphore, e_masked.at(t - 1))
                for m in range(HALVES):
                    r = HALVES * g + m
                    last = act.activation(AT[p][:, g, m, :], ps_e[:, m * N:(m + 1) * N], ACT.Copy,
                                          accum_out=sums[:, R + r:R + r + 1])
                last.then_inc(e_at.semaphore, 1)

            def row_sums(t, p):
                for r in range(R):
                    last = act.activation(row_copy[:, r, :], A[p][:, r, :], ACT.Copy, accum_out=sums[:, r:r + 1])
                last.then_inc(e_sums.semaphore, 1)

            def degree_roots(t):
                act.wait_ge(e_degc.semaphore, e_degc.at(t))
                act.activation(degc[:, :], degc[:, :], ACT.Ln).then_inc(e_scl.semaphore, 1)
                act.wait_ge(e_scl.semaphore, e_scl.at(t, 1))
                act.activation(scl[:, :], degc[:, :], ACT.Exp, scale=-0.5).then_inc(e_scl.semaphore, 1)

            def rstd(t, k, mv, lv, rs, s_mv, s_lv, s_rs):
                act.wait_ge(s_mv.semaphore, s_mv.at(t, k))
                act.activation(lv[:, :], mv[:, :, 1], ACT.Ln, bias=ln_guard[:, 0:1]).then_inc(s_lv.semaphore, 1)
                act.wait_ge(s_lv.semaphore, s_lv.at(t, k))
                act.activation(rs[:, :], lv[:, :], ACT.Exp, scale=-0.5).then_inc(s_rs.semaphore, 1)

            def rstd_e(t, k):
                rstd(t, k, mv_e, lv_e, rs_e, e_mv, e_lv, e_rs)

            def rstd_l(t, k):
                rstd(t, k, mv_l, lv_l, rs_l, l_mv, l_lv, l_rs)

            def relu_t0(t):
                act.wait_ge(e_tr0.semaphore, e_tr0.at(t))
                act.activation(ht_e[:, :], ps_e[:, :], ACT.Relu).then_inc(e_ht0.semaphore, 1)

            def gate_sigmoid(t):
                flat = gate[:, :, :].rearrange("p r d -> p (r d)")
                act.wait_ge(e_clamped.semaphore, e_clamped.at(t))
                act.activation(flat, flat, ACT.Exp, scale=-1.0).then_inc(e_gate.semaphore, 1)
                act.wait_ge(e_gate.semaphore, e_gate.at(t, 1))
                act.activation(flat, flat, ACT.Ln, bias=1.0).then_inc(e_gate.semaphore, 1)
                act.wait_ge(e_gate.semaphore, e_gate.at(t, 2))
                act.activation(flat, flat, ACT.Exp, scale=-1.0).then_inc(e_gate.semaphore, 1)

            def elu_exp(t):
                flat = elu[:, :, :].rearrange("p r d -> p (r d)")
                act.wait_ge(e_min.semaphore, e_min.at(t))
                act.activation(flat, flat, ACT.Exp).then_inc(e_expm.semaphore, 1)

            def softplus(t):
                flat = softp[:, :, :].rearrange("p r d -> p (r d)")
                act.wait_ge(e_pre.semaphore, e_pre.at(t))
                act.activation(flat, pre[:, :, :].rearrange("p r d -> p (r d)"), ACT.Abs).then_inc(e_sp.semaphore, 1)
                act.wait_ge(e_sp.semaphore, e_sp.at(t, 1))
                act.activation(flat, flat, ACT.Exp, scale=-1.0).then_inc(e_sp.semaphore, 1)
                act.wait_ge(e_sp.semaphore, e_sp.at(t, 2))
                act.activation(flat, flat, ACT.Ln, bias=1.0).then_inc(e_sp.semaphore, 1)

            def zt_evac(t):
                act.wait_ge(l_z_ps.semaphore, l_z_ps.at(t))
                act.activation(zt[:, :], ps_l[1][:, :], ACT.Copy).then_inc(l_zt.semaphore, 1)

            def hid_evac(t, b):
                act.wait_ge(l_hid_ps.semaphore, l_hid_ps.at(t, b + 1))
                act.activation(hid[:, b, :], ps_l[b % 2][:, :], ACT.Identity, bias=b1_sb[:, b:b + 1])\
                    .then_inc(l_hid.semaphore, 1)

            def square(t, b):
                act.wait_ge(l_hid.semaphore, l_hid.at(t, b + 1))
                act.activation(sq[:, b, :], hid[:, b, :], ACT.Square).then_inc(l_sq.semaphore, 1)

            def rms(t):
                act.wait_ge(l_ss_ps.semaphore, l_ss_ps.at(t))
                act.activation(rms_b[:, :], ps_l[0][:, :], ACT.Ln, bias=rms_guard[:, 0:1], scale=1.0 / HID)\
                    .then_inc(l_rms.semaphore, 1)
                act.wait_ge(l_rms.semaphore, l_rms.at(t, 1))
                act.activation(rms_b[:, :], rms_b[:, :], ACT.Exp, scale=-0.5).then_inc(l_rms.semaphore, 1)

            def half(i):
                return sq[:, 2 * i:2 * i + 2, :].rearrange("p b n -> p (b n)")

            def silu_exp(t, i):
                act.wait_ge(l_cl.semaphore, l_cl.at(t, 2 * i + 2))
                act.activation(half(i), half(i), ACT.Exp, scale=-1.0).then_inc(l_sig.semaphore, 1)

            def silu_ln(t, i):
                act.wait_ge(l_sig.semaphore, l_sig.at(t, 1 + i))
                act.activation(half(i), half(i), ACT.Ln, bias=1.0).then_inc(l_sig.semaphore, 1)

            def silu_sig(t, i):
                act.wait_ge(l_sig.semaphore, l_sig.at(t, 3 + i))
                act.activation(half(i), half(i), ACT.Exp, scale=-1.0).then_inc(l_sig.semaphore, 1)

            def relu_t3(t):
                act.wait_ge(l_tr.semaphore, l_tr.at(t))
                act.activation(ht_l[:, :], ps_l[0][:, :], ACT.Relu).then_inc(l_ht.semaphore, 1)

            def g_evac(t, q, k):
                act.wait_ge(l_g_ps.semaphore, l_g_ps.at(t, k + 1))
                if k == 0:
                    if due(h_av.at(t - 2)):
                        act.wait_ge(h_av.semaphore, h_av.at(t - 2))
                act.activation(G[q][:, k // 2, 4 * (k % 2):4 * (k % 2) + 4, :].rearrange("p h d -> p (h d)"),
                                    ps_l[k % 2][:, :], ACT.Copy)\
                    .then_inc(l_features.semaphore, 1)

            def exp(pair, u, k):
                if k == 0:
                    act.wait_ge(h_leaky.semaphore, h_leaky.at(pair, u + 1))
                row = S[u % SB][:, k // 2, k % 2, :]
                ins = act.activation(row, row, ACT.Exp, bias=nm[u % SB][:, k:k + 1],
                                     accum_out=sm[u % SB][:, k:k + 1])
                if k == 3:
                    ins.then_inc(h_exp.semaphore, 1)

            def et_evac(pair, u, j):
                act.wait_ge(h_tr.semaphore, h_tr.at(pair, 2 * u + j + 1))
                if due(h_av.at(pair, 2 * u + j - 1)):
                    act.wait_ge(h_av.semaphore, h_av.at(pair, 2 * u + j - 1))
                act.activation(ET[j][:, :, :].rearrange("p a n -> p (a n)"), ps_t[j][:, :], ACT.Copy)\
                    .then_inc(h_et.semaphore, 1)

            def final_sigmoid(pair, g):
                flat = zf[g][:, :, :].rearrange("p r d -> p (r d)")
                act.wait_ge(f_c.semaphore, f_c.at(pair, g + 1))
                act.activation(flat, flat, ACT.Exp, scale=-1.0).then_inc(f_s.semaphore, 1)
                act.wait_ge(f_s.semaphore, f_s.at(pair, 3 * g + 1))
                act.activation(flat, flat, ACT.Ln, bias=1.0).then_inc(f_s.semaphore, 1)
                act.wait_ge(f_s.semaphore, f_s.at(pair, 3 * g + 2))
                act.activation(flat, flat, ACT.Exp, scale=-1.0).then_inc(f_s.semaphore, 1)

            def body(t, p, known):
                early, late, heads, tail = (mine(known, back) for back in range(4))
                if early:
                    adj_evac(t, p, 0)
                if tail:
                    exp(t - 3, 4, 0)
                    et_evac(t - 3, 2, 1)
                if early:
                    adj_evac(t, p, 1)
                    row_sums(t, p)
                    rstd_e(t, 1)
                if tail:
                    exp(t - 3, 4, 1)
                    exp(t - 3, 4, 2)
                    exp(t - 3, 4, 3)
                    et_evac(t - 3, 3, 0)
                    exp(t - 3, 5, 0)
                if early:
                    degree_roots(t)
                if tail:
                    et_evac(t - 3, 3, 1)
                if early:
                    relu_t0(t)
                if heads:
                    rstd_l(t - 2, 2)
                if tail:
                    exp(t - 3, 5, 1)
                    exp(t - 3, 5, 2)
                    exp(t - 3, 5, 3)
                    exp(t - 3, 6, 0)
                if heads:
                    relu_t3(t - 2)
                if tail:
                    exp(t - 3, 6, 1)
                    exp(t - 3, 6, 2)
                    et_evac(t - 3, 4, 0)
                    exp(t - 3, 6, 3)
                    et_evac(t - 3, 4, 1)
                if heads:
                    g_evac(t - 2, p, 0)
                if tail:
                    exp(t - 3, 7, 0)
                    exp(t - 3, 7, 1)
                if heads:
                    g_evac(t - 2, p, 1)
                    g_evac(t - 2, p, 2)
                if tail:
                    et_evac(t - 3, 5, 0)
                if heads:
                    g_evac(t - 2, p, 3)
                if tail:
                    exp(t - 3, 7, 2)
                if heads:
                    g_evac(t - 2, p, 4)
                    g_evac(t - 2, p, 5)
                if tail:
                    exp(t - 3, 7, 3)
                if heads:
                    g_evac(t - 2, p, 6)
                    g_evac(t - 2, p, 7)
                if late:
                    rstd_l(t - 1, 1)
                if early:
                    gate_sigmoid(t)
                if heads:
                    exp(t - 2, 0, 0)
                    exp(t - 2, 0, 1)
                    exp(t - 2, 0, 2)
                if tail:
                    et_evac(t - 3, 5, 1)
                if heads:
                    exp(t - 2, 0, 3)
                if tail:
                    et_evac(t - 3, 6, 0)
                    final_sigmoid(t - 3, 0)
                if late:
                    zt_evac(t - 1)
                if heads:
                    exp(t - 2, 1, 0)
                if early:
                    elu_exp(t)
                if heads:
                    exp(t - 2, 1, 1)
                if late:
                    hid_evac(t - 1, 0)
                    hid_evac(t - 1, 1)
                    square(t - 1, 0)
                    square(t - 1, 1)
                    hid_evac(t - 1, 2)
                    hid_evac(t - 1, 3)
                    square(t - 1, 2)
                    square(t - 1, 3)
                if early:
                    rstd_e(t, 2)
                if tail:
                    et_evac(t - 3, 6, 1)
                    et_evac(t - 3, 7, 0)
                if heads:
                    exp(t - 2, 1, 2)
                    exp(t - 2, 1, 3)
                    exp(t - 2, 2, 0)
                if tail:
                    et_evac(t - 3, 7, 1)
                if heads:
                    exp(t - 2, 2, 1)
                if late:
                    rms(t - 1)
                if early:
                    rstd_e(t, 3)
                if heads:
                    et_evac(t - 2, 0, 0)
                    exp(t - 2, 2, 2)
                    exp(t - 2, 2, 3)
                    exp(t - 2, 3, 0)
                    exp(t - 2, 3, 1)
                    et_evac(t - 2, 0, 1)
                if tail:
                    final_sigmoid(t - 3, 1)
                if heads:
                    et_evac(t - 2, 1, 0)
                if late:
                    silu_exp(t - 1, 0)
                    silu_exp(t - 1, 1)
                    silu_ln(t - 1, 0)
                    silu_ln(t - 1, 1)
                    silu_sig(t - 1, 0)
                if heads:
                    exp(t - 2, 3, 2)
                    et_evac(t - 2, 1, 1)
                if late:
                    silu_sig(t - 1, 1)
                if heads:
                    exp(t - 2, 3, 3)
                    et_evac(t - 2, 2, 0)
                if early:
                    softplus(t)
                if known == 0:
                    act.wait_ge(p_weights, 5)

            iterations(act, body)

        @block.vector
        def _(dve):
            dve.memset(w_qk[:, :, :], 0.0).then_inc(p_zeroed, 1)
            dve.memset(bq_prod[:, :, :], 0.0).then_inc(p_zeroed, 1)
            dve.memset(qkb_row[:, :, :], 0.0).then_inc(p_zeroed, 1)
            dve.memset(ln_guard[:, :], 1e-5)
            dve.memset(rms_guard[:, :], 1e-6)
            dve.memset(fcb_cols, 0.0).then_inc(p_zeroed, 1)
            dve.wait_ge(p_first, 16 * 11)
            dve.wait_ge(p_zeroed, 4)
            dve.tensor_tensor(w_l1[:, 0:D], ws_sb, w_l1[:, D:2 * D], ALU.add)
            dve.wait_ge(p_pe, 1)
            dve.tensor_copy(bt_rows[:, :], ps_l[0][:, 0:D])
            dve.tensor_copy(b2_rows[:, :], ps_l[0][:, D:2 * D])
            dve.tensor_copy(eps_col[:, :], ps_l[0][:, 3 * D:3 * D + 1]).then_inc(p_early, 1)

            def prepare_products():
                dve.wait_ge(p_load, 16 * 12)
                for b in range(HB):
                    dve.tensor_scalar(w2_sb[:, b, :], w2_sb[:, b, :], rmsw_sb[:, b:b + 1], None, ALU.mult)
                for part in range(3):
                    for kind in range(2):
                        dve.tensor_scalar(bq_prod[:, part, 8 * kind:8 * kind + 8], fcb_sb[:, :],
                                          qkw_sb[:, kind:kind + 1], None, ALU.mult)
                        dve.tensor_scalar(qkb_row[:, part, 8 * kind:8 * kind + 8], qkb_row[:, part, 8 * kind:8 * kind + 8],
                                          qkb_sb[:, kind:kind + 1], None, ALU.add)
                for h in range(HEADS):
                    last = dve.tensor_scalar(fcb_cols[:, h, :], fcb_cols[:, h, :], fcb_sb[:, h:h + 1], None, ALU.add)
                last.then_inc(p_products, 1)
                dve.wait_ge(p_early, 1)
                dve.wait_ge(p_pool, 4)
                dve.tensor_scalar(eps_ident[:, :], ident[:, :], eps_col[:, 0:1], None, ALU.mult).then_inc(p_weights, 1)

            def prepare_transposed():
                dve.wait_ge(p_pe, 2)
                dve.tensor_copy(bfin_rows[:, :], ps_l[1][:, 0:D]).then_inc(p_weights, 1)
                dve.wait_ge(p_pe, 3)
                for i in range(2):
                    last = dve.tensor_copy(fct[:, 512 * i:512 * i + 512], ps_t[i][:, :])
                last.then_inc(p_fct, 1)

            def prepare_heads():
                dve.wait_ge(p_pe, 4)
                for i in range(2):
                    last = dve.tensor_copy(w_head[:, 512 * i:512 * i + 512], ps_s[i][:, :])
                last.then_inc(p_weights, 1)
                for part in range(3):
                    for kind in range(2):
                        last = dve.tensor_copy(w_qk[:, part, 8 * kind:8 * kind + 8], ps_o[:, kind:16:2])
                last.then_inc(p_weights, 1)
                dve.tensor_copy(b_qk[:, :], ps_o[0:QROWS, 32:33]).then_inc(p_weights, 1)

            carried = [0]

            def carrier():
                carried[0] += 1
                return fence[:, carried[0] % 16:carried[0] % 16 + 1]

            def stats(t, k, src, st, mv, s_bn, s_mv):
                for r in range(R):
                    last = dve.bn_stats(st[:, r, :], src[:, r, :])
                last.then_inc(s_bn.semaphore, 1)
                dve.wait_ge(s_bn.semaphore, s_bn.at(t, k))
                dve.memset(carrier(), 0.0)
                for r in range(R):
                    last = dve.bn_aggr(mv[:, r, :], st[:, r, :])
                last.then_inc(s_mv.semaphore, 1)

            def apply(t, k, dst, src, mv, rs, s_rs, sig):
                dve.wait_ge(s_rs.semaphore, s_rs.at(t, k))
                for r in range(R):
                    last = dve.tensor_scalar(dst[:, r, :], src[:, r, :], mv[:, r, 0:1], rs[:, r:r + 1],
                                             ALU.subtract, ALU.mult)
                last.then_inc(sig.semaphore, 1)

            def stats_e(t, k, src):
                stats(t, k, src, st_e, mv_e, e_bn, e_mv)

            def stats_l(t, k, src):
                stats(t, k, src, st_l, mv_l, l_bn, l_mv)

            def degrees(t):
                dve.wait_ge(e_sums.semaphore, e_sums.at(t))
                dve.tensor_scalar(degc[:, 0:4], sums[:, 0:4], 1e-6, 1e-19, ALU.add, ALU.max)
                dve.tensor_scalar(degc[:, 4:12], sums[:, :], 1e-19, None, ALU.max).then_inc(e_degc.semaphore, 1)

            def degree_masks(t):
                dve.wait_ge(e_scl.semaphore, e_scl.at(t))
                dve.scalar_tensor_tensor(out=s_in_out[:, :], in0=sums[:, :], scalar=0.0,
                                              in1=scl[:, 4:12], op0=ALU.not_equal, op1=ALU.mult)\
                    .then_inc(e_masked.semaphore, 1)
                dve.wait_ge(e_masked.semaphore, e_masked.at(t))
                dve.tensor_scalar(neg_s_out[:, :], s_in_out[:, 4:8], -1.0, None, ALU.mult).then_inc(e_norms.semaphore, 1)

            def proj_evac(t, r):
                dve.wait_ge(e_proj_ps.semaphore, e_proj_ps.at(t, r + 1))
                dve.tensor_scalar(y_e[:, r, :], ps_e[:, 0:D], scl[:, r:r + 1], None, ALU.mult)
                dve.tensor_copy(het[:, r, :], ps_e[:, D:2 * D])
                dve.tensor_tensor(gate[:, r, :], ps_e[:, 2 * D:3 * D], bt_rows[:, :], ALU.add)\
                    .then_inc(e_proj.semaphore, 1)

            def hop0_evac(t):
                dve.wait_ge(e_hop0.semaphore, e_hop0.at(t))
                for r in range(R):
                    last = dve.scalar_tensor_tensor(out=mix[:, r, :], in0=ps_e[:, r * D:(r + 1) * D],
                                                    scalar=scl[:, r:r + 1], in1=het[:, r, :],
                                                    op0=ALU.mult, op1=ALU.subtract)
                last.then_inc(e_dif.semaphore, 1)

            def gate_clamp(t):
                dve.wait_ge(e_proj.semaphore, e_proj.at(t))
                dve.tensor_scalar(gate[:, :, :], gate[:, :, :], FLOOR, None, ALU.max).then_inc(e_clamped.semaphore, 1)

            def elu_min(t):
                dve.wait_ge(e_mix.semaphore, e_mix.at(t))
                dve.tensor_scalar(elu[:, :, :], mix[:, :, :], 0.0, None, ALU.min).then_inc(e_min.semaphore, 1)

            def elu_out(t):
                dve.wait_ge(e_expm.semaphore, e_expm.at(t))
                dve.scalar_tensor_tensor(out=mix[:, :, :], in0=elu[:, :, :], scalar=-1.0,
                                         in1=mix[:, :, :], op0=ALU.add, op1=ALU.max)\
                    .then_inc(e_elu.semaphore, 1)

            def stats0(t):
                dve.wait_ge(x_loaded.semaphore, x_loaded.at(t))
                if due(e_xn.at(t - 1)):
                    dve.wait_ge(e_xn.semaphore, e_xn.at(t - 1))
                stats_e(t, 1, x_in)

            def stats1(t, p):
                dve.wait_ge(e_x0.semaphore, e_x0.at(t))
                stats_e(t, 2, X[p])

            def normed_x0(t, p):
                apply(t, 2, h1_e, X[p], mv_e, rs_e, e_rs, e_xn)

            def relu1(t):
                dve.wait_ge(e_xn.semaphore, e_xn.at(t, 2))
                dve.tensor_scalar(h1_e[:, :, :], h1_e[:, :, :], 0.0, None, ALU.max).then_inc(e_h1.semaphore, 1)

            def stats_h1(t):
                dve.wait_ge(e_h1.semaphore, e_h1.at(t))
                stats_e(t, 3, h1_e)

            def normed0(t):
                apply(t, 1, xn_e, x_in, mv_e, rs_e, e_rs, e_xn)

            def normed1(t):
                apply(t, 3, xn_e, h1_e, mv_e, rs_e, e_rs, e_xn)

            def ht1_evac(t):
                dve.wait_ge(e_tr1.semaphore, e_tr1.at(t))
                dve.tensor_scalar(ht_e[:, :], ps_e[:, :], gamma_sb[:, 0:1], beta_sb[:, 0:1],
                                       ALU.mult, ALU.add)\
                    .then_inc(e_ht1.semaphore, 1)

            def u_evac(t, i):
                dve.wait_ge(e_u_ps.semaphore, e_u_ps.at(t, i + 1))
                if i == 0:
                    dve.wait_ge(e_norms.semaphore, e_norms.at(t))
                for n in range(2):
                    r = 2 * i + n
                    dve.tensor_scalar(y_e[:, r, :], ps_e[:, n * 2 * D + D:(n + 1) * 2 * D],
                                      s_in_out[:, r:r + 1], None, ALU.mult)
                dve.tensor_copy(u1[:, 2 * i:2 * i + 2, :],
                                     ps_e[:, :].rearrange("p (n c) -> p n c", n=2)[:, :, 0:D])\
                    .then_inc(e_u.semaphore, 1)

            def hop1_evac(t):
                dve.wait_ge(e_hop1.semaphore, e_hop1.at(t))
                for r in range(R):
                    last = dve.scalar_tensor_tensor(out=pre[:, r, :], in0=ps_e[:, r * D:(r + 1) * D],
                                                    scalar=neg_s_out[:, r:r + 1], in1=u1[:, r, :],
                                                    op0=ALU.mult, op1=ALU.add)
                last.then_inc(e_pre.semaphore, 1)

            def softplus_part(t, p):
                dve.wait_ge(e_sp.semaphore, e_sp.at(t, 1))
                dve.scalar_tensor_tensor(out=pre[:, :, :], in0=pre[:, :, :], scalar=0.0,
                                         in1=X[p][:, :, :], op0=ALU.max, op1=ALU.add)\
                    .then_inc(e_part.semaphore, 1)

            def stats2(t, q):
                dve.wait_ge(e_x1.semaphore, e_x1.at(t))
                stats_l(t, 1, X[q])

            def normed_x1(t, q):
                if due(l_zh.at(t - 1)):
                    dve.wait_ge(l_zh.semaphore, l_zh.at(t - 1))
                apply(t, 1, xn_l, X[q], mv_l, rs_l, l_rs, l_xn)

            def relu2(t):
                dve.wait_ge(l_xn.semaphore, l_xn.at(t, 1))
                dve.tensor_scalar(h2[:, :, :], xn_l[:, :, :], 0.0, None, ALU.max).then_inc(l_h2.semaphore, 1)

            def silu_clamp(t, b):
                dve.wait_ge(l_g.semaphore, l_g.at(t, b + 1))
                dve.tensor_scalar(sq[:, b, :], hid[:, b, :], rmsw_sb[:, b:b + 1], FLOOR, ALU.mult, ALU.max)\
                    .then_inc(l_cl.semaphore, 1)

            def residual2(t, q):
                dve.wait_ge(l_w2_ps.semaphore, l_w2_ps.at(t))
                dve.wait_ge(l_xb.semaphore, l_xb.at(t))
                if due(f_res.at(t - 2)):
                    dve.wait_ge(f_res.semaphore, f_res.at(t - 2))
                dve.tensor_tensor(XH[q][:, :, :].rearrange("p r d -> p (r d)"), ps_l[1][:, :],
                                       x_b2[:, :, :].rearrange("p r d -> p (r d)"), ALU.add)\
                    .then_inc(l_x2.semaphore, 1)
                dve.wait_ge(l_x2.semaphore, l_x2.at(t))
                stats_l(t, 2, XH[q])

            def h3(t, q):
                apply(t, 2, xn_l, XH[q], mv_l, rs_l, l_rs, l_xn)

            def h3_bias(t, q):
                dve.wait_ge(l_xn.semaphore, l_xn.at(t, 2))
                if due(f_z.at(t - 2)):
                    dve.wait_ge(f_z.semaphore, f_z.at(t - 2))
                for r in range(R):
                    last = dve.scalar_tensor_tensor(out=ZH[q][:, r, :], in0=xn_l[:, r, :], scalar=0.0,
                                                    in1=bfin_rows[:, :], op0=ALU.max, op1=ALU.add)
                last.then_inc(l_zh.semaphore, 1)

            def qk_split(t):
                dve.wait_ge(l_qk_ps.semaphore, l_qk_ps.at(t))
                dve.tensor_scalar(qk_f[:, :], ps_l[1][0:QROWS, :], b_qk[:, 0:1], None, ALU.add)\
                    .then_inc(l_split.semaphore, 1)
                dve.wait_ge(l_split.semaphore, l_split.at(t, 1))
                dve.tensor_copy(qk_s[:, :], qk_f[:, :]).then_inc(l_split.semaphore, 1)

            def qk_later(t):
                dve.wait_ge(l_rest.semaphore, l_rest.at(t))
                dve.tensor_copy(qk_s[32:64, :], qk_r[32:64, :])
                dve.tensor_copy(qk_s[64:96, :], qk_r[64:96, :]).then_inc(l_split.semaphore, 1)
                dve.wait_ge(l_split.semaphore, l_split.at(t, 3))
                dve.tensor_tensor(qk_s[64:96, :], qk_r[64:96, :], qk_s[64:96, :], ALU.subtract)\
                    .then_inc(l_split.semaphore, 1)

            def qk_rows(t, q):
                dve.wait_ge(l_split.semaphore, l_split.at(t))
                if due(h_qk.at(t - 2)):
                    dve.wait_ge(h_qk.semaphore, h_qk.at(t - 2))
                dve.tensor_scalar(q_rows[q][:, :], qk_s[:, :], select[:, 0:1], select[:, 1:2], ALU.mult, ALU.add)
                for h in range(HEADS - HEADS // 2):
                    last = dve.tensor_scalar(k_rows[q][:, h, :], qk_s[:, :], select[:, 2 + h:3 + h],
                                             select[:, 2 + HEADS + h:3 + HEADS + h], ALU.mult, ALU.add)
                last.then_inc(l_rows.semaphore, 1)

            def head_max(pair, u, j, q):
                if j == 0:
                    if due(h_tr.at(pair, 2 * (u - SB) + 2)):
                        dve.wait_ge(h_tr.semaphore, h_tr.at(pair, 2 * (u - SB) + 2))
                    dve.wait_ge(h_qk.semaphore, h_qk.at(pair, 2 * u + 2))
                    dve.memset(carrier(), 0.0)
                g = u // GPG
                for i in range(HALVES):
                    last = dve.tensor_tensor_reduce(S[u % SB][:, j, i, :], ps_s[j][:, i * N:(i + 1) * N],
                                                    M[q][:, HALVES * g + i, :], 1.0, -3e38, ALU.add, ALU.max,
                                                    mx[u % SB][:, 2 * j + i:2 * j + i + 1])
                last.then_inc(h_max.semaphore, 1)

            def head_leaky(pair, u):
                b = u % SB
                dve.wait_ge(h_max.semaphore, h_max.at(pair, 2 * u + 2))
                dve.tensor_scalar(ng[b][:, :], mx[b][:, :], -1.0, None, ALU.mult).then_inc(h_neg.semaphore, 1)
                flat = S[b][:, :, :, :].rearrange("p j i n -> p (j i n)")
                dve.scalar_tensor_tensor(out=flat, in0=flat, scalar=SLOPE, in1=flat, op0=ALU.mult, op1=ALU.max)
                dve.wait_ge(h_neg.semaphore, h_neg.at(pair, u + 1))
                dve.scalar_tensor_tensor(out=nm[b][:, :], in0=mx[b][:, :], scalar=-SLOPE, in1=ng[b][:, :],
                                              op0=ALU.mult, op1=ALU.min)\
                    .then_inc(h_leaky.semaphore, 1)

            def head_recip(pair, u):
                dve.wait_ge(h_exp.semaphore, h_exp.at(pair, u + 1))
                dve.reciprocal(rc[u % SB][:, :], sm[u % SB][:, :]).then_inc(h_rc.semaphore, 1)

            def final_in(pair, g, q):
                dve.wait_ge(l_zh.semaphore, l_zh.at(pair))
                dve.wait_ge(h_av.semaphore, h_av.at(pair, 8 * (g + 1)))
                flat = zf[g][:, :, :].rearrange("p r d -> p (r d)")
                dve.tensor_tensor(flat, ps_o[:, g * HALVES * D:(g + 1) * HALVES * D],
                                       ZH[q][:, HALVES * g:HALVES * g + HALVES, :].rearrange("p r d -> p (r d)"),
                                       ALU.add)\
                    .then_inc(f_z.semaphore, 1)

            def final_clamp(pair, g):
                flat = zf[g][:, :, :].rearrange("p r d -> p (r d)")
                dve.wait_ge(f_z.semaphore, f_z.at(pair, g + 1))
                dve.tensor_scalar(flat, flat, FLOOR, None, ALU.max).then_inc(f_c.semaphore, 1)

            def body(t, p, known):
                early, late, heads, tail = (mine(known, back) for back in range(4))
                if early:
                    stats0(t)
                    if known == 0:
                        prepare_products()
                    degrees(t)
                    normed0(t)
                if tail:
                    head_recip(t - 3, 4)
                if heads:
                    residual2(t - 2, p)
                if tail:
                    head_max(t - 3, 7, 0, 1 - p)
                if heads:
                    h3(t - 2, p)
                if early:
                    degree_masks(t)
                    proj_evac(t, 0)
                if tail:
                    final_in(t - 3, 0, 1 - p)
                    head_recip(t - 3, 5)
                    head_max(t - 3, 7, 1, 1 - p)
                if early:
                    proj_evac(t, 1)
                if tail:
                    head_leaky(t - 3, 7)
                if heads:
                    qk_split(t - 2)
                    h3_bias(t - 2, p)
                if early:
                    proj_evac(t, 2)
                if heads:
                    qk_later(t - 2)
                    qk_rows(t - 2, p)
                if late:
                    stats2(t - 1, 1 - p)
                if tail:
                    final_clamp(t - 3, 0)
                if early:
                    proj_evac(t, 3)
                if tail:
                    head_recip(t - 3, 6)
                if heads:
                    head_max(t - 2, 0, 0, p)
                    head_max(t - 2, 0, 1, p)
                if early:
                    gate_clamp(t)
                if heads:
                    head_leaky(t - 2, 0)
                if tail:
                    head_recip(t - 3, 7)
                if late:
                    normed_x1(t - 1, 1 - p)
                    relu2(t - 1)
                if early:
                    hop0_evac(t)
                if heads:
                    head_max(t - 2, 1, 0, p)
                    head_max(t - 2, 1, 1, p)
                    head_leaky(t - 2, 1)
                    head_recip(t - 2, 0)
                if early:
                    elu_min(t)
                    elu_out(t)
                    if known == 0:
                        prepare_transposed()
                if heads:
                    head_max(t - 2, 2, 0, p)
                if early:
                    stats1(t, p)
                if heads:
                    head_max(t - 2, 2, 1, p)
                    head_leaky(t - 2, 2)
                if early:
                    normed_x0(t, p)
                if heads:
                    head_max(t - 2, 3, 0, p)
                if early:
                    relu1(t)
                if heads:
                    head_recip(t - 2, 1)
                if early:
                    stats_h1(t)
                if heads:
                    head_max(t - 2, 3, 1, p)
                    head_leaky(t - 2, 3)
                if early:
                    normed1(t)
                    if known == 0:
                        prepare_heads()
                if tail:
                    final_in(t - 3, 1, 1 - p)
                    final_clamp(t - 3, 1)
                if heads:
                    head_recip(t - 2, 2)
                if late:
                    silu_clamp(t - 1, 0)
                if early:
                    ht1_evac(t)
                if late:
                    silu_clamp(t - 1, 1)
                    silu_clamp(t - 1, 2)
                    silu_clamp(t - 1, 3)
                if early:
                    u_evac(t, 0)
                if heads:
                    head_max(t - 2, 4, 0, p)
                    head_max(t - 2, 4, 1, p)
                if early:
                    u_evac(t, 1)
                if heads:
                    head_leaky(t - 2, 4)
                    head_max(t - 2, 5, 0, p)
                    head_max(t - 2, 5, 1, p)
                if early:
                    hop1_evac(t)
                if heads:
                    head_recip(t - 2, 3)
                    head_leaky(t - 2, 5)
                    head_max(t - 2, 6, 0, p)
                    head_max(t - 2, 6, 1, p)
                    head_leaky(t - 2, 6)
                if early:
                    softplus_part(t, p)

            iterations(dve, body)

        @block.tensor
        def _(pe):
            def mm(dst, left, right, start=True, stop=True):
                return pe.matmul(dst, left, right, start=start, stop=stop)

            pe.wait_ge(p_pool, 4)
            pe.wait_ge(p_first, 16 * 11)
            mm(ps_l[0][:, 0:3 * D + 1], ones[0:1, :], bias_row[:, :]).then_inc(p_pe, 1)
            pe.wait_ge(p_early, 1)

            def prepare_products():
                pe.wait_ge(p_load, 16 * 12)
                pe.wait_ge(p_products, 1)
                mm(ps_l[1][:, 0:D], ones[0:1, :], bias_row[:, 2 * D:3 * D], stop=False)
                for h in range(HEADS):
                    last = mm(ps_l[1][:, 0:D], fcb_cols[:, h, :], fp_sb[:, h, :], start=False, stop=(h == HEADS - 1))
                last.then_inc(p_pe, 1)
                for h in range(HEADS):
                    last = pe.transpose(ps_t[h // 4][:, (h % 4) * P:(h % 4 + 1) * P], fc_sb[:, h * P:(h + 1) * P],
                                        ident[:, :])
                last.then_inc(p_pe, 1)

            def prepare_heads():
                pe.wait_ge(p_fct, 1)
                for h in range(HEADS):
                    mm(ps_s[h // 4][:, (h % 4) * P:(h % 4 + 1) * P], fct[:, h * P:(h + 1) * P], fp_sb[:, h, :])
                    mm(ps_o[:, 2 * h:2 * h + 2], fct[:, h * P:(h + 1) * P], qkw_sb[:, :])
                mm(ps_o[0:QROWS, 32:33], bq_prod[:, :, :].rearrange("p a n -> p (a n)"), ones[:, 0:1], stop=False)
                mm(ps_o[0:QROWS, 32:33], qkb_row[:, :, :].rearrange("p a n -> p (a n)"), ones[0:1, 0:1],
                   start=False).then_inc(p_pe, 1)

            def transposes(dst, src):
                for r in range(R):
                    last = pe.transpose(dst[:, r * P:(r + 1) * P], src[:, r, :], ident[:, :])
                return last

            def adj_transpose(t, p, g):
                if g == 0:
                    pe.wait_ge(adj_in[p], (t - p) * 8 + 16)
                    if due(e_pre.at(t - 1)):
                        pe.wait_ge(e_pre.semaphore, e_pre.at(t - 1))
                else:
                    pe.wait_ge(e_at.semaphore, e_at.at(t, 1))
                for m in range(HALVES):
                    for i in range(HALVES):
                        last = pe.transpose(ps_e[:, m * N + i * P:m * N + (i + 1) * P],
                                            A[p][:, HALVES * g + i, m * P:(m + 1) * P], ident[:, :])
                last.then_inc(e_adj_tr.semaphore, 1)

            def transpose0(t):
                pe.wait_ge(e_xn.semaphore, e_xn.at(t, 1))
                pe.wait_ge(e_at.semaphore, e_at.at(t, 2))
                transposes(ps_e, xn_e).then_inc(e_tr0.semaphore, 1)

            def project(t, r):
                if r == 0:
                    pe.wait_ge(e_ht0.semaphore, e_ht0.at(t))
                else:
                    pe.wait_ge(e_proj.semaphore, e_proj.at(t, r))
                mm(ps_e[:, 0:3 * D], ht_e[:, r * P:(r + 1) * P], w_proj[:, :]).then_inc(e_proj_ps.semaphore, 1)

            def hop(t, p, sig):
                for r in range(R):
                    g, i = divmod(r, HALVES)
                    for m in range(HALVES):
                        last = mm(ps_e[:, r * D:(r + 1) * D], AT[p][:, g, m, i * P:(i + 1) * P],
                                  y_e[:, HALVES * g + m, :], start=(m == 0), stop=(m == HALVES - 1))
                last.then_inc(sig.semaphore, 1)

            def hop0(t, p):
                pe.wait_ge(e_proj.semaphore, e_proj.at(t, 4))
                hop(t, p, e_hop0)

            def transpose1(t):
                pe.wait_ge(e_xn.semaphore, e_xn.at(t, 3))
                transposes(ps_e, xn_e).then_inc(e_tr1.semaphore, 1)

            def mix1(t, i):
                if i == 0:
                    pe.wait_ge(e_ht1.semaphore, e_ht1.at(t))
                else:
                    pe.wait_ge(e_u.semaphore, e_u.at(t, 1))
                for n in range(2):
                    r = 2 * i + n
                    last = mm(ps_e[:, n * 2 * D:(n + 1) * 2 * D], ht_e[:, r * P:(r + 1) * P], w_l1[:, :])
                last.then_inc(e_u_ps.semaphore, 1)

            def hop1(t, p):
                pe.wait_ge(e_u.semaphore, e_u.at(t, 2))
                hop(t, p, e_hop1)

            def neighbour_sum(t, q):
                pe.wait_ge(l_h2.semaphore, l_h2.at(t))
                if due(l_features.at(t - 1)):
                    pe.wait_ge(l_features.semaphore, l_features.at(t - 1))
                for g in range(2):
                    for m in range(HALVES):
                        pe.matmul(ps_l[1][:, g * N:(g + 1) * N], h2[:, HALVES * g + m, :], AT[q][:, g, m, :],
                                  start=(m == 0), stop=False, skip_group_check=True)
                    for i in range(HALVES):
                        last = pe.matmul(ps_l[1][:, g * N + i * P:g * N + (i + 1) * P], h2[:, HALVES * g + i, :],
                                         eps_ident[:, :], start=False, stop=(i == HALVES - 1),
                                         skip_group_check=True)
                last.then_inc(l_z_ps.semaphore, 1)

            def hidden(t, b):
                if b == 0:
                    pe.wait_ge(l_zt.semaphore, l_zt.at(t))
                if b >= 2:
                    pe.wait_ge(l_hid.semaphore, l_hid.at(t, b - 1))
                mm(ps_l[b % 2][:, :], w1_sb[:, b * P:(b + 1) * P], zt[:, :]).then_inc(l_hid_ps.semaphore, 1)

            def squares_sum(t):
                pe.wait_ge(l_sum.semaphore, l_sum.at(t))
                pe.wait_ge(l_hid.semaphore, l_hid.at(t))
                mm(ps_l[0][:, :], ones[:, :], sq[:, 0, :]).then_inc(l_ss_ps.semaphore, 1)

            def down(t):
                pe.wait_ge(l_act.semaphore, l_act.at(t))
                for r in range(R):
                    for b in range(HB):
                        last = mm(ps_l[1][:, r * D:(r + 1) * D], hid[:, b, r * P:(r + 1) * P], w2_sb[:, b, :],
                                  start=(b == 0), stop=(b == HB - 1))
                last.then_inc(l_w2_ps.semaphore, 1)

            def transpose3(t):
                pe.wait_ge(l_xn.semaphore, l_xn.at(t, 2))
                transposes(ps_l[0], xn_l).then_inc(l_tr.semaphore, 1)

            def queries_keys(t):
                pe.wait_ge(l_ht.semaphore, l_ht.at(t))
                mm(ps_l[1][0:QROWS, :], w_qk[:, :, :].rearrange("p a n -> p (a n)"), ht_l[:, :])\
                    .then_inc(l_qk_ps.semaphore, 1)

            def head_features(t, k):
                if k == 1:
                    pe.wait_ge(l_split.semaphore, l_split.at(t, 1))
                if k >= 2:
                    pe.wait_ge(l_features.semaphore, l_features.at(t, k - 1))
                mm(ps_l[k % 2][:, :], ht_l[:, (k // 2) * P:(k // 2 + 1) * P], w_head[:, 512 * (k % 2):512 * (k % 2) + 512])\
                    .then_inc(l_g_ps.semaphore, 1)

            def scores(pair, u, j, q):
                if u == 0 and j == 0:
                    pe.wait_ge(l_rows.semaphore, l_rows.at(pair))
                if u == GPG // 2 and j == 0:
                    pe.wait_ge(l_late_rows.semaphore, l_late_rows.at(pair))
                if due(h_max.at(pair, 2 * u + j - 1)):
                    pe.wait_ge(h_max.semaphore, h_max.at(pair, 2 * u + j - 1))
                g, h = u // GPG, 2 * (u % GPG) + j
                for i in range(HALVES):
                    last = mm(ps_s[j][:, i * N:(i + 1) * N], q_rows[q][:, g * N + i * P:g * N + (i + 1) * P],
                              k_rows[q][:, h, g * N:(g + 1) * N])
                last.then_inc(h_qk.semaphore, 1)

            def head_transpose(pair, u, j):
                pe.wait_ge(h_norm.semaphore, h_norm.at(pair, u + 1))
                if due(h_et.at(pair, 2 * u + j - 1)):
                    pe.wait_ge(h_et.semaphore, h_et.at(pair, 2 * u + j - 1))
                for m in range(HALVES):
                    for i in range(HALVES):
                        last = pe.transpose(ps_t[j][:, m * N + i * P:m * N + (i + 1) * P],
                                            S[u % SB][:, j, i, m * P:(m + 1) * P], ident[:, :])
                last.then_inc(h_tr.semaphore, 1)

            def attend(pair, u, j, q):
                g, h = u // GPG, 2 * (u % GPG) + j
                pe.wait_ge(h_et.semaphore, h_et.at(pair, 2 * u + j + 1))
                if u == 0 and j == 0:
                    pe.wait_ge(l_features.semaphore, l_features.at(pair))
                if h == 0:
                    if due(f_z.at(pair, g)):
                        pe.wait_ge(f_z.semaphore, f_z.at(pair, g))
                for i in range(HALVES):
                    for m in range(HALVES):
                        last = pe.matmul(ps_o[:, (HALVES * g + i) * D:(HALVES * g + i + 1) * D], ET[j][:, m, i * P:(i + 1) * P],
                                         G[q][:, HALVES * g + m, h, :],
                                         start=(h == 0 and i == 0 and m == 0),
                                         stop=(h == HEADS - 1 and m == HALVES - 1), skip_group_check=True)
                last.then_inc(h_av.semaphore, 1)

            def body(t, p, known):
                early, late, heads, tail = (mine(known, back) for back in range(4))
                if tail:
                    head_transpose(t - 3, 2, 0)
                    attend(t - 3, 1, 0, 1 - p)
                    head_transpose(t - 3, 2, 1)
                    scores(t - 3, 6, 0, 1 - p)
                    scores(t - 3, 6, 1, 1 - p)
                if early:
                    adj_transpose(t, p, 0)
                if tail:
                    attend(t - 3, 1, 1, 1 - p)
                    attend(t - 3, 2, 0, 1 - p)
                    scores(t - 3, 7, 0, 1 - p)
                if early:
                    adj_transpose(t, p, 1)
                if heads:
                    down(t - 2)
                if tail:
                    head_transpose(t - 3, 3, 0)
                    attend(t - 3, 2, 1, 1 - p)
                if early:
                    transpose0(t)
                if tail:
                    head_transpose(t - 3, 3, 1)
                    scores(t - 3, 7, 1, 1 - p)
                    attend(t - 3, 3, 0, 1 - p)
                    attend(t - 3, 3, 1, 1 - p)
                if early:
                    project(t, 0)
                if tail:
                    head_transpose(t - 3, 4, 0)
                if heads:
                    transpose3(t - 2)
                if tail:
                    head_transpose(t - 3, 4, 1)
                if early:
                    project(t, 1)
                if heads:
                    queries_keys(t - 2)
                    head_features(t - 2, 0)
                if early:
                    project(t, 2)
                if tail:
                    attend(t - 3, 4, 0, 1 - p)
                    head_transpose(t - 3, 5, 0)
                    head_transpose(t - 3, 5, 1)
                if heads:
                    head_features(t - 2, 1)
                    head_features(t - 2, 2)
                    head_features(t - 2, 3)
                    head_features(t - 2, 4)
                if early:
                    project(t, 3)
                if heads:
                    scores(t - 2, 0, 0, p)
                    scores(t - 2, 0, 1, p)
                    head_features(t - 2, 5)
                    head_features(t - 2, 6)
                    head_features(t - 2, 7)
                if early:
                    hop0(t, p)
                    if known == 0:
                        prepare_products()
                    if known == 0:
                        prepare_heads()
                if heads:
                    scores(t - 2, 1, 0, p)
                    scores(t - 2, 1, 1, p)
                if tail:
                    attend(t - 3, 4, 1, 1 - p)
                    attend(t - 3, 5, 0, 1 - p)
                    head_transpose(t - 3, 6, 0)
                if late:
                    neighbour_sum(t - 1, 1 - p)
                if heads:
                    scores(t - 2, 2, 0, p)
                    scores(t - 2, 2, 1, p)
                if late:
                    hidden(t - 1, 0)
                    hidden(t - 1, 1)
                if tail:
                    head_transpose(t - 3, 6, 1)
                if late:
                    hidden(t - 1, 2)
                    hidden(t - 1, 3)
                if tail:
                    attend(t - 3, 5, 1, 1 - p)
                    attend(t - 3, 6, 0, 1 - p)
                    head_transpose(t - 3, 7, 0)
                if heads:
                    scores(t - 2, 3, 0, p)
                    scores(t - 2, 3, 1, p)
                if tail:
                    head_transpose(t - 3, 7, 1)
                    attend(t - 3, 6, 1, 1 - p)
                if heads:
                    head_transpose(t - 2, 0, 0)
                if late:
                    squares_sum(t - 1)
                if tail:
                    attend(t - 3, 7, 0, 1 - p)
                    attend(t - 3, 7, 1, 1 - p)
                if heads:
                    head_transpose(t - 2, 0, 1)
                    head_transpose(t - 2, 1, 0)
                    scores(t - 2, 4, 0, p)
                    scores(t - 2, 4, 1, p)
                if early:
                    transpose1(t)
                if heads:
                    attend(t - 2, 0, 0, p)
                    head_transpose(t - 2, 1, 1)
                if early:
                    mix1(t, 0)
                    mix1(t, 1)
                if heads:
                    attend(t - 2, 0, 1, p)
                    scores(t - 2, 5, 0, p)
                    scores(t - 2, 5, 1, p)
                if early:
                    hop1(t, p)
                if known == 0:
                    pe.wait_ge(p_weights, 5)

            iterations(pe, body)


_INS = ['x', 'adj', 'L0_gnn_theta', 'L0_gnn_W_h', 'L0_gnn_W_t', 'L0_gnn_b_t', 'L1_gnn_gamma', 'L1_gnn_beta',
        'L1_gnn_W_self', 'L1_gnn_W_neigh', 'L2_gnn_epsilon', 'L2_gnn_W1', 'L2_gnn_b1', 'L2_gnn_rms_weight',
        'L2_gnn_W2', 'L2_gnn_b2', 'L3_gnn_fc_w', 'L3_gnn_fc_b', 'L3_gnn_q_w', 'L3_gnn_q_b', 'L3_gnn_k_w',
        'L3_gnn_k_b', 'L3_gnn_fp_w', 'L3_gnn_fp_b']


def row_select(heads):
    import numpy as _np
    select = _np.zeros((96, 2 + 2 * heads), _np.float32)
    for part in range(3):
        for h in range(heads):
            q, k = 32 * part + h, 32 * part + heads + h
            select[q, 0] = 1.0
            select[k, 1] = 1.0
            select[k, 2 + h] = 1.0
            select[q, 2 + heads + h] = 1.0
    return select


def kernel(**inputs):
    import numpy as _np
    import concourse.bacc as _bacc
    from concourse import mybir as _mybir
    from concourse.bass_utils import run_bass_kernel_spmd as _run

    nc = _bacc.Bacc("TRN2", target_bir_lowering=False, num_devices=1)
    arrays, args = {}, []
    for name in _INS:
        a = _np.ascontiguousarray(inputs[name])
        if a.ndim == 0:
            a = a.reshape(1, 1)
        if name == 'L2_gnn_epsilon':
            a = a.reshape(1, 1)
        arrays[f"in_{name}_dram"] = a
        args.append(nc.dram_tensor(f"in_{name}_dram", a.shape, _mybir.dt.from_np(a.dtype), kind="ExternalInput").ap())
    select = row_select(8)
    arrays["row_select_dram"] = select
    args.append(nc.dram_tensor("row_select_dram", select.shape, _mybir.dt.float32, kind="ExternalInput").ap())
    shape = tuple(inputs['x'].shape)
    args.append(nc.dram_tensor("out_0_dram", shape, _mybir.dt.float32, kind="ExternalOutput").ap())
    four_layer_gnn_kernel(nc, *args)
    r = _run(nc, [arrays], core_ids=[0])
    return r.results[0]["out_0_dram"]
```
